# Optimizing a Trainium2 kernel written in Bass

```python
import numpy as np
import jax
import jax.numpy as jnp

def _softmax(x, axis=-1):
    return jax.nn.softmax(x, axis=axis)

def _gelu(x):
    return jax.nn.gelu(x, approximate=True)

def _silu(x):
    return jax.nn.silu(x)

def _sigmoid(x):
    return jax.nn.sigmoid(x)

def _layernorm(x, axis=-1, eps=1e-05):
    m = jnp.mean(x, axis=axis, keepdims=True)
    v = jnp.var(x, axis=axis, keepdims=True)
    return (x - m) / jnp.sqrt(v + eps)

def _scatter_add(tgt, idx, src, axis=0):
    return tgt.at[idx].add(src)

def _segment_sum(src, seg, n):
    return jax.ops.segment_sum(src, seg, n)
kernel_name = 'mk_gnn_ffn_d2_gnn_r8_843361'

def setup_inputs(seed: int=0):
    np.random.seed(seed)
    _w = jnp.asarray

    def _rec_inputs():
        import jax
        import jax.numpy as jnp
        _gk = jax.random.key(seed)
        x = -0.0002928 + 1 * jax.random.normal(jax.random.fold_in(_gk, 1), (1024, 512), jnp.float32)
        src = jax.random.randint(jax.random.fold_in(_gk, 2), (16384,), 0, 1024, jnp.int32)
        dst = jax.random.randint(jax.random.fold_in(_gk, 3), (16384,), 0, 1024, jnp.int32)
        _o = jnp.argsort(dst, stable=True)
        src = src[_o]
        dst = dst[_o]
        return (x, src, dst)
    x, src, dst = _rec_inputs()

    def _L0_gnn_setup():
        import jax, jax.numpy as jnp
        import numpy as np
        NUM_NODES = 1024
        NUM_EDGES = 32768
        IN_C = 512
        OUT_C = 512
        key = jax.random.key(seed)
        k1, k2, k3, k4 = jax.random.split(key, 4)
        x = jax.random.normal(k1, (NUM_NODES, IN_C), dtype=jnp.float32)
        edge_index = jax.random.randint(k2, (2, NUM_EDGES), 0, NUM_NODES, dtype=jnp.int64)
        W = jax.random.normal(k3, (OUT_C, IN_C), dtype=jnp.float32) * (1.0 / np.sqrt(IN_C))
        b = jax.random.normal(k4, (OUT_C,), dtype=jnp.float32) * 0.01
        return {'x': x, 'edge_index': edge_index, 'W': W, 'b': b}
    _L0_gnn_all = _L0_gnn_setup()
    _L0_gnn_in = {k: v for k, v in _L0_gnn_all.items() if k in ('W', 'b')}
    del _L0_gnn_all

    def _L0_ffn_setup():
        import jax, jax.numpy as jnp
        import numpy as np
        B, S, D = (4, 256, 512)
        E, H, K = (8, 1024, 2)

        def _moe_forward(x, router_w, router_b, w1, b1, wg, bg, wv, bv, w2, b2):
            b, s, d = x.shape
            xf = x.reshape(-1, d)
            T = xf.shape[0]
            scores = xf @ router_w + router_b
            probs = jax.nn.softmax(scores, axis=-1)
            topk_p, topk_i = jax.lax.top_k(probs, K)
            gates = jnp.zeros((T, E), xf.dtype).at[jnp.arange(T)[:, None], topk_i].set(topk_p)
            h = jnp.einsum('td,edh->teh', xf, w1) + b1[None]
            gated = jax.nn.silu(jnp.einsum('teh,ehf->tef', h, wg) + bg[None]) * (jnp.einsum('teh,ehf->tef', h, wv) + bv[None])
            y = jnp.einsum('tef,efd->ted', gated, w2) + b2[None]
            out = jnp.einsum('ted,te->td', y, gates)
            return out.reshape(b, s, d)
        key = jax.random.key(seed)
        ks = jax.random.split(key, 8)
        s_in = 0.02
        return {'x': jax.random.normal(ks[0], (B, S, D), jnp.float32), 'router_w': jax.random.normal(ks[1], (D, E), jnp.float32) * s_in, 'router_b': jnp.zeros((E,), jnp.float32), 'w1': jax.random.normal(ks[2], (E, D, H), jnp.float32) * s_in, 'b1': jnp.zeros((E, H), jnp.float32), 'wg': jax.random.normal(ks[3], (E, H, H), jnp.float32) * s_in, 'bg': jnp.zeros((E, H), jnp.float32), 'wv': jax.random.normal(ks[4], (E, H, H), jnp.float32) * s_in, 'bv': jnp.zeros((E, H), jnp.float32), 'w2': jax.random.normal(ks[5], (E, H, D), jnp.float32) * s_in, 'b2': jnp.zeros((E, D), jnp.float32)}
    _L0_ffn_all = _L0_ffn_setup()
    _L0_ffn_in = {k: v for k, v in _L0_ffn_all.items() if k in ('router_w', 'router_b', 'w1', 'b1', 'wg', 'bg', 'wv', 'bv', 'w2', 'b2')}
    del _L0_ffn_all

    def _L1_gnn_setup():
        import jax, jax.numpy as jnp
        import numpy as np
        N = 6250
        IN_CH = 512
        OUT_CH = 512
        DEG = 32
        E = N * DEG
        key = jax.random.key(seed)
        kx, kwc, kwn, kb, ke = jax.random.split(key, 5)
        x = jax.random.normal(kx, (N, IN_CH), dtype=jnp.float32)
        bound = 1.0 / np.sqrt(IN_CH)
        wc = jax.random.uniform(kwc, (IN_CH, OUT_CH), minval=-bound, maxval=bound, dtype=jnp.float32)
        wn = jax.random.uniform(kwn, (IN_CH, OUT_CH), minval=-bound, maxval=bound, dtype=jnp.float32)
        bias = jax.random.uniform(kb, (OUT_CH,), minval=-bound, maxval=bound, dtype=jnp.float32)
        src = jnp.repeat(jnp.arange(N, dtype=jnp.int64), DEG)
        dst = jax.random.randint(ke, (E,), 0, N, dtype=jnp.int64)
        edge_index = jnp.stack([src, dst], axis=0)
        return {'x': x, 'wc': wc, 'wn': wn, 'bias': bias, 'edge_index': edge_index}
    _L1_gnn_all = _L1_gnn_setup()
    _L1_gnn_in = {k: v for k, v in _L1_gnn_all.items() if k in ('wc', 'wn', 'bias')}
    del _L1_gnn_all

    def _L1_ffn_setup():
        import jax, jax.numpy as jnp
        import numpy as np
        import math
        B, T, D, H, E, TOPK = (8, 512, 512, 256, 8, 2)
        CAP_FRAC = 1.0

        def _expert_ffn(x, w1, w2, w3):
            h = jax.nn.gelu(x @ w2 * (x @ w1), approximate=False)
            return h @ w3
        key = jax.random.key(seed)
        ks = jax.random.split(key, 6)
        x = jax.random.normal(ks[0], (B, T, D), dtype=jnp.float32)
        Wr = jax.random.normal(ks[1], (D, E), dtype=jnp.float32) * 0.02
        br = jnp.zeros((E,), dtype=jnp.float32)
        W1 = jax.random.normal(ks[2], (E, D, H), dtype=jnp.float32) * 0.02
        W2 = jax.random.normal(ks[3], (E, D, H), dtype=jnp.float32) * 0.02
        W3 = jax.random.normal(ks[4], (E, H, D), dtype=jnp.float32) * 0.02
        return {'x': x, 'Wr': Wr, 'br': br, 'W1': W1, 'W2': W2, 'W3': W3}
    _L1_ffn_all = _L1_ffn_setup()
    _L1_ffn_in = {k: v for k, v in _L1_ffn_all.items() if k in ('Wr', 'br', 'W1', 'W2', 'W3')}
    del _L1_ffn_all
    return {'x': x, 'src': src, 'dst': dst, 'L0_gnn_W': _L0_gnn_in['W'], 'L0_gnn_b': _L0_gnn_in['b'], 'L0_ffn_router_w': _L0_ffn_in['router_w'], 'L0_ffn_router_b': _L0_ffn_in['router_b'], 'L0_ffn_w1': _L0_ffn_in['w1'], 'L0_ffn_b1': _L0_ffn_in['b1'], 'L0_ffn_wg': _L0_ffn_in['wg'], 'L0_ffn_bg': _L0_ffn_in['bg'], 'L0_ffn_wv': _L0_ffn_in['wv'], 'L0_ffn_bv': _L0_ffn_in['bv'], 'L0_ffn_w2': _L0_ffn_in['w2'], 'L0_ffn_b2': _L0_ffn_in['b2'], 'L1_gnn_wc': _L1_gnn_in['wc'], 'L1_gnn_wn': _L1_gnn_in['wn'], 'L1_gnn_bias': _L1_gnn_in['bias'], 'L1_ffn_Wr': _L1_ffn_in['Wr'], 'L1_ffn_br': _L1_ffn_in['br'], 'L1_ffn_W1': _L1_ffn_in['W1'], 'L1_ffn_W2': _L1_ffn_in['W2'], 'L1_ffn_W3': _L1_ffn_in['W3']}

def reference(x, src, dst, L0_gnn_W, L0_gnn_b, L0_ffn_router_w, L0_ffn_router_b, L0_ffn_w1, L0_ffn_b1, L0_ffn_wg, L0_ffn_bg, L0_ffn_wv, L0_ffn_bv, L0_ffn_w2, L0_ffn_b2, L1_gnn_wc, L1_gnn_wn, L1_gnn_bias, L1_ffn_Wr, L1_ffn_br, L1_ffn_W1, L1_ffn_W2, L1_ffn_W3):
    import jax
    import jax.numpy as jnp

    def _L0_gnn_ref(x, edge_index, W, b):
        import jax, jax.numpy as jnp
        import numpy as np
        NUM_NODES = 1024
        NUM_EDGES = 32768
        IN_C = 512
        OUT_C = 512
        n = x.shape[0]
        loop = jnp.arange(n, dtype=edge_index.dtype)
        rows = jnp.concatenate([edge_index[0], loop])
        cols = jnp.concatenate([edge_index[1], loop])
        adj = jnp.zeros((n, n), dtype=jnp.float32).at[rows, cols].set(1.0)
        deg = adj.sum(axis=1)
        deg_inv_sqrt = jnp.where(deg > 0, jax.lax.rsqrt(jnp.maximum(deg, 1e-30)), 0.0)
        norm = deg_inv_sqrt[:, None] * adj * deg_inv_sqrt[None, :]
        h = x @ W.T + b
        return norm @ h

    def _L0_ffn_ref(x, router_w, router_b, w1, b1, wg, bg, wv, bv, w2, b2):
        import jax, jax.numpy as jnp
        import numpy as np
        B, S, D = (4, 256, 512)
        E, H, K = (8, 1024, 2)

        def _moe_forward(x, router_w, router_b, w1, b1, wg, bg, wv, bv, w2, b2):
            b, s, d = x.shape
            xf = x.reshape(-1, d)
            T = xf.shape[0]
            scores = xf @ router_w + router_b
            probs = jax.nn.softmax(scores, axis=-1)
            topk_p, topk_i = jax.lax.top_k(probs, K)
            gates = jnp.zeros((T, E), xf.dtype).at[jnp.arange(T)[:, None], topk_i].set(topk_p)
            h = jnp.einsum('td,edh->teh', xf, w1) + b1[None]
            gated = jax.nn.silu(jnp.einsum('teh,ehf->tef', h, wg) + bg[None]) * (jnp.einsum('teh,ehf->tef', h, wv) + bv[None])
            y = jnp.einsum('tef,efd->ted', gated, w2) + b2[None]
            out = jnp.einsum('ted,te->td', y, gates)
            return out.reshape(b, s, d)
        return _moe_forward(x, router_w, router_b, w1, b1, wg, bg, wv, bv, w2, b2)

    def _L1_gnn_ref(x, wc, wn, bias, edge_index):
        import jax, jax.numpy as jnp
        import numpy as np
        N = 6250
        IN_CH = 512
        OUT_CH = 512
        DEG = 32
        E = N * DEG
        alpha = x @ wc
        beta = x @ wn
        src, dst = (edge_index[0], edge_index[1])
        sums = jax.ops.segment_sum(beta[dst], src, num_segments=x.shape[0])
        counts = jax.ops.segment_sum(jnp.ones_like(src, dtype=beta.dtype), src, num_segments=x.shape[0])
        gamma = sums / counts[:, None]
        return alpha + gamma + bias

    def _L1_ffn_ref(x, Wr, br, W1, W2, W3):
        import jax, jax.numpy as jnp
        import numpy as np
        import math
        B, T, D, H, E, TOPK = (8, 512, 512, 256, 8, 2)
        CAP_FRAC = 1.0

        def _expert_ffn(x, w1, w2, w3):
            h = jax.nn.gelu(x @ w2 * (x @ w1), approximate=False)
            return h @ w3
        b, t, d = x.shape
        Bt = b * t
        x_flat = x.reshape(Bt, d)
        logits = x_flat.astype(jnp.float32) @ Wr + br
        vals, idx = jax.lax.top_k(logits, TOPK)
        scores = jax.nn.softmax(vals, axis=-1).astype(x.dtype).reshape(b, t, TOPK)
        onehot = jax.nn.one_hot(idx, E, dtype=jnp.float32)
        pos = jnp.cumsum(jnp.cumsum(onehot, axis=0), axis=1).astype(jnp.int32)
        capacity = math.floor(Bt * CAP_FRAC)
        mask3 = onehot * (pos < capacity)
        token_mask = mask3.sum(-1).reshape(b, t, TOPK)
        assign = jnp.einsum('tke,e->tk', mask3, jnp.arange(E, dtype=jnp.float32)).astype(jnp.int32)
        i_max = assign.reshape(b, t, TOPK).max(axis=-1)
        y = jnp.zeros_like(x)
        for i in range(E):
            yi = _expert_ffn(x, W1[i], W2[i], W3[i])
            y = jnp.where((i_max == i)[..., None], yi, y)
        expert_outputs = jnp.where(token_mask[..., None] > 0, y[:, :, None, :], x[:, :, None, :])
        return jnp.einsum('btkD,btk->btD', expert_outputs, scores)
    edge_index = jnp.stack([src, dst])
    x = x + _L0_gnn_ref(_layernorm(x, axis=-1), edge_index, L0_gnn_W, L0_gnn_b)
    x = x + _L0_ffn_ref(_layernorm(x, axis=-1)[None], L0_ffn_router_w, L0_ffn_router_b, L0_ffn_w1, L0_ffn_b1, L0_ffn_wg, L0_ffn_bg, L0_ffn_wv, L0_ffn_bv, L0_ffn_w2, L0_ffn_b2)[0]
    x = x + _L1_gnn_ref(_layernorm(x, axis=-1), L1_gnn_wc, L1_gnn_wn, L1_gnn_bias, edge_index)
    x = x + _L1_ffn_ref(_layernorm(x, axis=-1)[None], L1_ffn_Wr, L1_ffn_br, L1_ffn_W1, L1_ffn_W2, L1_ffn_W3)[0]
    return x

_drawn_inputs = setup_inputs


def setup_inputs(seed=0):
    import zlib

    import numpy as np

    out = dict(_drawn_inputs(seed))
    spreads = {'L0_ffn_router_b': (0.0, 0.8),
     'L0_ffn_b1': (0.0, 0.8),
     'L0_ffn_bg': (0.0, 0.8),
     'L0_ffn_bv': (0.0, 0.8),
     'L0_ffn_b2': (0.0, 2.0),
     'L1_ffn_br': (0.0, 2.0)}
    factors = {'L0_gnn_b': 5.035,
     'L0_ffn_w1': 6.07,
     'L0_ffn_wg': 6.266,
     'L0_ffn_wv': 6.295,
     'L0_ffn_w2': 5.959,
     'L1_gnn_bias': 100.319,
     'L1_gnn_wc': 8.0,
     'L1_gnn_wn': 8.0,
     'L1_ffn_Wr': 8.0,
     'L1_ffn_W1': 8.0,
     'L1_ffn_W2': 8.0,
     'L1_ffn_W3': 8.0}
    for name, (base, spread) in spreads.items():
        noise = np.random.default_rng([zlib.crc32(name.encode()), seed]).standard_normal(out[name].shape)
        drawn = base * np.exp(spread * noise) if base else spread * noise
        out[name] = jnp.asarray(drawn.astype(out[name].dtype))
    for name, factor in factors.items():
        out[name] = (out[name] * factor).astype(out[name].dtype)
    return out
```

```python
import concourse.bass as bass
from concourse import mybir
from contextlib import ExitStack


def gnn_moe_two_layer_kernel(
    nc, x, src, dst, gnn0_w, gnn0_b, router0_w, router0_b, w1, b1, wg, bg, wv, bv, w2, b2,
    wc, wn, gnn1_b, router1_w, router1_b, e1_w1, e1_w2, e1_w3, out,
):
    f32, bf16, f16, i32 = mybir.dt.float32, mybir.dt.bfloat16, mybir.dt.float16, mybir.dt.int32
    ALU = mybir.AluOpType
    ACT = mybir.ActivationFunctionType
    AX = mybir.AxisListType.X
    ds = bass.ds

    P = 128
    T, D = x.shape
    NT = T // P
    DK = D // P
    EDGES = src.shape[0]
    NCH = EDGES // P
    E, _, H = w1.shape
    HK = H // P
    HALF = 512
    H1 = e1_w1.shape[2]
    HK1 = H1 // P
    SLOTS0 = 2 * T // P + E
    SLOTS1 = T // P + E
    NOH = 4
    EPS = 1e-5
    BIG = 1e30

    ctx = ExitStack()
    with ctx:
        def sb(name, shape, dt=f32):
            return ctx.enter_context(nc.sbuf_tensor(name, shape, dt))

        def sem(name):
            return ctx.enter_context(nc.semaphore(name))

        def dram(name, shape):
            return nc.dram_tensor(name, shape, f32, kind="Internal").ap()

        counts_d = dram("edge_counts", [NT, P, T])
        slots0_x = dram("slots0_x", [SLOTS0 * P, D])
        slots0_y = dram("slots0_y", [SLOTS0 * P, D])
        slots1_x = dram("slots1_x", [SLOTS1 * P, D])
        slots1_y = dram("slots1_y", [SLOTS1 * P, D])

        X = sb("X", [P, NT, D])
        w1_sb = sb("w1_sb", [P, 2, DK, H])
        wg_sb = sb("wg_sb", [P, 2, HK, H])
        wv_sb = sb("wv_sb", [P, HK, H])
        w2_sb = sb("w2_sb", [P, HK, D])
        R = sb("R", [P, 9216])

        def region(at, *shape, dt=f32):
            n = 1
            for m in shape:
                n *= m
            words = n if dt in (f32, i32) else n // 2
            v = R[:, at:at + words]
            if dt != f32:
                v = v.bitcast(dt)
            if len(shape) == 2:
                v = v.rearrange("p (a b) -> p a b", a=shape[0])
            if len(shape) == 3:
                v = v.rearrange("p (a b c) -> p a b c", a=shape[0], b=shape[1])
            return v

        AT = wv_sb
        w2_flat = w2_sb[:, :, :].rearrange("p a b -> p (a b)")
        MT = w2_flat.rearrange("p (k t) -> p k t", k=DK)
        XNT = w2_flat.rearrange("p (i k t) -> p i k t", i=NT, k=DK)
        ct_stage = region(0, 2, T)
        oh_src = region(2048, NOH, T, dt=bf16)
        oh_dst = region(4096, NOH, P, dt=bf16)
        zero_b = region(4352, HALF, dt=bf16)
        W_raw = region(4608, DK, D)
        WT = region(6656, DK, D)
        bias_bc = region(8704, D)
        XN = region(0, NT, D)
        zero_row = X[:, 0, :]

        ident = sb("ident", [P, P])
        iota_h = sb("iota_h", [P, T], f16)
        ones_b = sb("ones_b", [P, P], bf16)
        upper_b = sb("upper_b", [P, P], bf16)
        ones_f = sb("ones_f", [P, 1])
        eps_t = sb("eps_t", [P, 1])
        tile_lo = sb("tile_lo", [P, NT])
        chunk_up = sb("chunk_up", [P, 1])
        chunk_down = sb("chunk_down", [P, 1])
        e_key = sb("e_key", [P, NT, E])
        e_idx = sb("e_idx", [P, NT, E])
        k128 = sb("k128", [P, E, 8])
        before = sb("before", [P, E, E])
        last_tok = sb("last_tok", [P, NT])
        b1T = sb("b1T", [P, E * HK])
        b1_rows = sb("b1_rows", [E * HK, P])
        edges_i = sb("edges_i", [P, 2, P], i32)
        edges_f = sb("edges_f", [P, 2, P])
        edges_T = sb("edges_T", [P, 2, P])
        etab = sb("etab", [1, 2 * NT], i32)
        rtab = sb("rtab", [1, 2 * E + 1], i32)
        rtab1 = sb("rtab1", [1, 2 * E + 1], i32)
        sm = sb("sm", [P, 8, NT])
        mv = sb("mv", [P, NT, 2])
        bst = sb("bst", [P, NT, 6])
        rstd = sb("rstd", [P, NT])
        dinv = sb("dinv", [P, NT])
        wdeg = sb("wdeg", [P, NT])
        rw_sb = sb("rw_sb", [P, DK, E])
        rb_bc = sb("rb_bc", [P, E])
        rw1_sb = sb("rw1_sb", [P, DK, E])
        rb1_bc = sb("rb1_bc", [P, E])
        rt = sb("rt", [P, 6, NT, E])
        cmp8 = sb("cmp8", [P, E, 8])
        oh_b = sb("oh_b", [P, NT, E], bf16)
        oh2_b = sb("oh2_b", [P, NT, E], bf16)
        topv = sb("topv", [P, 2, NT])
        gate = sb("gate", [P, 2, NT])
        nexp = sb("nexp", [P, 3, E])
        dest = sb("dest", [P, 2, NT])
        dest_i = sb("dest_i", [P, 2, NT], i32)
        PS = ctx.enter_context(nc.psum_tensor("PS", [P, 8, HALF], f32))

        dve_own, act_own, pool_own, pe_own = sem("dve_own"), sem("act_own"), sem("pool_own"), sem("pe_own")
        own_count = {}

        def after(eng, own, ins):
            own_count[id(own)] = own_count.get(id(own), 0) + 1
            ins.then_inc(own, 1)
            eng.wait_ge(own, own_count[id(own)])

        edges_in, x_in, gw_in, gb_in, b1_in, r_in, zeros_out = (
            sem(n) for n in "edges_in x_in gw_in gb_in b1_in r_in zeros_out".split())
        w1_in = [sem(f"w1_in{i}") for i in range(2)]
        wg_in = [sem(f"wg_in{i}") for i in range(2)]
        wv_in, w2_in = sem("wv_in"), sem("w2_in")
        bg_in = [sem(f"bg_in{i}") for i in range(2)]
        bvb2_in = [sem("bv_in"), sem("b2_in")]
        consts_ready = sem("consts_ready")
        oh_free = [sem(f"oh_free{t}") for t in range(NT)]
        oh_ready = [sem(f"oh_ready{t}") for t in range(NT)]
        counts_ps, counts_copied, at_ready = sem("counts_ps"), sem("counts_copied"), sem("at_ready")
        counts_out = [sem(f"counts_out{i}") for i in range(2)]
        edge_rows, edge_T_ps, edge_T_sb, span, span_ps, span_cols, span_row, etab_ready = (
            sem(n) for n in "edge_rows edge_T_ps edge_T_sb span span_ps span_cols span_row etab_ready".split())
        wt_ps, wt_sb = sem("wt_ps"), sem("wt_sb")

        with nc.Block() as block:

            @block.sync
            def _(sp):
                sp.dma_start(edges_i[:, 0, :], src.rearrange("(k e) -> k e", e=P)).then_inc(edges_in, 16)
                sp.dma_start(edges_i[:, 1, :], dst.rearrange("(k e) -> k e", e=P)).then_inc(edges_in, 16)
                sp.dma_start(W_raw, gnn0_w.rearrange("(o p) d -> p o d", p=P)).then_inc(gw_in, 16)
                sp.dma_start(b1_rows[:, :], b1.rearrange("e (j p) -> (e j) p", p=P)).then_inc(b1_in, 16)
                sp.dma_start(X[:, :, :], x.rearrange("(i p) d -> p i d", p=P)).then_inc(x_in, 16)
                sp.dma_start(bias_bc, gnn0_b.rearrange("(a d) -> a d", a=1).broadcast_to([P, D])).then_inc(gb_in, 16)
                for r_sb, rb, r_dram, rb_dram in ((rw_sb, rb_bc, router0_w, router0_b),
                                                  (rw1_sb, rb1_bc, router1_w, router1_b)):
                    sp.dma_start(r_sb[:, :, :], r_dram.rearrange("(k p) e -> p k e", p=P)).then_inc(r_in, 16)
                    sp.dma_start(rb[:, :], rb_dram.rearrange("(a e) -> a e", a=1).broadcast_to([P, E])).then_inc(r_in, 16)
                sp.wait_ge(consts_ready, 1)
                zeros = zero_b.bitcast(f32).rearrange("p (a d) -> p a d", a=1)
                for slots, n in ((slots0_x, SLOTS0), (slots1_x, SLOTS1)):
                    sp.dma_start(slots.rearrange("(p s) d -> p (s d)", p=P).rearrange("p (m c) -> p m c", c=D // 2),
                                 zeros.broadcast_to([P, 2 * n, D // 2])).then_inc(zeros_out, 16)
                for t in range(NT):
                    sp.wait_ge(counts_copied, t + 1)
                    sp.dma_start(counts_d[t], ct_stage[:, t % 2, :]).then_inc(counts_out[t % 2], 16)
                    if t == 0:
                        for e in range(2):
                            sp.dma_start(w1_sb[:, e], w1[e].rearrange("(k p) h -> p k h", p=P)).then_inc(w1_in[e], 16)
                            sp.dma_start(wg_sb[:, e], wg[e].rearrange("(k p) h -> p k h", p=P)).then_inc(wg_in[e], 16)
                for i in range(2):
                    sp.wait_ge(counts_out[i], 16 * (NT // 2))
                sp.wait_ge(zeros_out, 32)

            @block.gpsimd
            def _(pool):
                def own(ins):
                    after(pool, pool_own, ins)

                own(nc.gpsimd.memset(ident[:, :], 0.0))
                own(nc.gpsimd.affine_select(out=ident[:, :], in_=ident[:, :], compare_op=ALU.not_equal, fill=1.0,
                                            base=0, pattern=[[-1, P]], channel_multiplier=1))
                own(nc.gpsimd.iota(tile_lo[:, :], [[P, NT]], base=0, channel_multiplier=0,
                                   allow_small_or_imprecise_dtypes=True))
                own(nc.gpsimd.iota(chunk_up[:, :], [[0, 1]], base=1, channel_multiplier=1,
                                   allow_small_or_imprecise_dtypes=True))
                own(nc.gpsimd.iota(chunk_down[:, :], [[0, 1]], base=P, channel_multiplier=-1,
                                   allow_small_or_imprecise_dtypes=True))
                own(nc.gpsimd.memset(zero_b, 0.0))
                nc.gpsimd.iota(iota_h[:, :], [[1, T]], base=0, channel_multiplier=0,
                               allow_small_or_imprecise_dtypes=True).then_inc(consts_ready, 1)
                own(nc.gpsimd.memset(ones_b[:, :], 1.0))
                own(nc.gpsimd.memset(ones_f[:, :], 1.0))
                own(nc.gpsimd.memset(eps_t[:, :], EPS))
                own(nc.gpsimd.affine_select(out=upper_b[:, :], in_=ones_b[:, :], compare_op=ALU.is_gt, fill=0.0,
                                            base=0, pattern=[[1, P]], channel_multiplier=-1))
                own(nc.gpsimd.iota(e_key[:, :, :], [[0, NT], [-1, E]], base=E, channel_multiplier=0,
                                   allow_small_or_imprecise_dtypes=True))
                own(nc.gpsimd.iota(e_idx[:, :, :], [[0, NT], [1, E]], base=0, channel_multiplier=0,
                                   allow_small_or_imprecise_dtypes=True))
                own(nc.gpsimd.iota(k128[:, :, :], [[0, E], [P, 8]], base=P, channel_multiplier=0,
                                   allow_small_or_imprecise_dtypes=True))
                own(nc.gpsimd.memset(before[:, :, :], 1.0))
                own(nc.gpsimd.affine_select(out=before[:, :, :], in_=before[:, :, :], compare_op=ALU.is_gt, fill=0.0,
                                            base=0, pattern=[[1, E], [-1, E]], channel_multiplier=0))
                own(nc.gpsimd.memset(last_tok[:, :], 0.0))
                own(nc.gpsimd.affine_select(out=last_tok[:, :], in_=last_tok[:, :], compare_op=ALU.not_equal, fill=1.0,
                                            base=-(T - 1), pattern=[[P, NT]], channel_multiplier=1))
                for t in range(NT):
                    pool.wait_ge(counts_copied, t + 1)
                    own(nc.gpsimd.tensor_scalar(AT[:, t, :], ct_stage[:, t % 2, :], 1.0, None, ALU.min))
                    nc.gpsimd.affine_select(out=AT[:, t, t * P:(t + 1) * P], in_=AT[:, t, t * P:(t + 1) * P],
                                            compare_op=ALU.not_equal, fill=1.0, base=0, pattern=[[-1, P]],
                                            channel_multiplier=1).then_inc(at_ready, 1)

            @block.vector
            def _(dve):
                def own(ins):
                    after(dve, dve_own, ins)

                dve.wait_ge(edges_in, 32)
                nc.vector.tensor_copy(edges_f[:, :, :], edges_i[:, :, :]).then_inc(edge_rows, 1)
                dve.wait_ge(edge_rows, 1)
                dve.wait_ge(consts_ready, 1)
                own(nc.vector.tensor_reduce(sm[:, 0, 0:1], edges_f[:, 1, :], AX, ALU.min))
                own(nc.vector.tensor_reduce(sm[:, 0, 1:2], edges_f[:, 1, :], AX, ALU.max))
                own(nc.vector.tensor_scalar(sm[:, 1, :], tile_lo[:, :], sm[:, 0, 1:2], None, ALU.is_le))
                own(nc.vector.tensor_scalar(sm[:, 2, :], tile_lo[:, :], float(P), sm[:, 0, 0:1], ALU.add, ALU.is_gt))
                own(nc.vector.tensor_tensor(sm[:, 1, :], sm[:, 1, :], sm[:, 2, :], ALU.mult))
                nc.vector.tensor_scalar(sm[:, 3, :], sm[:, 1, :], chunk_down[:, 0:1], None, ALU.mult)
                nc.vector.tensor_scalar(sm[:, 4, :], sm[:, 1, :], chunk_up[:, 0:1], None, ALU.mult).then_inc(span, 1)
                dve.wait_ge(edge_T_ps, 1)
                nc.vector.tensor_copy(edges_T[:, :, :], PS[:, 0, 0:2 * P].rearrange("p (a b) -> p a b", a=2)).then_inc(edge_T_sb, 1)
                dve.wait_ge(span_ps, 1)
                own(nc.vector.tensor_reduce(sm[0:NT, 5, 0:1], PS[0:NT, 1, 0:P], AX, ALU.max))
                own(nc.vector.tensor_reduce(sm[0:NT, 6, 0:1], PS[0:NT, 1, P:2 * P], AX, ALU.max))
                own(nc.vector.tensor_scalar(sm[0:NT, 5, 0:1], sm[0:NT, 5, 0:1], -1.0, float(NCH), ALU.mult, ALU.add))
                own(nc.vector.tensor_scalar(sm[0:NT, 5, 0:1], sm[0:NT, 5, 0:1], float(NCH - 1), None, ALU.min))
                own(nc.vector.tensor_tensor(sm[0:NT, 6, 0:1], sm[0:NT, 6, 0:1], sm[0:NT, 5, 0:1], ALU.subtract))
                nc.vector.tensor_scalar(sm[0:NT, 6, 0:1], sm[0:NT, 6, 0:1], 1.0, None, ALU.max).then_inc(span_cols, 1)
                dve.wait_ge(span_row, 1)
                nc.vector.tensor_copy(etab[0:1, :], PS[0:1, 0, 256:256 + 2 * NT]).then_inc(etab_ready, 1)
                dve.wait_ge(etab_ready, 1)
                dve.wait_ge(edge_T_sb, 1)
                for t in range(NT):
                    first = dve.value_load(etab[0:1, t:t + 1], min_val=0, max_val=NCH - 1)
                    n = dve.value_load(etab[0:1, NT + t:NT + t + 1], min_val=1, max_val=NCH)
                    with dve.Fori(0, n) as j:
                        k = nc.s_assert_within(first + j, 0, NCH - 1,
                                               skip_runtime_bounds_check_because="a span ends at the last chunk")
                        dve.wait_ge(oh_free[t], j + 1)
                        nc.vector.tensor_scalar(oh_src[:, ds(j % NOH, 1), :], iota_h[:, :].rearrange("p (a n) -> p a n", a=1),
                                                edges_T[:, 0, ds(k, 1)], None, ALU.is_equal)
                        nc.vector.tensor_scalar(oh_dst[:, ds(j % NOH, 1), :],
                                                iota_h[:, t * P:(t + 1) * P].rearrange("p (a n) -> p a n", a=1),
                                                edges_T[:, 1, ds(k, 1)], None, ALU.is_equal).then_inc(oh_ready[t], 1)

            @block.tensor
            def _(pe):
                pe.wait_ge(consts_ready, 1)
                pe.wait_ge(edge_rows, 1)
                nc.tensor.transpose(PS[:, 0, 0:P], edges_f[:, 0, :], ident[:, :])
                nc.tensor.transpose(PS[:, 0, P:2 * P], edges_f[:, 1, :], ident[:, :]).then_inc(edge_T_ps, 1)
                pe.wait_ge(span, 1)
                nc.tensor.transpose(PS[0:NT, 1, 0:P], sm[:, 3, :], ident[:, :])
                nc.tensor.transpose(PS[0:NT, 1, P:2 * P], sm[:, 4, :], ident[:, :]).then_inc(span_ps, 1)
                pe.wait_ge(span_cols, 1)
                nc.tensor.matmul(PS[0:1, 0, 256:256 + NT], sm[0:NT, 5, 0:1], ident[0:NT, 0:NT], start=True, stop=True)
                nc.tensor.matmul(PS[0:1, 0, 256 + NT:256 + 2 * NT], sm[0:NT, 6, 0:1], ident[0:NT, 0:NT],
                                 start=True, stop=True).then_inc(span_row, 1)
                pe.wait_ge(etab_ready, 1)
                for t in range(NT):
                    n = pe.value_load(etab[0:1, NT + t:NT + t + 1], min_val=1, max_val=NCH)
                    if t >= 2:
                        pe.wait_ge(counts_copied, t - 1)
                    acc = [PS[:, 2 + 2 * (t % 2) + b, :] for b in range(2)]
                    for b in range(2):
                        last = nc.tensor.matmul(acc[b], zero_b[:, 0:P], zero_b[:, :], start=True, stop=False,
                                                skip_group_check=True)
                    last.then_inc(oh_free[t], NOH)
                    with pe.Fori(0, n) as j:
                        pe.wait_ge(oh_ready[t], j + 1)
                        for b in range(2):
                            last = nc.tensor.matmul(acc[b], oh_dst[:, ds(j % NOH, 1), :],
                                                    oh_src[:, ds(j % NOH, 1), b * HALF:(b + 1) * HALF], start=False,
                                                    stop=False, skip_group_check=True)
                        last.then_inc(oh_free[t], 1)
                    for b in range(2):
                        last = nc.tensor.matmul(acc[b], zero_b[:, 0:P], zero_b[:, :], start=False, stop=True,
                                                skip_group_check=True)
                    last.then_inc(counts_ps, 1)
                    if t == 0:
                        pe.wait_ge(gw_in, 16)
                        for dk in range(DK):
                            if dk >= 2:
                                pe.wait_ge(wt_sb, dk - 1)
                            for o in range(DK):
                                last = nc.tensor.transpose(PS[:, 6 + dk % 2, o * P:(o + 1) * P],
                                                           W_raw[:, o, dk * P:(dk + 1) * P], ident[:, :])
                            last.then_inc(wt_ps, 1)
                        pe.wait_ge(b1_in, 16)
                        pe.wait_ge(wt_sb, DK - 1)
                        nc.tensor.transpose(PS[:, 6, 0:E * HK], b1_rows[:, :], ident[0:E * HK, 0:E * HK]).then_inc(wt_ps, 1)

            @block.scalar
            def _(act):
                for t in range(NT):
                    act.wait_ge(counts_ps, t + 1)
                    if t >= 2:
                        act.wait_ge(counts_out[t % 2], 16 * (t // 2))
                        act.wait_ge(at_ready, t - 1)
                    nc.scalar.activation(ct_stage[:, t % 2, :],
                                         PS[:, 2 + 2 * (t % 2):4 + 2 * (t % 2), :].rearrange("p a b -> p (a b)"),
                                         ACT.Copy).then_inc(counts_copied, 1)
                    if t == 0:
                        for dk in range(DK):
                            act.wait_ge(wt_ps, dk + 1)
                            nc.scalar.activation(WT[:, dk, :], PS[:, 6 + dk % 2, :], ACT.Copy).then_inc(wt_sb, 1)
                        act.wait_ge(wt_ps, DK + 1)
                        nc.scalar.activation(b1T[:, :], PS[:, 6, 0:E * HK], ACT.Copy).then_inc(wt_sb, 1)

        def norm_stats(own, act_ready, act_done, wait_tile=None):
            for i in range(NT):
                nc.vector.bn_stats(bst[:, i, :], X[:, i, :])
            own(nc.vector.tensor_copy(sm[:, 7, 0:1], ones_f[:, :]))
            for i in range(NT):
                last = nc.vector.bn_aggr(mv[:, i, :], bst[:, i, :])
            last.then_inc(act_ready, 1)

        stats0, std0 = sem("stats0"), sem("std0")
        deg_ps, deg_sb, dinv_ready = sem("deg_ps"), sem("deg_sb"), sem("dinv_ready")
        wdeg_ps, xs_ready, mt_ps, mt_sb, out_ps, out_done = (
            sem(n) for n in "wdeg_ps xs_ready mt_ps mt_sb out_ps out_done".split())

        with nc.Block() as block:

            @block.tensor
            def _(pe):
                for i in range(NT):
                    for c in range(NT):
                        last = nc.tensor.matmul(PS[:, 0, i:i + 1], AT[:, c, i * P:(i + 1) * P], ones_f[:, :],
                                                start=(c == 0), stop=(c == NT - 1))
                last.then_inc(deg_ps, 1)
                pe.wait_ge(dinv_ready, 1)
                for i in range(NT):
                    for c in range(NT):
                        last = nc.tensor.matmul(PS[:, 1, i:i + 1], AT[:, c, i * P:(i + 1) * P], dinv[:, c:c + 1],
                                                start=(c == 0), stop=(c == NT - 1))
                last.then_inc(wdeg_ps, 1)
                pe.wait_ge(xs_ready, 1)
                for g in range(2 * DK):
                    dk, rh = g // 2, g % 2
                    if g >= 2:
                        pe.wait_ge(mt_sb, g - 1)
                    for c in range(NT):
                        last = nc.tensor.matmul(PS[:, 2 + g % 2, :], XN[:, c, dk * P:(dk + 1) * P],
                                                AT[:, c, rh * HALF:(rh + 1) * HALF], start=(c == 0), stop=(c == NT - 1))
                    last.then_inc(mt_ps, 1)
                pe.wait_ge(mt_sb, 2 * DK)
                for i in range(NT):
                    if i >= 2:
                        pe.wait_ge(out_done, i - 1)
                    for dk in range(DK):
                        last = nc.tensor.matmul(PS[:, 4 + i % 2, :], MT[:, dk, i * P:(i + 1) * P], WT[:, dk, :],
                                                start=(dk == 0), stop=(dk == DK - 1))
                    last.then_inc(out_ps, 1)

            @block.vector
            def _(dve):
                def own(ins):
                    after(dve, dve_own, ins)

                dve.wait_ge(x_in, 16)
                norm_stats(own, stats0, std0)
                dve.wait_ge(deg_ps, 1)
                nc.vector.tensor_copy(sm[:, 0, :], PS[:, 0, 0:NT]).then_inc(deg_sb, 1)
                dve.wait_ge(std0, 2)
                nc.vector.reciprocal(rstd[:, :], sm[:, 1, :])
                own(nc.vector.reciprocal(dinv[:, :], sm[:, 2, :]))
                own(nc.vector.tensor_tensor(rstd[:, :], rstd[:, :], dinv[:, :], ALU.mult))
                for i in range(NT):
                    last = nc.vector.tensor_scalar(XN[:, i, :], X[:, i, :], mv[:, i, 0:1], rstd[:, i:i + 1],
                                                   ALU.subtract, ALU.mult)
                    if i == 0:
                        last.then_inc(dinv_ready, 1)
                last.then_inc(xs_ready, 1)
                dve.wait_ge(wdeg_ps, 1)
                own(nc.vector.tensor_copy(wdeg[:, :], PS[:, 1, 0:NT]))
                dve.wait_ge(gb_in, 16)
                for i in range(NT):
                    dve.wait_ge(out_ps, i + 1)
                    own(nc.vector.scalar_tensor_tensor(PS[:, 4 + i % 2, :], bias_bc, wdeg[:, i:i + 1],
                                                       PS[:, 4 + i % 2, :], ALU.mult, ALU.add))
                    nc.vector.scalar_tensor_tensor(X[:, i, :], PS[:, 4 + i % 2, :], dinv[:, i:i + 1], X[:, i, :],
                                                   ALU.mult, ALU.add).then_inc(out_done, 1)

            @block.scalar
            def _(act):
                act.wait_ge(stats0, 1)
                nc.scalar.activation(sm[:, 1, :], mv[:, :, 1], ACT.Sqrt, bias=eps_t[:, 0:1]).then_inc(std0, 1)
                act.wait_ge(deg_sb, 1)
                nc.scalar.activation(sm[:, 2, :], sm[:, 0, :], ACT.Sqrt).then_inc(std0, 1)
                for g in range(2 * DK):
                    dk, rh = g // 2, g % 2
                    act.wait_ge(mt_ps, g + 1)
                    nc.scalar.activation(MT[:, dk, rh * HALF:(rh + 1) * HALF], PS[:, 2 + g % 2, :],
                                         ACT.Copy).then_inc(mt_sb, 1)
        def spread(ap, *shape):
            return ap.rearrange("p (n a) -> p n a", a=1).broadcast_to(list(shape))

        def over_tiles(ap, *shape):
            return ap.rearrange("p (a m) -> p a m", a=1).broadcast_to(list(shape))

        class Norm:
            def __init__(self, n):
                self.stats, self.std, self.normed = sem(f"stats_{n}"), sem(f"std_{n}"), sem(f"normed_{n}")
                self.xnt_ps, self.xnt_sb = sem(f"xnt_ps_{n}"), sem(f"xnt_sb_{n}")

        class Routing(Norm):
            def __init__(self, n):
                super().__init__(n)
                self.logits_ps, self.exp_in, self.exp_out = sem(f"logits_ps_{n}"), sem(f"exp_in_{n}"), sem(f"exp_out_{n}")
                self.mask_ready, self.pos_ps, self.dest_ready = sem(f"mask_ready_{n}"), sem(f"pos_ps_{n}"), sem(f"dest_ready_{n}")
                self.pairs_ready, self.pairs_ps, self.scattered = sem(f"pairs_ready_{n}"), sem(f"pairs_ps_{n}"), sem(f"scattered_{n}")

        route = [Routing(0), Routing(1)]

        def norm_tiles(dve_own_fn, r):
            norm_stats(dve_own_fn, r.stats, r.std)

        def norm_apply(own, dve, r):
            dve.wait_ge(r.std, 1)
            own(nc.vector.reciprocal(rstd[:, :], sm[:, 1, :]))
            for i in range(NT):
                nc.vector.tensor_scalar(XN[:, i, :], X[:, i, :], mv[:, i, 0:1], rstd[:, i:i + 1],
                                        ALU.subtract, ALU.mult).then_inc(r.normed, 1)

        def norm_std(act, r):
            act.wait_ge(r.stats, 1)
            nc.scalar.activation(sm[:, 1, :], mv[:, :, 1], ACT.Sqrt, bias=eps_t[:, 0:1]).then_inc(r.std, 1)

        def transposes_and_logits(pe, r, xnt, r_sb):
            for i in range(NT + 1):
                if i < NT:
                    pe.wait_ge(r.normed, i + 1)
                    if i >= 2:
                        pe.wait_ge(r.xnt_sb, i - 1)
                    for k in range(DK):
                        last = nc.tensor.transpose(PS[:, i % 2, k * P:(k + 1) * P], XN[:, i, k * P:(k + 1) * P],
                                                   ident[:, :])
                    last.then_inc(r.xnt_ps, 1)
                if i >= 1 and r_sb is not None:
                    pe.wait_ge(r.xnt_sb, i)
                    for k in range(DK):
                        last = nc.tensor.matmul(PS[:, 4, (i - 1) * E:i * E], xnt[:, i - 1, k, :], r_sb[:, k, :],
                                                start=(k == 0), stop=(k == DK - 1))
            if r_sb is not None:
                last.then_inc(r.logits_ps, 1)

        def xnt_copies(act, r, xnt):
            for i in range(NT):
                act.wait_ge(r.xnt_ps, i + 1)
                nc.scalar.activation(xnt[:, i, :, :], PS[:, i % 2, :].rearrange("p (k t) -> p k t", k=DK),
                                     ACT.Copy).then_inc(r.xnt_sb, 1)

        def top_two(own):
            for k in range(2):
                vals = rt[:, 0] if k == 0 else rt[:, 3]
                own(nc.vector.tensor_reduce(topv[:, k, :], vals, AX, ALU.max))
                own(nc.vector.tensor_tensor(rt[:, 4], vals, spread(topv[:, k, :], P, NT, E), ALU.is_equal))
                own(nc.vector.tensor_tensor(rt[:, 4], rt[:, 4], e_key[:, :, :], ALU.mult))
                own(nc.vector.tensor_reduce(sm[:, 0, :], rt[:, 4], AX, ALU.max))
                own(nc.vector.tensor_tensor(rt[:, 1 + k], rt[:, 4], spread(sm[:, 0, :], P, NT, E), ALU.is_equal))
                if k == 0:
                    own(nc.vector.scalar_tensor_tensor(rt[:, 3], rt[:, 1], -BIG, rt[:, 0], ALU.mult, ALU.add))

        def positions(pe, r):
            pe.wait_ge(r.mask_ready, 1)
            pos = PS[:, 0, 0:NT * E].rearrange("p (i e) -> p i e", i=NT)
            nc.tensor.matmul(PS[:, 0, 0:NT * E], upper_b[:, :], oh_b[:, :, :].rearrange("p i e -> p (i e)"),
                             start=True, stop=False)
            for i in range(NT - 1):
                nc.tensor.matmul(pos[:, i + 1:NT, :], ones_b[:, :],
                                 oh_b[:, i:i + 1, :].broadcast_to([P, NT - 1 - i, E]), start=False, stop=(i == NT - 2))
            for i in range(NT):
                last = nc.tensor.matmul(PS[:, 1, 0:E], ones_b[:, :], oh_b[:, i, :], start=(i == 0), stop=(i == NT - 1))
            last.then_inc(r.pos_ps, 1)

        def slot_tables(own, dve, r, tab, hots):
            dve.wait_ge(r.pos_ps, 1)
            own(nc.vector.tensor_tensor(cmp8[:, :, :], spread(PS[:, 1, 0:E], P, E, 8), k128[:, :, :], ALU.is_gt))
            own(nc.vector.tensor_reduce(nexp[:, 0, :], cmp8[:, :, :], AX, ALU.add))
            own(nc.vector.tensor_scalar(nexp[:, 0, :], nexp[:, 0, :], 1.0, None, ALU.add))
            own(nc.vector.tensor_tensor(cmp8[:, :, :], before[:, :, :], over_tiles(nexp[:, 0, :], P, E, E), ALU.mult))
            own(nc.vector.tensor_reduce(nexp[:, 1, :], cmp8[:, :, :], AX, ALU.add))
            own(nc.vector.tensor_scalar(nexp[:, 2, :], nexp[:, 1, :], float(P), None, ALU.mult))
            own(nc.vector.tensor_tensor(rt[:, 4], PS[:, 0, 0:NT * E].rearrange("p (i e) -> p i e", i=NT),
                                        over_tiles(nexp[:, 2, :], P, NT, E), ALU.add))
            for k, hot in enumerate(hots):
                own(nc.vector.tensor_tensor(rt[:, 3], rt[:, 4], hot, ALU.mult))
                own(nc.vector.tensor_reduce(dest[:, k, :], rt[:, 3], AX, ALU.add))
                nc.vector.tensor_copy(dest_i[:, k, :], dest[:, k, :])
            nc.vector.tensor_copy(tab[0:1, 0:2 * E].rearrange("p (a e) -> p a e", a=2), nexp[0:1, 0:2, :])
            nc.vector.tensor_tensor(tab[0:1, 2 * E:2 * E + 1], nexp[0:1, 0, E - 1:E], nexp[0:1, 1, E - 1:E],
                                    ALU.add).then_inc(r.dest_ready, 1)

        def scatter(pool, r, slots, choices):
            pool.wait_ge(r.dest_ready, 1)
            for k in range(choices):
                for i in range(NT):
                    nc.gpsimd.indirect_dma_start(slots, bass.IndirectOffsetOnAxis(dest_i[:, k, i:i + 1], 0),
                                                 XN[:, i, :], None).then_inc(r.scattered, 16)
            pool.wait_ge(r.scattered, 16 * NT * choices)

        hT = region(0, HK, P)
        gated = region(1024, H)
        v_biased = region(2048, HALF)
        gT = region(2560, HK, P)
        bg_bc = region(4096, 2, H)
        bv_bc = region(6144, H)
        b2_bc = region(7168, D)
        x_slot = region(7680, D)
        xT = region(8192, DK, P)
        y_slot = region(8704, D)

        def row_bc(ap, n):
            return ap.rearrange("(a d) -> a d", a=1).broadcast_to([P, n])

        with nc.Block() as block:
            r0 = route[0]

            @block.sync
            def _(sp):
                sp.dma_start(wv_sb[:, :, :], wv[0].rearrange("(k p) h -> p k h", p=P)).then_inc(wv_in, 16)
                for e in range(2):
                    sp.dma_start(bg_bc[:, e, :], row_bc(bg[e], H)).then_inc(bg_in[e], 16)
                sp.dma_start(bv_bc, row_bc(bv[0], H)).then_inc(bvb2_in[0], 16)
                sp.dma_start(b2_bc, row_bc(b2[0], D)).then_inc(bvb2_in[1], 16)

            @block.vector
            def _(dve):
                def own(ins):
                    after(dve, dve_own, ins)

                norm_tiles(own, r0)
                norm_apply(own, dve, r0)
                dve.wait_ge(r_in, 64)
                dve.wait_ge(r0.logits_ps, 1)
                own(nc.vector.tensor_tensor(rt[:, 0], PS[:, 4, 0:NT * E].rearrange("p (i e) -> p i e", i=NT),
                                            over_tiles(rb_bc[:, :], P, NT, E), ALU.add))
                own(nc.vector.tensor_reduce(sm[:, 0, :], rt[:, 0], AX, ALU.max))
                nc.vector.tensor_tensor(rt[:, 1], rt[:, 0], spread(sm[:, 0, :], P, NT, E), ALU.subtract).then_inc(r0.exp_in, 1)
                dve.wait_ge(r0.exp_out, 1)
                own(nc.vector.tensor_reduce(sm[:, 2, :], rt[:, 2], AX, ALU.add))
                own(nc.vector.reciprocal(sm[:, 3, :], sm[:, 2, :]))
                own(nc.vector.tensor_tensor(rt[:, 0], rt[:, 2], spread(sm[:, 3, :], P, NT, E), ALU.mult))
                top_two(own)
                nc.vector.tensor_copy(gate[:, :, :], topv[:, :, :])
                nc.vector.tensor_tensor(oh_b[:, :, :], rt[:, 1], rt[:, 2], ALU.add).then_inc(r0.mask_ready, 1)
                slot_tables(own, dve, r0, rtab, [rt[:, 1], rt[:, 2]])

            @block.scalar
            def _(act):
                norm_std(act, r0)
                xnt_copies(act, r0, XNT)
                act.wait_ge(r0.exp_in, 1)
                nc.scalar.activation(rt[:, 2], rt[:, 1], ACT.Exp).then_inc(r0.exp_out, 1)

            @block.tensor
            def _(pe):
                pe.wait_ge(r_in, 64)
                transposes_and_logits(pe, r0, XNT, rw_sb)
                positions(pe, r0)

            @block.gpsimd
            def _(pool):
                scatter(pool, r0, slots0_x, 2)

        (h_ps, xtr_ps, xT_ready, hT_ready, g_ps, v_ps, g_biased, silu_done, v_ready, gated_ready, gtr_ps, gT_ready,
         y_ps, y_free, y_sb, y_stored, xg_in) = (
            sem(n) for n in "h_ps xtr_ps xT_ready hT_ready g_ps v_ps g_biased silu_done v_ready gated_ready gtr_ps "
                            "gT_ready y_ps y_free y_sb y_stored xg_in".split())

        all_stored = sem("all_stored")
        y_filled = [sem(f"y_filled{i}") for i in range(2)]

        def slots_of(eng, tab, e):
            n = eng.value_load(tab[0:1, ds(e, 1)], min_val=1, max_val=NT)
            base = eng.value_load(tab[0:1, ds(E + e, 1)], min_val=0, max_val=SLOTS0 - 2)
            return n, base

        with nc.Block() as block:

            @block.sync
            def _(sp):
                sp.dma_start(w2_sb[:, :, :], w2[0].rearrange("(k p) d -> p k d", p=P)).then_inc(w2_in, 16)
                total = sp.value_load(rtab[0:1, 2 * E:2 * E + 1], min_val=E, max_val=SLOTS0 - 1)
                with sp.Fori(0, total) as s:
                    sp.sem_inc(y_filled[0], 16)
                with sp.Fori(total, SLOTS0) as s:
                    sp.dma_start(slots0_y[ds(s * P, P), :], slots0_x[ds(s * P, P), :]).then_inc(y_filled[0], 16)
                sp.wait_ge(y_filled[0], SLOTS0 * 16)
                for e in range(1, E):
                    done = sp.value_load(rtab[0:1, E + e:E + e + 1], min_val=1, max_val=SLOTS0 - 2)
                    sp.wait_ge(v_ps, done * 2)
                    sp.dma_start(wv_sb[:, :, :], wv[e].rearrange("(k p) h -> p k h", p=P)).then_inc(wv_in, 16)
                    sp.wait_ge(v_ready, done * 2)
                    sp.dma_start(bv_bc, row_bc(bv[e], H)).then_inc(bvb2_in[0], 16)
                    sp.wait_ge(y_ps, done)
                    sp.dma_start(w2_sb[:, :, :], w2[e].rearrange("(k p) d -> p k d", p=P)).then_inc(w2_in, 16)
                    sp.wait_ge(y_sb, done)
                    sp.dma_start(b2_bc, row_bc(b2[e], D)).then_inc(bvb2_in[1], 16)
                    if e + 1 < E:
                        q = (e + 1) % 2
                        sp.dma_start(w1_sb[:, q], w1[e + 1].rearrange("(k p) h -> p k h", p=P)).then_inc(w1_in[q], 16)
                        sp.dma_start(wg_sb[:, q], wg[e + 1].rearrange("(k p) h -> p k h", p=P)).then_inc(wg_in[q], 16)
                        sp.dma_start(bg_bc[:, q, :], row_bc(bg[e + 1], H)).then_inc(bg_in[q], 16)

            @block.gpsimd
            def _(pool):
                total = pool.value_load(rtab[0:1, 2 * E:2 * E + 1], min_val=E, max_val=SLOTS0 - 1)
                pool.dma_start(x_slot, slots0_x[0:P, :]).then_inc(xg_in, 16)
                with pool.Fori(1, total + 1) as s:
                    pool.wait_ge(xtr_ps, s)
                    pool.dma_start(x_slot, slots0_x[ds(s * P, P), :]).then_inc(xg_in, 16)

            @block.tensor
            def _(pe):
                def x_transposes():
                    for k in range(DK):
                        last = nc.tensor.transpose(PS[:, 7, k * P:(k + 1) * P], x_slot[:, k * P:(k + 1) * P], ident[:, :])
                    last.then_inc(xtr_ps, 1)

                def gate_or_value(w, half, bank, done):
                    for k in range(HK):
                        last = nc.tensor.matmul(PS[:, bank, :], hT[:, k, :], w[:, k, half * HALF:(half + 1) * HALF],
                                                start=(k == 0), stop=(k == HK - 1))
                    last.then_inc(done, 1)

                def gated_transposes(half):
                    for k in range(4):
                        at = half * HALF + k * P
                        last = nc.tensor.transpose(PS[:, half, k * P:(k + 1) * P], gated[:, at:at + P], ident[:, :])
                    last.then_inc(gtr_ps, 1)

                pe.wait_ge(xg_in, 16)
                x_transposes()
                with pe.Fori(0, E // 2) as pair:
                    for q in range(2):
                        n, base = slots_of(pe, rtab, pair * 2 + q)
                        with pe.Fori(0, n) as j:
                            s = base + j
                            pe.wait_ge(w1_in[q], pair * 16 + 16)
                            pe.wait_ge(xT_ready, s + 1)
                            for m in range(HK):
                                for k in range(DK):
                                    last = nc.tensor.matmul(PS[:, m // 4, (m % 4) * P:(m % 4 + 1) * P],
                                                            w1_sb[:, q, k, m * P:(m + 1) * P], xT[:, k, :],
                                                            start=(k == 0), stop=(k == DK - 1))
                                if m % 4 == 3:
                                    last.then_inc(h_ps, 1)
                            pe.wait_ge(xg_in, s * 16 + 32)
                            x_transposes()
                            pe.wait_ge(hT_ready, s * 2 + 2)
                            pe.wait_ge(wg_in[q], pair * 16 + 16)
                            gate_or_value(wg_sb[:, q], 0, 2, g_ps)
                            pe.wait_ge(wv_in, pair * 32 + 16 * q + 16)
                            gate_or_value(wv_sb, 0, 4, v_ps)
                            gate_or_value(wg_sb[:, q], 1, 3, g_ps)
                            pe.wait_ge(gated_ready, s * 2 + 1)
                            gated_transposes(0)
                            gate_or_value(wv_sb, 1, 5, v_ps)
                            pe.wait_ge(w2_in, pair * 32 + 16 * q + 16)
                            pe.wait_ge(y_free, s + 1)
                            for half in range(2):
                                if half == 1:
                                    pe.wait_ge(gated_ready, s * 2 + 2)
                                    gated_transposes(1)
                                pe.wait_ge(gT_ready, s * 2 + 1 + half)
                                for k in range(4 * half, 4 * half + 4):
                                    last = nc.tensor.matmul(PS[:, 6, :], gT[:, k, :], w2_sb[:, k, :],
                                                            start=(k == 0), stop=(k == HK - 1))
                            last.then_inc(y_ps, 1)

            @block.vector
            def _(dve):
                dve.sem_inc(y_free, 1)
                with dve.Fori(0, E // 2) as pair:
                    for q in range(2):
                        e = pair * 2 + q
                        n, base = slots_of(dve, rtab, e)
                        with dve.Fori(0, n) as j:
                            s = base + j
                            for half in range(2):
                                dve.wait_ge(h_ps, s * 2 + 1 + half)
                                bias = b1T[:, ds(e * HK + half * 4, 4)].rearrange("p (k a) -> p k a", a=1)
                                nc.vector.tensor_tensor(hT[:, 4 * half:4 * half + 4, :],
                                                        PS[:, half, :].rearrange("p (k t) -> p k t", k=4),
                                                        bias.broadcast_to([P, 4, P]), ALU.add).then_inc(hT_ready, 1)
                            dve.wait_ge(bg_in[q], pair * 16 + 16)
                            dve.wait_ge(bvb2_in[0], pair * 32 + 16 * q + 16)
                            for half in range(2):
                                cols = slice(half * HALF, (half + 1) * HALF)
                                dve.wait_ge(g_ps, s * 2 + 1 + half)
                                nc.vector.tensor_tensor(gated[:, cols], PS[:, 2 + half, :], bg_bc[:, q, cols],
                                                        ALU.add).then_inc(g_biased, 1)
                                dve.wait_ge(v_ps, s * 2 + 1 + half)
                                nc.vector.tensor_tensor(v_biased, PS[:, 4 + half, :], bv_bc[:, cols],
                                                        ALU.add).then_inc(v_ready, 1)
                                dve.wait_ge(v_ready, s * 2 + 1 + half)
                                dve.wait_ge(silu_done, s * 2 + 1 + half)
                                nc.vector.tensor_tensor(gated[:, cols], gated[:, cols], v_biased,
                                                        ALU.mult).then_inc(gated_ready, 1)
                            dve.wait_ge(bvb2_in[1], pair * 32 + 16 * q + 16)
                            dve.wait_ge(y_ps, s + 1)
                            dve.wait_ge(y_stored, s * 16 + 16)
                            nc.vector.tensor_tensor(y_slot, PS[:, 6, :], b2_bc, ALU.add).then_inc(y_sb, 1)
                            dve.wait_ge(y_sb, s + 1)
                            dve.sem_inc(y_free, 1)

            @block.scalar
            def _(act):
                def xT_copy():
                    nc.scalar.activation(xT, PS[:, 7, :].rearrange("p (k t) -> p k t", k=DK),
                                         ACT.Copy).then_inc(xT_ready, 1)

                act.sem_inc(y_stored, 16)
                act.wait_ge(xtr_ps, 1)
                xT_copy()
                total = act.value_load(rtab[0:1, 2 * E:2 * E + 1], min_val=E, max_val=SLOTS0 - 1)
                with act.Fori(0, total) as s:
                    act.wait_ge(xtr_ps, s + 2)
                    act.wait_ge(h_ps, s * 2 + 2)
                    xT_copy()
                    for half in range(2):
                        cols = slice(half * HALF, (half + 1) * HALF)
                        act.wait_ge(g_biased, s * 2 + 1 + half)
                        nc.scalar.activation(gated[:, cols], gated[:, cols], ACT.Silu).then_inc(silu_done, 1)
                    for half in range(2):
                        act.wait_ge(gtr_ps, s * 2 + 1 + half)
                        nc.scalar.activation(gT[:, 4 * half:4 * half + 4, :],
                                             PS[:, half, :].rearrange("p (k t) -> p k t", k=4),
                                             ACT.Copy).then_inc(gT_ready, 1)
                    act.wait_ge(y_sb, s + 1)
                    act.dma_start(slots0_y[ds(s * P, P), :], y_slot).then_inc(y_stored, 16)
                act.wait_ge(y_stored, total * 16 + 16)
                act.sem_inc(all_stored, 1)

        w1_flat = w1_sb[:, :, :, :].rearrange("p q k h -> p (q k h)")
        picked = w1_flat.rearrange("p (i k d) -> p i k d", i=NT, k=2)
        XNT1 = w1_flat[:, 0:NT * D].rearrange("p (i k t) -> p i k t", i=NT, k=DK)
        CT = wv_sb
        W12 = wg_sb[:, :, :, :].rearrange("p q k h -> p (q k h)").rearrange("p (e k h) -> p e k h", e=E, k=DK)
        W3 = wv_sb[:, :, :].rearrange("p k h -> p (k h)").rearrange("p (e k d) -> p e k d", e=E, k=HK1)
        wc_sb = region(4096, DK, D)
        wn_sb = region(6144, DK, D)
        bias1_bc = region(8192, D)
        picked_in = [sem(f"picked_in{i}") for i in range(NT)]
        counts_in, gnn1_in, w12_in, w3_in, added = (sem(n) for n in "counts_in gnn1_in w12_in w3_in added".split())
        indeg_ps, ut_ps, ut_sb, out1_ps, out1_done = (
            sem(n) for n in "indeg_ps ut_ps ut_sb out1_ps out1_done".split())
        mid = Norm("mid")

        with nc.Block() as block:

            @block.sync
            def _(sp):
                sp.dma_start(CT[:, :, :], counts_d.rearrange("t p s -> p t s")).then_inc(counts_in, 16)
                sp.dma_start(wc_sb, wc.rearrange("(k p) d -> p k d", p=P)).then_inc(gnn1_in, 16)
                sp.dma_start(wn_sb, wn.rearrange("(k p) d -> p k d", p=P)).then_inc(gnn1_in, 16)
                sp.dma_start(bias1_bc, row_bc(gnn1_b, D)).then_inc(gnn1_in, 16)
                for e in range(E):
                    sp.dma_start(W12[:, e, :, 0:H1], e1_w1[e].rearrange("(k p) h -> p k h", p=P)).then_inc(w12_in, 16)
                    sp.dma_start(W12[:, e, :, H1:2 * H1], e1_w2[e].rearrange("(k p) h -> p k h", p=P)).then_inc(w12_in, 16)

            @block.gpsimd
            def _(pool):
                for i in range(NT):
                    for k in range(2):
                        nc.gpsimd.indirect_dma_start(picked[:, i, k, :], None, slots0_y,
                                                     bass.IndirectOffsetOnAxis(dest_i[:, k, i:i + 1], 0)
                                                     ).then_inc(picked_in[i], 16)

            @block.vector
            def _(dve):
                def own(ins):
                    after(dve, dve_own, ins)

                for i in range(NT):
                    dve.wait_ge(picked_in[i], 32)
                    own(nc.vector.scalar_tensor_tensor(X[:, i, :], picked[:, i, 0, :], gate[:, 0, i:i + 1], X[:, i, :],
                                                       ALU.mult, ALU.add))
                    own(nc.vector.scalar_tensor_tensor(X[:, i, :], picked[:, i, 1, :], gate[:, 1, i:i + 1], X[:, i, :],
                                                       ALU.mult, ALU.add))
                norm_tiles(own, mid)
                norm_apply(own, dve, mid)
                dve.wait_ge(indeg_ps, 1)
                own(nc.vector.reciprocal(wdeg[:, :], PS[:, 5, 0:NT]))
                dve.wait_ge(gnn1_in, 48)
                for i in range(NT):
                    alpha, gamma = PS[:, 6 + i % 2, :], PS[:, 2 + i % 2, :]
                    own(nc.vector.tensor_tensor(X[:, i, :], X[:, i, :], bias1_bc, ALU.add))
                    dve.wait_ge(out1_ps, i + 1)
                    own(nc.vector.scalar_tensor_tensor(X[:, i, :], gamma, wdeg[:, i:i + 1], X[:, i, :], ALU.mult, ALU.add))
                    nc.vector.tensor_tensor(X[:, i, :], alpha, X[:, i, :], ALU.add).then_inc(out1_done, 1)

            @block.tensor
            def _(pe):
                pe.wait_ge(counts_in, 16)
                for i in range(NT):
                    for c in range(NT):
                        last = nc.tensor.matmul(PS[:, 5, i:i + 1], CT[:, c, i * P:(i + 1) * P], ones_f[:, :],
                                                start=(c == 0), stop=(c == NT - 1))
                last.then_inc(indeg_ps, 1)
                transposes_and_logits(pe, mid, XNT1, None)
                for g in range(2 * DK):
                    dk, rh = g // 2, g % 2
                    if g >= 2:
                        pe.wait_ge(ut_sb, g - 1)
                    for c in range(NT):
                        last = nc.tensor.matmul(PS[:, 2 + g % 2, :], XN[:, c, dk * P:(dk + 1) * P],
                                                CT[:, c, rh * HALF:(rh + 1) * HALF], start=(c == 0), stop=(c == NT - 1))
                    last.then_inc(ut_ps, 1)
                pe.wait_ge(ut_sb, 2 * DK)
                pe.wait_ge(mid.xnt_sb, NT)
                pe.wait_ge(gnn1_in, 48)
                for i in range(NT):
                    if i >= 2:
                        pe.wait_ge(out1_done, i - 1)
                    for k in range(DK):
                        nc.tensor.matmul(PS[:, 2 + i % 2, :], MT[:, k, i * P:(i + 1) * P], wn_sb[:, k, :],
                                         start=(k == 0), stop=(k == DK - 1))
                    for k in range(DK):
                        last = nc.tensor.matmul(PS[:, 6 + i % 2, :], XNT1[:, i, k, :], wc_sb[:, k, :],
                                                start=(k == 0), stop=(k == DK - 1))
                    last.then_inc(out1_ps, 1)

            @block.scalar
            def _(act):
                norm_std(act, mid)
                xnt_copies(act, mid, XNT1)
                for g in range(2 * DK):
                    dk, rh = g // 2, g % 2
                    act.wait_ge(ut_ps, g + 1)
                    nc.scalar.activation(MT[:, dk, rh * HALF:(rh + 1) * HALF], PS[:, 2 + g % 2, :],
                                         ACT.Copy).then_inc(ut_sb, 1)
        s_gate = sm[:, 4:6, :]
        kept = sm[:, 2:4, :]
        coef = gate
        with nc.Block() as block:
            r1 = route[1]

            @block.sync
            def _(sp):
                for e in range(E):
                    sp.dma_start(W3[:, e, :, :], e1_w3[e].rearrange("(k p) d -> p k d", p=P)).then_inc(w3_in, 16)

            @block.vector
            def _(dve):
                def own(ins):
                    after(dve, dve_own, ins)

                norm_tiles(own, r1)
                norm_apply(own, dve, r1)
                dve.wait_ge(r1.logits_ps, 1)
                own(nc.vector.tensor_tensor(rt[:, 0], PS[:, 4, 0:NT * E].rearrange("p (i e) -> p i e", i=NT),
                                            over_tiles(rb1_bc[:, :], P, NT, E), ALU.add))
                top_two(own)
                nc.vector.tensor_tensor(sm[:, 6, :], topv[:, 1, :], topv[:, 0, :], ALU.subtract).then_inc(r1.exp_in, 1)
                nc.vector.tensor_copy(oh_b[:, :, :], rt[:, 1])
                nc.vector.tensor_copy(oh2_b[:, :, :], rt[:, 2]).then_inc(r1.pairs_ready, 1)
                dve.wait_ge(r1.exp_out, 1)
                own(nc.vector.tensor_scalar(sm[:, 0, :], sm[:, 7, :], 1.0, None, ALU.add))
                own(nc.vector.reciprocal(s_gate[:, 0, :], sm[:, 0, :]))
                own(nc.vector.tensor_tensor(s_gate[:, 1, :], sm[:, 7, :], s_gate[:, 0, :], ALU.mult))
                dve.wait_ge(r1.pairs_ps, 1)
                own(nc.vector.tensor_copy(nexp[:, 0:2, :], PS[:, 5, 0:2 * E].rearrange("p (a e) -> p a e", a=2)))
                own(nc.vector.tensor_scalar(nexp[:, 0:2, :], nexp[:, 0:2, :], float(T), None, ALU.is_ge))
                for k in range(2):
                    own(nc.vector.tensor_tensor(rt[:, 4], rt[:, 1 + k], over_tiles(nexp[:, k, :], P, NT, E), ALU.mult))
                    own(nc.vector.tensor_reduce(kept[:, k, :], rt[:, 4], AX, ALU.add))
                    own(nc.vector.tensor_tensor(kept[:, k, :], kept[:, k, :], last_tok[:, :], ALU.mult))
                    own(nc.vector.tensor_scalar(kept[:, k, :], kept[:, k, :], -1.0, 1.0, ALU.mult, ALU.add))
                    own(nc.vector.tensor_tensor(rt[:, 4], rt[:, 1 + k], e_idx[:, :, :], ALU.mult))
                    own(nc.vector.tensor_reduce(dest[:, k, :], rt[:, 4], AX, ALU.add))
                    own(nc.vector.tensor_tensor(dest[:, k, :], dest[:, k, :], kept[:, k, :], ALU.mult))
                own(nc.vector.tensor_tensor(sm[:, 0, :], dest[:, 0, :], dest[:, 1, :], ALU.max))
                own(nc.vector.tensor_tensor(rt[:, 5], e_idx[:, :, :], spread(sm[:, 0, :], P, NT, E), ALU.is_equal))
                nc.vector.tensor_copy(oh_b[:, :, :], rt[:, 5]).then_inc(r1.mask_ready, 1)
                own(nc.vector.tensor_tensor(topv[:, :, :], s_gate, kept, ALU.mult))
                own(nc.vector.tensor_tensor(coef[:, 0, :], topv[:, 0, :], topv[:, 1, :], ALU.add))
                own(nc.vector.tensor_scalar(kept, kept, -1.0, 1.0, ALU.mult, ALU.add))
                own(nc.vector.tensor_tensor(topv[:, :, :], s_gate, kept, ALU.mult))
                own(nc.vector.tensor_tensor(coef[:, 1, :], topv[:, 0, :], topv[:, 1, :], ALU.add))
                slot_tables(own, dve, r1, rtab1, [rt[:, 5]])

            @block.scalar
            def _(act):
                norm_std(act, r1)
                xnt_copies(act, r1, XNT)
                act.wait_ge(r1.exp_in, 1)
                nc.scalar.activation(sm[:, 7, :], sm[:, 6, :], ACT.Exp).then_inc(r1.exp_out, 1)

            @block.tensor
            def _(pe):
                transposes_and_logits(pe, r1, XNT, rw1_sb)
                pe.wait_ge(r1.pairs_ready, 1)
                for i in range(NT):
                    nc.tensor.matmul(PS[:, 5, 0:E], ones_b[:, :], oh_b[:, i, :], start=(i == 0), stop=(i == NT - 1))
                for m, hot in enumerate((oh_b, oh2_b)):
                    for i in range(NT):
                        last = nc.tensor.matmul(PS[:, 5, E:2 * E], ones_b[:, :], hot[:, i, :], start=(m == 0 and i == 0),
                                                stop=(m == 1 and i == NT - 1))
                last.then_inc(r1.pairs_ps, 1)
                positions(pe, r1)

            @block.gpsimd
            def _(pool):
                scatter(pool, r1, slots1_x, 1)

        x1_slot = region(4096, D)
        x1T = region(4608, DK, P)
        y1_slot = region(5120, D)
        left = region(5632, H1)
        act_in = region(5888, H1)
        act_out = region(6144, H1)
        aT = region(6400, HK1, P)
        (ab_ps, x1tr_ps, x1T_ready, left_ready, prod_ready, gelu_done, atr_ps, aT_ready, y1_ps, y1_free, y1_sb,
         y1_stored, x1_in) = (
            sem(n) for n in "ab_ps x1tr_ps x1T_ready left_ready prod_ready gelu_done atr_ps aT_ready y1_ps y1_free y1_sb "
                            "y1_stored x1_in".split())
        with nc.Block() as block:

            @block.sync
            def _(sp):
                total = sp.value_load(rtab1[0:1, 2 * E:2 * E + 1], min_val=E, max_val=SLOTS1 - 1)
                with sp.Fori(0, total) as s:
                    sp.sem_inc(y_filled[1], 16)
                with sp.Fori(total, SLOTS1) as s:
                    sp.dma_start(slots1_y[ds(s * P, P), :], slots1_x[ds(s * P, P), :]).then_inc(y_filled[1], 16)
                sp.wait_ge(y_filled[1], SLOTS1 * 16)

            @block.gpsimd
            def _(pool):
                total = pool.value_load(rtab1[0:1, 2 * E:2 * E + 1], min_val=E, max_val=SLOTS1 - 1)
                pool.dma_start(x1_slot, slots1_x[0:P, :]).then_inc(x1_in, 16)
                with pool.Fori(1, total + 1) as s:
                    pool.wait_ge(x1tr_ps, s)
                    pool.dma_start(x1_slot, slots1_x[ds(s * P, P), :]).then_inc(x1_in, 16)

            @block.tensor
            def _(pe):
                def x_transposes():
                    for k in range(DK):
                        last = nc.tensor.transpose(PS[:, 7, k * P:(k + 1) * P], x1_slot[:, k * P:(k + 1) * P], ident[:, :])
                    last.then_inc(x1tr_ps, 1)

                pe.wait_ge(w12_in, 32 * E)
                pe.wait_ge(w3_in, 16 * E)
                pe.wait_ge(x1_in, 16)
                x_transposes()
                with pe.Fori(0, E) as e:
                    n = pe.value_load(rtab1[0:1, ds(e, 1)], min_val=1, max_val=NT)
                    base = pe.value_load(rtab1[0:1, ds(E + e, 1)], min_val=0, max_val=SLOTS1 - 2)
                    with pe.Fori(0, n) as j:
                        s = base + j
                        pe.wait_ge(x1T_ready, s + 1)
                        for k in range(DK):
                            last = nc.tensor.matmul(PS[:, 0, :], x1T[:, k, :], W12[:, ds(e, 1), k, :],
                                                    start=(k == 0), stop=(k == DK - 1))
                        last.then_inc(ab_ps, 1)
                        pe.wait_ge(x1_in, s * 16 + 32)
                        x_transposes()
                        pe.wait_ge(gelu_done, s + 1)
                        for k in range(HK1):
                            last = nc.tensor.transpose(PS[:, 1, k * P:(k + 1) * P], act_out[:, k * P:(k + 1) * P], ident[:, :])
                        last.then_inc(atr_ps, 1)
                        pe.wait_ge(aT_ready, s + 1)
                        pe.wait_ge(y1_free, s + 1)
                        for k in range(HK1):
                            last = nc.tensor.matmul(PS[:, 2, :], aT[:, k, :], W3[:, ds(e, 1), k, :],
                                                    start=(k == 0), stop=(k == HK1 - 1))
                        last.then_inc(y1_ps, 1)

            @block.vector
            def _(dve):
                dve.sem_inc(y1_free, 1)
                total = dve.value_load(rtab1[0:1, 2 * E:2 * E + 1], min_val=E, max_val=SLOTS1 - 1)
                with dve.Fori(0, total) as s:
                    dve.wait_ge(left_ready, s + 1)
                    nc.vector.tensor_tensor(act_in, PS[:, 0, H1:2 * H1], left, ALU.mult).then_inc(prod_ready, 1)
                    dve.wait_ge(atr_ps, s + 1)
                    nc.vector.tensor_copy(aT, PS[:, 1, 0:H1].rearrange("p (k t) -> p k t", k=HK1)).then_inc(aT_ready, 1)
                    dve.wait_ge(y1_ps, s + 1)
                    dve.wait_ge(y1_stored, s * 16 + 16)
                    nc.vector.tensor_copy(y1_slot, PS[:, 2, :]).then_inc(y1_sb, 1)
                    dve.wait_ge(y1_sb, s + 1)
                    dve.sem_inc(y1_free, 1)

            @block.scalar
            def _(act):
                def xT_copy():
                    nc.scalar.activation(x1T, PS[:, 7, :].rearrange("p (k t) -> p k t", k=DK),
                                         ACT.Copy).then_inc(x1T_ready, 1)

                act.sem_inc(y1_stored, 16)
                act.wait_ge(x1tr_ps, 1)
                xT_copy()
                total = act.value_load(rtab1[0:1, 2 * E:2 * E + 1], min_val=E, max_val=SLOTS1 - 1)
                with act.Fori(0, total) as s:
                    act.wait_ge(ab_ps, s + 1)
                    nc.scalar.activation(left, PS[:, 0, 0:H1], ACT.Copy).then_inc(left_ready, 1)
                    act.wait_ge(x1tr_ps, s + 2)
                    xT_copy()
                    act.wait_ge(prod_ready, s + 1)
                    nc.scalar.activation(act_out, act_in, ACT.Gelu).then_inc(gelu_done, 1)
                    act.wait_ge(y1_sb, s + 1)
                    act.dma_start(slots1_y[ds(s * P, P), :], y1_slot).then_inc(y1_stored, 16)
                act.wait_ge(y1_stored, total * 16 + 16)
                act.sem_inc(all_stored, 1)

        final_x, stored = sem("final_x"), sem("stored")
        with nc.Block() as block:

            @block.gpsimd
            def _(pool):
                for i in range(NT):
                    nc.gpsimd.indirect_dma_start(picked[:, i, 0, :], None, slots1_y,
                                                 bass.IndirectOffsetOnAxis(dest_i[:, 0, i:i + 1], 0)
                                                 ).then_inc(picked_in[i], 16)

            @block.vector
            def _(dve):
                def own(ins):
                    after(dve, dve_own, ins)

                for i in range(NT):
                    own(nc.vector.scalar_tensor_tensor(X[:, i, :], XN[:, i, :], coef[:, 1, i:i + 1], X[:, i, :],
                                                       ALU.mult, ALU.add))
                    dve.wait_ge(picked_in[i], 32 + 16)
                    nc.vector.scalar_tensor_tensor(X[:, i, :], picked[:, i, 0, :], coef[:, 0, i:i + 1], X[:, i, :],
                                                   ALU.mult, ALU.add).then_inc(final_x, 1)

            @block.sync
            def _(sp):
                for i in range(NT):
                    sp.wait_ge(final_x, i + 1)
                    sp.dma_start(out[i * P:(i + 1) * P, :], X[:, i, :]).then_inc(stored, 16)
                sp.wait_ge(stored, 16 * NT)


_INS = ['x', 'src', 'dst', 'L0_gnn_W', 'L0_gnn_b', 'L0_ffn_router_w', 'L0_ffn_router_b', 'L0_ffn_w1', 'L0_ffn_b1',
        'L0_ffn_wg', 'L0_ffn_bg', 'L0_ffn_wv', 'L0_ffn_bv', 'L0_ffn_w2', 'L0_ffn_b2', 'L1_gnn_wc', 'L1_gnn_wn',
        'L1_gnn_bias', 'L1_ffn_Wr', 'L1_ffn_br', 'L1_ffn_W1', 'L1_ffn_W2', 'L1_ffn_W3']
_OUTS = [((1024, 512), 'float32')]


def kernel(**inputs):
    import numpy as _np
    import concourse.bacc as _bacc
    from concourse import mybir as _mybir
    from concourse.bass_utils import run_bass_kernel_spmd as _run

    nc = _bacc.Bacc("TRN2", target_bir_lowering=False, num_devices=1)
    arrays, args = {}, []
    for name in _INS:
        a = _np.ascontiguousarray(inputs[name])
        arrays[f"in_{name}_dram"] = a
        args.append(nc.dram_tensor(f"in_{name}_dram", a.shape, _mybir.dt.from_np(a.dtype), kind="ExternalInput").ap())
    for i, (shape, dtype) in enumerate(_OUTS):
        dt = _mybir.dt.from_np(_np.dtype(dtype))
        args.append(nc.dram_tensor(f"out_{i}_dram", shape, dt, kind="ExternalOutput").ap())
    gnn_moe_two_layer_kernel(nc, *args)
    r = _run(nc, [arrays], core_ids=[0])
    got = tuple(r.results[0][f"out_{i}_dram"] for i in range(len(_OUTS)))
    return got[0]
```

```python
import concourse.bass as bass
from concourse import mybir
from contextlib import ExitStack


def gnn_moe_two_layer_kernel(
    nc, x, src, dst, gnn0_w, gnn0_b, router0_w, router0_b, w1, b1, wg, bg, wv, bv, w2, b2,
    wc, wn, gnn1_b, router1_w, router1_b, e1_w1, e1_w2, e1_w3, out,
):
    f32, bf16, f16, i32 = mybir.dt.float32, mybir.dt.bfloat16, mybir.dt.float16, mybir.dt.int32
    ALU = mybir.AluOpType
    ACT = mybir.ActivationFunctionType
    AX = mybir.AxisListType.X
    ds = bass.ds

    P = 128
    T, D = x.shape
    NT = T // P
    DK = D // P
    EDGES = src.shape[0]
    CG = 4
    NG = EDGES // (CG * P)
    E, _, H = w1.shape
    HK = H // P
    HALF = 512
    H1 = e1_w1.shape[2]
    HK1 = H1 // P
    SLOTS0 = 2 * T // P + E
    SLOTS1 = T // P + E
    NOH = 2
    EPS = 1e-5
    BIG = 1e30
    SPLIT = 2048.0

    ctx = ExitStack()
    with ctx:
        def sb(name, shape, dt=f32):
            return ctx.enter_context(nc.sbuf_tensor(name, shape, dt))

        def sem(name):
            return ctx.enter_context(nc.semaphore(name))

        def dram(name, shape, dt=f32):
            return nc.dram_tensor(name, shape, dt, kind="Internal").ap()

        counts_d = dram("edge_counts", [2, NT, P, T], f16)
        slots0_x = dram("slots0_x", [SLOTS0 * P, D])
        slots0_y = dram("slots0_y", [SLOTS0 * P, D])
        slots1_x = dram("slots1_x", [SLOTS1 * P, D])
        slots1_y = dram("slots1_y", [SLOTS1 * P, D])

        X = sb("X", [P, NT, D])
        w1_sb = sb("w1_sb", [P, 2, DK, H])
        wg_sb = sb("wg_sb", [P, 2, HK, H])
        wv_sb = sb("wv_sb", [P, HK, H])
        w2_sb = sb("w2_sb", [P, HK, D])
        R = sb("R", [P, 9216])

        def region(at, *shape, dt=f32):
            n = 1
            for m in shape:
                n *= m
            words = n if dt in (f32, i32) else n // 2
            v = R[:, at:at + words]
            if dt != f32:
                v = v.bitcast(dt)
            if len(shape) == 2:
                v = v.rearrange("p (a b) -> p a b", a=shape[0])
            if len(shape) == 3:
                v = v.rearrange("p (a b c) -> p a b c", a=shape[0], b=shape[1])
            return v

        half_flat = wg_sb[:, :, :, :].rearrange("p q k h -> p (q k h)").bitcast(f16)
        CAB = half_flat[:, 0:2 * NT * T].rearrange("p (m s) -> p m s", s=T)
        wv_flat = wv_sb[:, :, :].rearrange("p k h -> p (k h)")
        AT = wv_flat[:, 0:NT * T // 2].bitcast(f16).rearrange("p (t s) -> p t s", t=NT)
        split_flat = wv_flat[:, NT * T // 2:NT * T // 2 + NT * D].bitcast(f16)
        XA = split_flat[:, 0:NT * D].rearrange("p (i d) -> p i d", i=NT)
        XB = split_flat[:, NT * D:2 * NT * D].rearrange("p (i d) -> p i d", i=NT)
        w2_flat = w2_sb[:, :, :].rearrange("p a b -> p (a b)")
        MT = w2_flat.rearrange("p (k t) -> p k t", k=DK)
        XNT = w2_flat.rearrange("p (i k t) -> p i k t", i=NT, k=DK)
        ct_stage = region(0, 2, T)
        ca_stage = region(2048, 2, T, dt=f16)
        cb_stage = split_flat[:, 0:2 * T].rearrange("p (a s) -> p a s", a=2)
        oh_src = w2_flat[:, 0:NOH * CG * T // 2].bitcast(bf16).rearrange("p (a b n) -> p a b n", a=NOH, b=CG)
        oh_dst = region(3072, NOH, CG, P, dt=bf16)
        edges_T = region(3584, 2, CG, NG)
        b1_rows = region(3840, P)[0:E * HK]
        zero_b = region(4352, HALF, dt=bf16)
        edges_i = region(0, 2, CG * P, dt=i32)[0:NG]
        edges_f = region(1024, 2, CG * P)[0:NG]
        W_raw = region(4608, DK, D)
        WT = region(6656, DK, D)
        bias_bc = region(8704, D)
        XN = region(0, NT, D)
        zero_row = X[:, 0, :]

        ident = sb("ident", [P, P])
        iota_h = sb("iota_h", [P, T], f16)
        ones_b = sb("ones_b", [P, P], bf16)
        upper_b = sb("upper_b", [P, P], bf16)
        ones_f = sb("ones_f", [P, 1])
        eps_t = sb("eps_t", [P, 1])
        tile_lo = sb("tile_lo", [P, NT])
        chunk_up = sb("chunk_up", [P, 1])
        chunk_down = sb("chunk_down", [P, 1])
        e_key = sb("e_key", [P, NT, E])
        e_idx = sb("e_idx", [P, NT, E])
        k128 = sb("k128", [P, E, 8])
        before = sb("before", [P, E, E])
        last_tok = sb("last_tok", [P, NT])
        b1T = sb("b1T", [P, E * HK])
        etab = sb("etab", [1, 2 * NT], i32)
        parts = sb("parts", [1, 1], i32)
        rtab = sb("rtab", [1, 2 * E + 1], i32)
        rtab1 = sb("rtab1", [1, 2 * E + 1], i32)
        expert_of = sb("expert_of", [1, SLOTS1 + 1], i32)
        slot_idx = sb("slot_idx", [P, SLOTS1 + 1, E])
        slot_row = sb("slot_row", [P, SLOTS1 + 1])
        slot_cmp = region(8192, SLOTS1 + 1, E)
        sm = sb("sm", [P, 8, NT])
        mv = sb("mv", [P, NT, 2])
        bst = sb("bst", [P, NT, 6])
        rstd = sb("rstd", [P, NT])
        dinv = sb("dinv", [P, NT])
        wdeg = sb("wdeg", [P, NT])
        dinv_ab = sb("dinv_ab", [P, NT, 2], f16)
        rw_sb = sb("rw_sb", [P, DK, E])
        rb_bc = sb("rb_bc", [P, E])
        rw1_sb = sb("rw1_sb", [P, DK, E])
        rb1_bc = sb("rb1_bc", [P, E])
        rt = sb("rt", [P, 6, NT, E])
        cmp8 = sb("cmp8", [P, E, 8])
        oh_b = sb("oh_b", [P, NT, E], bf16)
        oh2_b = sb("oh2_b", [P, NT, E], bf16)
        topv = sb("topv", [P, 2, NT])
        gate = sb("gate", [P, 2, NT])
        nexp = sb("nexp", [P, 3, E])
        dest = sb("dest", [P, 2, NT])
        dest_i = sb("dest_i", [P, 2, NT], i32)
        PS = ctx.enter_context(nc.psum_tensor("PS", [P, 8, HALF], f32))

        dve_own, act_own, pool_own, pe_own = sem("dve_own"), sem("act_own"), sem("pool_own"), sem("pe_own")
        own_count = {}

        def after(eng, own, ins):
            own_count[id(own)] = own_count.get(id(own), 0) + 1
            ins.then_inc(own, 1)
            eng.wait_ge(own, own_count[id(own)])

        edges_in, x_in, gw_in, gb_in, b1_in, r_in, zeros_out = (
            sem(n) for n in "edges_in x_in gw_in gb_in b1_in r_in zeros_out".split())
        w1_in = [sem(f"w1_in{i}") for i in range(2)]
        wg_in = [sem(f"wg_in{i}") for i in range(2)]
        wv_in, w2_in = sem("wv_in"), sem("w2_in")
        bg_in = [sem(f"bg_in{i}") for i in range(2)]
        bvb2_in = [sem("bv_in"), sem("b2_in")]
        consts_ready = sem("consts_ready")
        oh_free = [sem(f"oh_free{t}") for t in range(NT)]
        oh_ready = [sem(f"oh_ready{t}") for t in range(NT)]
        counts_copied, at_ready = sem("counts_copied"), sem("at_ready")
        cb_made = sem("cb_made")
        counts_out = [sem(f"counts_out{i}") for i in range(2)]
        edge_rows, edge_T_ps, edge_T_sb, span, span_ps, span_cols, span_row, etab_ready = (
            sem(n) for n in "edge_rows edge_T_ps edge_T_sb span span_ps span_cols span_row etab_ready".split())
        wt_ps, wt_sb = sem("wt_ps"), sem("wt_sb")

        with nc.Block() as block:

            @block.sync
            def _(sp):
                sp.dma_start(edges_i[:, 0, :], src.rearrange("(k e) -> k e", e=CG * P)).then_inc(edges_in, 16)
                sp.dma_start(edges_i[:, 1, :], dst.rearrange("(k e) -> k e", e=CG * P)).then_inc(edges_in, 16)
                sp.dma_start(W_raw, gnn0_w.rearrange("(o p) d -> p o d", p=P)).then_inc(gw_in, 16)
                sp.dma_start(b1_rows[:, :], b1.rearrange("e (j p) -> (e j) p", p=P)).then_inc(b1_in, 16)
                sp.dma_start(X[:, :, :], x.rearrange("(i p) d -> p i d", p=P)).then_inc(x_in, 16)
                sp.dma_start(bias_bc, gnn0_b.rearrange("(a d) -> a d", a=1).broadcast_to([P, D])).then_inc(gb_in, 16)
                for r_sb, rb, r_dram, rb_dram in ((rw_sb, rb_bc, router0_w, router0_b),
                                                  (rw1_sb, rb1_bc, router1_w, router1_b)):
                    sp.dma_start(r_sb[:, :, :], r_dram.rearrange("(k p) e -> p k e", p=P)).then_inc(r_in, 16)
                    sp.dma_start(rb[:, :], rb_dram.rearrange("(a e) -> a e", a=1).broadcast_to([P, E])).then_inc(r_in, 16)
                sp.wait_ge(consts_ready, 1)
                zeros = zero_b.bitcast(f32).rearrange("p (a d) -> p a d", a=1)
                for slots, n in ((slots0_x, SLOTS0), (slots1_x, SLOTS1)):
                    sp.dma_start(slots.rearrange("(p s) d -> p (s d)", p=P).rearrange("p (m c) -> p m c", c=D // 2),
                                 zeros.broadcast_to([P, 2 * n, D // 2])).then_inc(zeros_out, 16)
                for t in range(NT):
                    sp.wait_ge(counts_copied, t + 1)
                    sp.dma_start(counts_d[0, t], ca_stage[:, t % 2, :]).then_inc(counts_out[t % 2], 16)
                    sp.wait_ge(cb_made, t + 1)
                    sp.dma_start(counts_d[1, t], cb_stage[:, t % 2, :]).then_inc(counts_out[t % 2], 16)
                    if t == 0:
                        for e in range(2):
                            sp.dma_start(w1_sb[:, e], w1[e].rearrange("(k p) h -> p k h", p=P)).then_inc(w1_in[e], 16)
                            sp.dma_start(wg_sb[:, e], wg[e].rearrange("(k p) h -> p k h", p=P)).then_inc(wg_in[e], 16)
                for i in range(2):
                    sp.wait_ge(counts_out[i], 32 * (NT // 2))
                sp.wait_ge(zeros_out, 32)

            @block.gpsimd
            def _(pool):
                def own(ins):
                    after(pool, pool_own, ins)

                own(nc.gpsimd.memset(ident[:, :], 0.0))
                own(nc.gpsimd.affine_select(out=ident[:, :], in_=ident[:, :], compare_op=ALU.not_equal, fill=1.0,
                                            base=0, pattern=[[-1, P]], channel_multiplier=1))
                own(nc.gpsimd.iota(tile_lo[:, :], [[P, NT]], base=0, channel_multiplier=0,
                                   allow_small_or_imprecise_dtypes=True))
                own(nc.gpsimd.iota(chunk_up[:, :], [[0, 1]], base=1, channel_multiplier=1,
                                   allow_small_or_imprecise_dtypes=True))
                own(nc.gpsimd.iota(chunk_down[:, :], [[0, 1]], base=NG, channel_multiplier=-1,
                                   allow_small_or_imprecise_dtypes=True))
                own(nc.gpsimd.memset(zero_b, 0.0))
                nc.gpsimd.iota(iota_h[:, :], [[1, T]], base=0, channel_multiplier=0,
                               allow_small_or_imprecise_dtypes=True).then_inc(consts_ready, 1)
                own(nc.gpsimd.memset(ones_b[:, :], 1.0))
                own(nc.gpsimd.memset(ones_f[:, :], 1.0))
                own(nc.gpsimd.memset(eps_t[:, :], EPS))
                own(nc.gpsimd.affine_select(out=upper_b[:, :], in_=ones_b[:, :], compare_op=ALU.is_gt, fill=0.0,
                                            base=0, pattern=[[1, P]], channel_multiplier=-1))
                own(nc.gpsimd.iota(e_key[:, :, :], [[0, NT], [-1, E]], base=E, channel_multiplier=0,
                                   allow_small_or_imprecise_dtypes=True))
                own(nc.gpsimd.iota(e_idx[:, :, :], [[0, NT], [1, E]], base=0, channel_multiplier=0,
                                   allow_small_or_imprecise_dtypes=True))
                own(nc.gpsimd.iota(k128[:, :, :], [[0, E], [P, 8]], base=P, channel_multiplier=0,
                                   allow_small_or_imprecise_dtypes=True))
                own(nc.gpsimd.memset(before[:, :, :], 1.0))
                own(nc.gpsimd.affine_select(out=before[:, :, :], in_=before[:, :, :], compare_op=ALU.is_gt, fill=0.0,
                                            base=0, pattern=[[1, E], [-1, E]], channel_multiplier=0))
                own(nc.gpsimd.iota(slot_idx[:, :, :], [[1, SLOTS1 + 1], [0, E]], base=0, channel_multiplier=0,
                                   allow_small_or_imprecise_dtypes=True))
                own(nc.gpsimd.memset(last_tok[:, :], 0.0))
                own(nc.gpsimd.affine_select(out=last_tok[:, :], in_=last_tok[:, :], compare_op=ALU.not_equal, fill=1.0,
                                            base=-(T - 1), pattern=[[P, NT]], channel_multiplier=1))
                for t in range(NT):
                    pool.wait_ge(counts_copied, t + 1)
                    if t >= 2:
                        pool.wait_ge(counts_out[t % 2], 32 * (t // 2))
                    nc.gpsimd.tensor_tensor(cb_stage[:, t % 2, :], ct_stage[:, t % 2, :], ca_stage[:, t % 2, :],
                                            ALU.subtract).then_inc(cb_made, 1)
                    own(nc.gpsimd.tensor_scalar(AT[:, t, :], ct_stage[:, t % 2, :], 1.0, None, ALU.min))
                    nc.gpsimd.affine_select(out=AT[:, t, t * P:(t + 1) * P], in_=AT[:, t, t * P:(t + 1) * P],
                                            compare_op=ALU.not_equal, fill=1.0, base=0, pattern=[[-1, P]],
                                            channel_multiplier=1).then_inc(at_ready, 1)

            @block.vector
            def _(dve):
                def own(ins):
                    after(dve, dve_own, ins)

                dve.wait_ge(edges_in, 32)
                nc.vector.tensor_copy(edges_f[:, :, :], edges_i[:, :, :]).then_inc(edge_rows, 1)
                dve.wait_ge(edge_rows, 1)
                dve.wait_ge(consts_ready, 1)
                g = slice(0, NG)
                own(nc.vector.tensor_reduce(sm[g, 0, 0:1], edges_f[:, 1, :], AX, ALU.min))
                own(nc.vector.tensor_reduce(sm[g, 0, 1:2], edges_f[:, 1, :], AX, ALU.max))
                own(nc.vector.tensor_scalar(sm[g, 1, :], tile_lo[g, :], sm[g, 0, 1:2], None, ALU.is_le))
                own(nc.vector.tensor_scalar(sm[g, 2, :], tile_lo[g, :], float(P), sm[g, 0, 0:1], ALU.add, ALU.is_gt))
                own(nc.vector.tensor_tensor(sm[g, 1, :], sm[g, 1, :], sm[g, 2, :], ALU.mult))
                nc.vector.tensor_scalar(sm[g, 3, :], sm[g, 1, :], chunk_down[g, 0:1], None, ALU.mult)
                nc.vector.tensor_scalar(sm[g, 4, :], sm[g, 1, :], chunk_up[g, 0:1], None, ALU.mult).then_inc(span, 1)
                dve.wait_ge(edge_T_ps, 1)
                nc.vector.tensor_copy(edges_T[:, :, :, :], PS[:, 0, 0:2 * CG * NG].rearrange("p (a b k) -> p a b k", a=2, b=CG)
                                      ).then_inc(edge_T_sb, 1)
                dve.wait_ge(span_ps, 1)
                own(nc.vector.tensor_reduce(sm[0:NT, 5, 0:1], PS[0:NT, 1, 0:NG], AX, ALU.max))
                own(nc.vector.tensor_reduce(sm[0:NT, 6, 0:1], PS[0:NT, 1, NG:2 * NG], AX, ALU.max))
                own(nc.vector.tensor_scalar(sm[0:NT, 5, 0:1], sm[0:NT, 5, 0:1], -1.0, float(NG), ALU.mult, ALU.add))
                own(nc.vector.tensor_scalar(sm[0:NT, 5, 0:1], sm[0:NT, 5, 0:1], float(NG - 1), None, ALU.min))
                own(nc.vector.tensor_tensor(sm[0:NT, 6, 0:1], sm[0:NT, 6, 0:1], sm[0:NT, 5, 0:1], ALU.subtract))
                nc.vector.tensor_scalar(sm[0:NT, 6, 0:1], sm[0:NT, 6, 0:1], 1.0, None, ALU.max).then_inc(span_cols, 1)
                dve.wait_ge(span_row, 1)
                nc.vector.tensor_copy(etab[0:1, :], PS[0:1, 1, 256:256 + 2 * NT]).then_inc(etab_ready, 1)
                dve.wait_ge(etab_ready, 1)
                dve.wait_ge(edge_T_sb, 1)
                for t in range(NT):
                    first = dve.value_load(etab[0:1, t:t + 1], min_val=0, max_val=NG - 1)
                    n = dve.value_load(etab[0:1, NT + t:NT + t + 1], min_val=1, max_val=NG)
                    with dve.Fori(0, n) as j:
                        k = nc.s_assert_within(first + j, 0, NG - 1,
                                               skip_runtime_bounds_check_because="a span ends at the last group")
                        dve.wait_ge(oh_free[t], j + 1)
                        buf = dve.snap(j % NOH)
                        for c in range(CG):
                            nc.vector.tensor_scalar(oh_dst[:, ds(buf, 1), c, :],
                                                    iota_h[:, t * P:(t + 1) * P].rearrange("p (a n) -> p a n", a=1),
                                                    edges_T[:, 1, c, ds(k, 1)], None, ALU.is_equal)
                            last = nc.vector.tensor_scalar(oh_src[:, ds(buf, 1), c, :],
                                                           iota_h[:, :].rearrange("p (a n) -> p a n", a=1),
                                                           edges_T[:, 0, c, ds(k, 1)], None, ALU.is_equal)
                        last.then_inc(oh_ready[t], 1)

            @block.tensor
            def _(pe):
                pe.wait_ge(consts_ready, 1)
                pe.wait_ge(edge_rows, 1)
                for m in range(2 * CG):
                    last = nc.tensor.transpose(PS[:, 0, m * NG:(m + 1) * NG], edges_f[:, m // CG, m % CG * P:(m % CG + 1) * P],
                                               ident[0:NG, 0:NG])
                last.then_inc(edge_T_ps, 1)
                pe.wait_ge(span, 1)
                nc.tensor.transpose(PS[0:NT, 1, 0:NG], sm[0:NG, 3, :], ident[0:NG, 0:NG])
                nc.tensor.transpose(PS[0:NT, 1, NG:2 * NG], sm[0:NG, 4, :], ident[0:NG, 0:NG]).then_inc(span_ps, 1)
                pe.wait_ge(span_cols, 1)
                nc.tensor.matmul(PS[0:1, 1, 256:256 + NT], sm[0:NT, 5, 0:1], ident[0:NT, 0:NT], start=True, stop=True)
                nc.tensor.matmul(PS[0:1, 1, 256 + NT:256 + 2 * NT], sm[0:NT, 6, 0:1], ident[0:NT, 0:NT],
                                 start=True, stop=True).then_inc(span_row, 1)
                pe.wait_ge(etab_ready, 1)
                for t in range(NT):
                    n = pe.value_load(etab[0:1, NT + t:NT + t + 1], min_val=1, max_val=NG)
                    if t >= 2:
                        pe.wait_ge(counts_copied, t - 1)
                    acc = [PS[:, 2 + 2 * (t % 2) + b, :] for b in range(2)]
                    for b in range(2):
                        last = nc.tensor.matmul(acc[b], zero_b[:, 0:P], zero_b[:, :], start=True, stop=False,
                                                skip_group_check=True)
                    last.then_inc(oh_free[t], NOH)
                    with pe.Fori(0, n) as j:
                        pe.wait_ge(oh_ready[t], j + 1)
                        buf = pe.snap(j % NOH)
                        for c in range(CG):
                            for b in range(2):
                                last = nc.tensor.matmul(acc[b], oh_dst[:, ds(buf, 1), c, :],
                                                        oh_src[:, ds(buf, 1), c, b * HALF:(b + 1) * HALF], start=False,
                                                        stop=True, skip_group_check=True)
                        last.then_inc(oh_free[t], 1)

            @block.scalar
            def _(act):
                act.wait_ge(etab_ready, 1)
                for t in range(NT):
                    n = act.value_load(etab[0:1, NT + t:NT + t + 1], min_val=1, max_val=NG)
                    act.wait_ge(oh_free[t], n + NOH)
                    if t >= 2:
                        act.wait_ge(counts_out[t % 2], 32 * (t // 2))
                        act.wait_ge(at_ready, t - 1)
                    counts = PS[:, 2 + 2 * (t % 2):4 + 2 * (t % 2), :].rearrange("p a b -> p (a b)")
                    nc.scalar.activation(ct_stage[:, t % 2, :], counts, ACT.Copy)
                    nc.scalar.activation(ca_stage[:, t % 2, :], counts, ACT.Copy).then_inc(counts_copied, 1)

        def norm_stats(own, act_ready, act_done, wait_tile=None):
            for i in range(NT):
                nc.vector.bn_stats(bst[:, i, :], X[:, i, :])
            own(nc.vector.tensor_copy(sm[:, 7, 0:1], ones_f[:, :]))
            for i in range(NT):
                last = nc.vector.bn_aggr(mv[:, i, :], bst[:, i, :])
            last.then_inc(act_ready, 1)

        stats0, std0 = sem("stats0"), sem("std0")
        deg_ps, deg_sb, dinv_ready = sem("deg_ps"), sem("deg_sb"), sem("dinv_ready")
        xn_ready, xa_ready = sem("xn_ready"), sem("xa_ready")
        wdeg_ps, xs_ready, mt_ps, mt_sb, out_ps, out_done = (
            sem(n) for n in "wdeg_ps xs_ready mt_ps mt_sb out_ps out_done".split())

        with nc.Block() as block:

            @block.tensor
            def _(pe):
                for i in range(NT):
                    for c in range(NT):
                        last = nc.tensor.matmul(PS[:, 0, i:i + 1], AT[:, c, i * P:(i + 1) * P], ones_b[:, 0:1],
                                                start=(c == 0), stop=(c == NT - 1))
                last.then_inc(deg_ps, 1)
                pe.wait_ge(gw_in, 16)
                for dk in range(DK):
                    for o in range(DK):
                        last = nc.tensor.transpose(PS[:, 4 + dk, o * P:(o + 1) * P],
                                                   W_raw[:, o, dk * P:(dk + 1) * P], ident[:, :])
                    last.then_inc(wt_ps, 1)
                pe.wait_ge(b1_in, 16)
                nc.tensor.transpose(PS[:, 2, 0:E * HK], b1_rows[:, :], ident[0:E * HK, 0:E * HK]).then_inc(wt_ps, 1)
                pe.wait_ge(dinv_ready, 1)
                for i in range(NT):
                    for c in range(NT):
                        last = nc.tensor.matmul(PS[:, 1, 2 * i:2 * i + 2], AT[:, c, i * P:(i + 1) * P], dinv_ab[:, c, :],
                                                start=(c == 0), stop=(c == NT - 1))
                last.then_inc(wdeg_ps, 1)
                pe.wait_ge(xs_ready, NT)
                for g in range(2 * DK):
                    dk, rh = g // 2, g % 2
                    if g >= 2:
                        pe.wait_ge(mt_sb, g - 1)
                    else:
                        pe.wait_ge(wt_sb, DK + 1)
                    for m, part in enumerate((XA, XB)):
                        for c in range(NT):
                            last = nc.tensor.matmul(PS[:, 2 + g % 2, :], part[:, c, dk * P:(dk + 1) * P],
                                                    AT[:, c, rh * HALF:(rh + 1) * HALF], start=(m == 0 and c == 0),
                                                    stop=(m == 1 and c == NT - 1))
                    last.then_inc(mt_ps, 1)
                pe.wait_ge(mt_sb, 2 * DK)
                for i in range(NT):
                    if i >= 2:
                        pe.wait_ge(out_done, i - 1)
                    for dk in range(DK):
                        last = nc.tensor.matmul(PS[:, 4 + i % 2, :], MT[:, dk, i * P:(i + 1) * P], WT[:, dk, :],
                                                start=(dk == 0), stop=(dk == DK - 1))
                    last.then_inc(out_ps, 1)

            @block.vector
            def _(dve):
                def own(ins):
                    after(dve, dve_own, ins)

                dve.wait_ge(x_in, 16)
                norm_stats(own, stats0, std0)
                dve.wait_ge(deg_ps, 1)
                nc.vector.tensor_copy(sm[:, 0, :], PS[:, 0, 0:NT]).then_inc(deg_sb, 1)
                dve.wait_ge(std0, 2)
                nc.vector.reciprocal(rstd[:, :], sm[:, 1, :])
                own(nc.vector.reciprocal(dinv[:, :], sm[:, 2, :]))
                own(nc.vector.scalar_tensor_tensor(rstd[:, :], rstd[:, :], SPLIT, dinv[:, :], ALU.mult, ALU.mult))
                own(nc.vector.tensor_scalar(dinv_ab[:, :, 0], dinv[:, :], SPLIT, None, ALU.mult))
                nc.vector.scalar_tensor_tensor(dinv_ab[:, :, 1], dinv[:, :], SPLIT, dinv_ab[:, :, 0], ALU.mult,
                                               ALU.subtract).then_inc(dinv_ready, 1)
                for i in range(NT + 1):
                    if i < NT:
                        nc.vector.tensor_scalar(XN[:, i, :], X[:, i, :], mv[:, i, 0:1], rstd[:, i:i + 1],
                                                ALU.subtract, ALU.mult).then_inc(xn_ready, 1)
                    if i >= 1:
                        dve.wait_ge(xa_ready, i)
                        nc.vector.tensor_tensor(XB[:, i - 1, :], XN[:, i - 1, :], XA[:, i - 1, :],
                                                ALU.subtract).then_inc(xs_ready, 1)
                dve.wait_ge(wdeg_ps, 1)
                own(nc.vector.tensor_reduce(wdeg[:, :], PS[:, 1, 0:2 * NT].rearrange("p (i a) -> p i a", a=2), AX, ALU.add))
                own(nc.vector.tensor_scalar(wdeg[:, :], wdeg[:, :], 1.0 / SPLIT, None, ALU.mult))
                dve.wait_ge(gb_in, 16)
                for i in range(NT):
                    dve.wait_ge(out_ps, i + 1)
                    own(nc.vector.scalar_tensor_tensor(PS[:, 4 + i % 2, :], bias_bc, wdeg[:, i:i + 1],
                                                       PS[:, 4 + i % 2, :], ALU.mult, ALU.add))
                    nc.vector.scalar_tensor_tensor(X[:, i, :], PS[:, 4 + i % 2, :], dinv[:, i:i + 1], X[:, i, :],
                                                   ALU.mult, ALU.add).then_inc(out_done, 1)

            @block.scalar
            def _(act):
                act.wait_ge(stats0, 1)
                nc.scalar.activation(sm[:, 1, :], mv[:, :, 1], ACT.Sqrt, bias=eps_t[:, 0:1]).then_inc(std0, 1)
                act.wait_ge(deg_sb, 1)
                nc.scalar.activation(sm[:, 2, :], sm[:, 0, :], ACT.Sqrt).then_inc(std0, 1)
                for dk in range(DK):
                    act.wait_ge(wt_ps, dk + 1)
                    nc.scalar.activation(WT[:, dk, :], PS[:, 4 + dk, :], ACT.Copy).then_inc(wt_sb, 1)
                act.wait_ge(wt_ps, DK + 1)
                nc.scalar.activation(b1T[:, :], PS[:, 2, 0:E * HK], ACT.Copy).then_inc(wt_sb, 1)
                for i in range(NT):
                    act.wait_ge(xn_ready, i + 1)
                    nc.scalar.activation(XA[:, i, :], XN[:, i, :], ACT.Copy).then_inc(xa_ready, 1)
                for g in range(2 * DK):
                    dk, rh = g // 2, g % 2
                    act.wait_ge(mt_ps, g + 1)
                    nc.scalar.activation(MT[:, dk, rh * HALF:(rh + 1) * HALF], PS[:, 2 + g % 2, :], ACT.Copy,
                                         scale=1.0 / SPLIT).then_inc(mt_sb, 1)
        def spread(ap, *shape):
            return ap.rearrange("p (n a) -> p n a", a=1).broadcast_to(list(shape))

        def over_tiles(ap, *shape):
            return ap.rearrange("p (a m) -> p a m", a=1).broadcast_to(list(shape))

        class Norm:
            def __init__(self, n):
                self.stats, self.std, self.normed = sem(f"stats_{n}"), sem(f"std_{n}"), sem(f"normed_{n}")
                self.xnt_ps, self.xnt_sb = sem(f"xnt_ps_{n}"), sem(f"xnt_sb_{n}")

        class Routing(Norm):
            def __init__(self, n):
                super().__init__(n)
                self.logits_ps, self.exp_in, self.exp_out = sem(f"logits_ps_{n}"), sem(f"exp_in_{n}"), sem(f"exp_out_{n}")
                self.mask_ready, self.pos_ps, self.dest_ready = sem(f"mask_ready_{n}"), sem(f"pos_ps_{n}"), sem(f"dest_ready_{n}")
                self.pairs_ready, self.pairs_ps, self.scattered = sem(f"pairs_ready_{n}"), sem(f"pairs_ps_{n}"), sem(f"scattered_{n}")

        route = [Routing(0), Routing(1)]

        def norm_tiles(dve_own_fn, r):
            norm_stats(dve_own_fn, r.stats, r.std)

        def norm_apply(own, dve, r):
            dve.wait_ge(r.std, 1)
            own(nc.vector.reciprocal(rstd[:, :], sm[:, 1, :]))
            for i in range(NT):
                nc.vector.tensor_scalar(XN[:, i, :], X[:, i, :], mv[:, i, 0:1], rstd[:, i:i + 1],
                                        ALU.subtract, ALU.mult).then_inc(r.normed, 1)

        def norm_std(act, r):
            act.wait_ge(r.stats, 1)
            nc.scalar.activation(sm[:, 1, :], mv[:, :, 1], ACT.Sqrt, bias=eps_t[:, 0:1]).then_inc(r.std, 1)

        def transposes_and_logits(pe, r, xnt, r_sb):
            for i in range(NT + 1):
                if i < NT:
                    pe.wait_ge(r.normed, i + 1)
                    if i >= 2:
                        pe.wait_ge(r.xnt_sb, i - 1)
                    for k in range(DK):
                        last = nc.tensor.transpose(PS[:, i % 2, k * P:(k + 1) * P], XN[:, i, k * P:(k + 1) * P],
                                                   ident[:, :])
                    last.then_inc(r.xnt_ps, 1)
                if i >= 1 and r_sb is not None:
                    pe.wait_ge(r.xnt_sb, i)
                    for k in range(DK):
                        last = nc.tensor.matmul(PS[:, 4, (i - 1) * E:i * E], xnt[:, i - 1, k, :], r_sb[:, k, :],
                                                start=(k == 0), stop=(k == DK - 1))
            if r_sb is not None:
                last.then_inc(r.logits_ps, 1)

        def xnt_copies(act, r, xnt):
            for i in range(NT):
                act.wait_ge(r.xnt_ps, i + 1)
                nc.scalar.activation(xnt[:, i, :, :], PS[:, i % 2, :].rearrange("p (k t) -> p k t", k=DK),
                                     ACT.Copy).then_inc(r.xnt_sb, 1)

        def top_two(own):
            for k in range(2):
                vals = rt[:, 0] if k == 0 else rt[:, 3]
                own(nc.vector.tensor_reduce(topv[:, k, :], vals, AX, ALU.max))
                own(nc.vector.tensor_tensor(rt[:, 4], vals, spread(topv[:, k, :], P, NT, E), ALU.is_equal))
                own(nc.vector.tensor_tensor(rt[:, 4], rt[:, 4], e_key[:, :, :], ALU.mult))
                own(nc.vector.tensor_reduce(sm[:, 0, :], rt[:, 4], AX, ALU.max))
                own(nc.vector.tensor_tensor(rt[:, 1 + k], rt[:, 4], spread(sm[:, 0, :], P, NT, E), ALU.is_equal))
                if k == 0:
                    own(nc.vector.scalar_tensor_tensor(rt[:, 3], rt[:, 1], -BIG, rt[:, 0], ALU.mult, ALU.add))

        def positions(pe, r):
            pe.wait_ge(r.mask_ready, 1)
            pos = PS[:, 0, 0:NT * E].rearrange("p (i e) -> p i e", i=NT)
            nc.tensor.matmul(PS[:, 0, 0:NT * E], upper_b[:, :], oh_b[:, :, :].rearrange("p i e -> p (i e)"),
                             start=True, stop=False)
            for i in range(NT - 1):
                nc.tensor.matmul(pos[:, i + 1:NT, :], ones_b[:, :],
                                 oh_b[:, i:i + 1, :].broadcast_to([P, NT - 1 - i, E]), start=False, stop=(i == NT - 2))
            for i in range(NT):
                last = nc.tensor.matmul(PS[:, 1, 0:E], ones_b[:, :], oh_b[:, i, :], start=(i == 0), stop=(i == NT - 1))
            last.then_inc(r.pos_ps, 1)

        def slot_tables(own, dve, r, tab, hots):
            dve.wait_ge(r.pos_ps, 1)
            own(nc.vector.tensor_tensor(cmp8[:, :, :], spread(PS[:, 1, 0:E], P, E, 8), k128[:, :, :], ALU.is_gt))
            own(nc.vector.tensor_reduce(nexp[:, 0, :], cmp8[:, :, :], AX, ALU.add))
            own(nc.vector.tensor_scalar(nexp[:, 0, :], nexp[:, 0, :], 1.0, None, ALU.add))
            own(nc.vector.tensor_tensor(cmp8[:, :, :], before[:, :, :], over_tiles(nexp[:, 0, :], P, E, E), ALU.mult))
            own(nc.vector.tensor_reduce(nexp[:, 1, :], cmp8[:, :, :], AX, ALU.add))
            own(nc.vector.tensor_scalar(nexp[:, 2, :], nexp[:, 1, :], float(P), None, ALU.mult))
            own(nc.vector.tensor_tensor(rt[:, 4], PS[:, 0, 0:NT * E].rearrange("p (i e) -> p i e", i=NT),
                                        over_tiles(nexp[:, 2, :], P, NT, E), ALU.add))
            for k, hot in enumerate(hots):
                own(nc.vector.tensor_tensor(rt[:, 3], rt[:, 4], hot, ALU.mult))
                own(nc.vector.tensor_reduce(dest[:, k, :], rt[:, 3], AX, ALU.add))
                nc.vector.tensor_copy(dest_i[:, k, :], dest[:, k, :])
            nc.vector.tensor_copy(tab[0:1, 0:2 * E].rearrange("p (a e) -> p a e", a=2), nexp[0:1, 0:2, :])
            nc.vector.tensor_tensor(tab[0:1, 2 * E:2 * E + 1], nexp[0:1, 0, E - 1:E], nexp[0:1, 1, E - 1:E],
                                    ALU.add).then_inc(r.dest_ready, 1)

        def scatter(pool, r, slots, choices):
            pool.wait_ge(r.dest_ready, 1)
            for k in range(choices):
                for i in range(NT):
                    nc.gpsimd.indirect_dma_start(slots, bass.IndirectOffsetOnAxis(dest_i[:, k, i:i + 1], 0),
                                                 XN[:, i, :], None).then_inc(r.scattered, 16)
            pool.wait_ge(r.scattered, 16 * NT * choices)

        hT = region(0, HK, P)
        gated = region(1024, H)
        v_biased = region(2048, HALF)
        gT = region(2560, HK, P)
        bg_bc = region(4096, 2, H)
        bv_bc = region(6144, H)
        b2_bc = region(7168, D)
        x_slot = region(7680, D)
        xT = region(8192, DK, P)
        y_slot = region(8704, D)

        def row_bc(ap, n):
            return ap.rearrange("(a d) -> a d", a=1).broadcast_to([P, n])

        with nc.Block() as block:
            r0 = route[0]

            @block.sync
            def _(sp):
                sp.dma_start(wv_sb[:, :, :], wv[0].rearrange("(k p) h -> p k h", p=P)).then_inc(wv_in, 16)
                for e in range(2):
                    sp.dma_start(bg_bc[:, e, :], row_bc(bg[e], H)).then_inc(bg_in[e], 16)
                sp.dma_start(bv_bc, row_bc(bv[0], H)).then_inc(bvb2_in[0], 16)
                sp.dma_start(b2_bc, row_bc(b2[0], D)).then_inc(bvb2_in[1], 16)

            @block.vector
            def _(dve):
                def own(ins):
                    after(dve, dve_own, ins)

                norm_tiles(own, r0)
                norm_apply(own, dve, r0)
                dve.wait_ge(r_in, 64)
                dve.wait_ge(r0.logits_ps, 1)
                own(nc.vector.tensor_tensor(rt[:, 0], PS[:, 4, 0:NT * E].rearrange("p (i e) -> p i e", i=NT),
                                            over_tiles(rb_bc[:, :], P, NT, E), ALU.add))
                own(nc.vector.tensor_reduce(sm[:, 0, :], rt[:, 0], AX, ALU.max))
                nc.vector.tensor_tensor(rt[:, 1], rt[:, 0], spread(sm[:, 0, :], P, NT, E), ALU.subtract).then_inc(r0.exp_in, 1)
                dve.wait_ge(r0.exp_out, 1)
                own(nc.vector.tensor_reduce(sm[:, 2, :], rt[:, 2], AX, ALU.add))
                own(nc.vector.reciprocal(sm[:, 3, :], sm[:, 2, :]))
                own(nc.vector.tensor_tensor(rt[:, 0], rt[:, 2], spread(sm[:, 3, :], P, NT, E), ALU.mult))
                top_two(own)
                nc.vector.tensor_copy(gate[:, :, :], topv[:, :, :])
                nc.vector.tensor_tensor(oh_b[:, :, :], rt[:, 1], rt[:, 2], ALU.add).then_inc(r0.mask_ready, 1)
                slot_tables(own, dve, r0, rtab, [rt[:, 1], rt[:, 2]])

            @block.scalar
            def _(act):
                norm_std(act, r0)
                xnt_copies(act, r0, XNT)
                act.wait_ge(r0.exp_in, 1)
                nc.scalar.activation(rt[:, 2], rt[:, 1], ACT.Exp).then_inc(r0.exp_out, 1)

            @block.tensor
            def _(pe):
                pe.wait_ge(r_in, 64)
                transposes_and_logits(pe, r0, XNT, rw_sb)
                positions(pe, r0)

            @block.gpsimd
            def _(pool):
                scatter(pool, r0, slots0_x, 2)

        (h_ps, xtr_ps, xT_ready, hT_ready, g_ps, v_ps, g_biased, silu_done, v_ready, gated_ready, gtr_ps, gT_ready,
         y_ps, y_free, y_sb, y_stored, xg_in) = (
            sem(n) for n in "h_ps xtr_ps xT_ready hT_ready g_ps v_ps g_biased silu_done v_ready gated_ready gtr_ps "
                            "gT_ready y_ps y_free y_sb y_stored xg_in".split())

        all_stored, counts_in = sem("all_stored"), sem("counts_in")
        y_filled = [sem(f"y_filled{i}") for i in range(2)]

        def slots_of(eng, tab, e):
            n = eng.value_load(tab[0:1, ds(e, 1)], min_val=1, max_val=NT)
            base = eng.value_load(tab[0:1, ds(E + e, 1)], min_val=0, max_val=SLOTS0 - 2)
            return n, base

        with nc.Block() as block:

            @block.sync
            def _(sp):
                sp.wait_ge(xg_in, 16)
                sp.dma_start(w2_sb[:, :, :], w2[0].rearrange("(k p) d -> p k d", p=P)).then_inc(w2_in, 16)
                total = sp.value_load(rtab[0:1, 2 * E:2 * E + 1], min_val=E, max_val=SLOTS0 - 1)
                with sp.Fori(0, total) as s:
                    sp.sem_inc(y_filled[0], 16)
                with sp.Fori(total, SLOTS0) as s:
                    sp.dma_start(slots0_y[ds(s * P, P), :], slots0_x[ds(s * P, P), :]).then_inc(y_filled[0], 16)
                sp.wait_ge(y_filled[0], SLOTS0 * 16)
                for e in range(1, E):
                    done = sp.value_load(rtab[0:1, E + e:E + e + 1], min_val=1, max_val=SLOTS0 - 2)
                    sp.wait_ge(v_ps, done * 2)
                    sp.dma_start(wv_sb[:, :, :], wv[e].rearrange("(k p) h -> p k h", p=P)).then_inc(wv_in, 16)
                    sp.wait_ge(v_ready, done * 2)
                    sp.dma_start(bv_bc, row_bc(bv[e], H)).then_inc(bvb2_in[0], 16)
                    sp.wait_ge(y_ps, done)
                    sp.dma_start(w2_sb[:, :, :], w2[e].rearrange("(k p) d -> p k d", p=P)).then_inc(w2_in, 16)
                    sp.wait_ge(y_sb, done)
                    sp.dma_start(b2_bc, row_bc(b2[e], D)).then_inc(bvb2_in[1], 16)
                    if e + 1 < E:
                        q = (e + 1) % 2
                        sp.dma_start(w1_sb[:, q], w1[e + 1].rearrange("(k p) h -> p k h", p=P)).then_inc(w1_in[q], 16)
                        sp.dma_start(wg_sb[:, q], wg[e + 1].rearrange("(k p) h -> p k h", p=P)).then_inc(wg_in[q], 16)
                        sp.dma_start(bg_bc[:, q, :], row_bc(bg[e + 1], H)).then_inc(bg_in[q], 16)
                sp.dma_start(CAB, counts_d.rearrange("m t p s -> p (m t) s")).then_inc(counts_in, 16)

            @block.gpsimd
            def _(pool):
                total = pool.value_load(rtab[0:1, 2 * E:2 * E + 1], min_val=E, max_val=SLOTS0 - 1)
                pool.dma_start(x_slot, slots0_x[0:P, :]).then_inc(xg_in, 16)
                with pool.Fori(1, total + 1) as s:
                    pool.wait_ge(xtr_ps, s)
                    pool.dma_start(x_slot, slots0_x[ds(s * P, P), :]).then_inc(xg_in, 16)

            @block.tensor
            def _(pe):
                def x_transposes():
                    for k in range(DK):
                        last = nc.tensor.transpose(PS[:, 7, k * P:(k + 1) * P], x_slot[:, k * P:(k + 1) * P], ident[:, :])
                    last.then_inc(xtr_ps, 1)

                def gate_or_value(w, half, bank, done):
                    for k in range(HK):
                        last = nc.tensor.matmul(PS[:, bank, :], hT[:, k, :], w[:, k, half * HALF:(half + 1) * HALF],
                                                start=(k == 0), stop=(k == HK - 1))
                    last.then_inc(done, 1)

                def gated_transposes(half):
                    for k in range(4):
                        at = half * HALF + k * P
                        last = nc.tensor.transpose(PS[:, half, k * P:(k + 1) * P], gated[:, at:at + P], ident[:, :])
                    last.then_inc(gtr_ps, 1)

                pe.wait_ge(xg_in, 16)
                x_transposes()
                with pe.Fori(0, E // 2) as pair:
                    for q in range(2):
                        n, base = slots_of(pe, rtab, pair * 2 + q)
                        with pe.Fori(0, n) as j:
                            s = base + j
                            pe.wait_ge(w1_in[q], pair * 16 + 16)
                            pe.wait_ge(xT_ready, s + 1)
                            for m in range(HK):
                                for k in range(DK):
                                    last = nc.tensor.matmul(PS[:, m // 4, (m % 4) * P:(m % 4 + 1) * P],
                                                            w1_sb[:, q, k, m * P:(m + 1) * P], xT[:, k, :],
                                                            start=(k == 0), stop=(k == DK - 1))
                                if m % 4 == 3:
                                    last.then_inc(h_ps, 1)
                            pe.wait_ge(xg_in, s * 16 + 32)
                            x_transposes()
                            pe.wait_ge(hT_ready, s * 2 + 2)
                            pe.wait_ge(wg_in[q], pair * 16 + 16)
                            gate_or_value(wg_sb[:, q], 0, 2, g_ps)
                            pe.wait_ge(wv_in, pair * 32 + 16 * q + 16)
                            gate_or_value(wv_sb, 0, 4, v_ps)
                            gate_or_value(wg_sb[:, q], 1, 3, g_ps)
                            pe.wait_ge(gated_ready, s * 2 + 1)
                            gated_transposes(0)
                            gate_or_value(wv_sb, 1, 5, v_ps)
                            pe.wait_ge(w2_in, pair * 32 + 16 * q + 16)
                            pe.wait_ge(y_free, s + 1)
                            for half in range(2):
                                if half == 1:
                                    pe.wait_ge(gated_ready, s * 2 + 2)
                                    gated_transposes(1)
                                pe.wait_ge(gT_ready, s * 2 + 1 + half)
                                for k in range(4 * half, 4 * half + 4):
                                    last = nc.tensor.matmul(PS[:, 6, :], gT[:, k, :], w2_sb[:, k, :],
                                                            start=(k == 0), stop=(k == HK - 1))
                            last.then_inc(y_ps, 1)

            @block.vector
            def _(dve):
                dve.sem_inc(y_free, 1)
                with dve.Fori(0, E // 2) as pair:
                    for q in range(2):
                        e = pair * 2 + q
                        n, base = slots_of(dve, rtab, e)
                        with dve.Fori(0, n) as j:
                            s = base + j
                            for half in range(2):
                                dve.wait_ge(h_ps, s * 2 + 1 + half)
                                bias = b1T[:, ds(e * HK + half * 4, 4)].rearrange("p (k a) -> p k a", a=1)
                                nc.vector.tensor_tensor(hT[:, 4 * half:4 * half + 4, :],
                                                        PS[:, half, :].rearrange("p (k t) -> p k t", k=4),
                                                        bias.broadcast_to([P, 4, P]), ALU.add).then_inc(hT_ready, 1)
                            dve.wait_ge(bg_in[q], pair * 16 + 16)
                            dve.wait_ge(bvb2_in[0], pair * 32 + 16 * q + 16)
                            for half in range(2):
                                cols = slice(half * HALF, (half + 1) * HALF)
                                dve.wait_ge(g_ps, s * 2 + 1 + half)
                                nc.vector.tensor_tensor(gated[:, cols], PS[:, 2 + half, :], bg_bc[:, q, cols],
                                                        ALU.add).then_inc(g_biased, 1)
                                dve.wait_ge(v_ps, s * 2 + 1 + half)
                                nc.vector.tensor_tensor(v_biased, PS[:, 4 + half, :], bv_bc[:, cols],
                                                        ALU.add).then_inc(v_ready, 1)
                                dve.wait_ge(v_ready, s * 2 + 1 + half)
                                dve.wait_ge(silu_done, s * 2 + 1 + half)
                                nc.vector.tensor_tensor(gated[:, cols], gated[:, cols], v_biased,
                                                        ALU.mult).then_inc(gated_ready, 1)
                            dve.wait_ge(bvb2_in[1], pair * 32 + 16 * q + 16)
                            dve.wait_ge(y_ps, s + 1)
                            dve.wait_ge(y_stored, s * 16 + 16)
                            nc.vector.tensor_tensor(y_slot, PS[:, 6, :], b2_bc, ALU.add).then_inc(y_sb, 1)
                            dve.wait_ge(y_sb, s + 1)
                            dve.sem_inc(y_free, 1)

            @block.scalar
            def _(act):
                def xT_copy():
                    nc.scalar.activation(xT, PS[:, 7, :].rearrange("p (k t) -> p k t", k=DK),
                                         ACT.Copy).then_inc(xT_ready, 1)

                act.sem_inc(y_stored, 16)
                act.wait_ge(xtr_ps, 1)
                xT_copy()
                total = act.value_load(rtab[0:1, 2 * E:2 * E + 1], min_val=E, max_val=SLOTS0 - 1)
                with act.Fori(0, total) as s:
                    act.wait_ge(xtr_ps, s + 2)
                    act.wait_ge(h_ps, s * 2 + 2)
                    xT_copy()
                    for half in range(2):
                        cols = slice(half * HALF, (half + 1) * HALF)
                        act.wait_ge(g_biased, s * 2 + 1 + half)
                        nc.scalar.activation(gated[:, cols], gated[:, cols], ACT.Silu).then_inc(silu_done, 1)
                    for half in range(2):
                        act.wait_ge(gtr_ps, s * 2 + 1 + half)
                        nc.scalar.activation(gT[:, 4 * half:4 * half + 4, :],
                                             PS[:, half, :].rearrange("p (k t) -> p k t", k=4),
                                             ACT.Copy).then_inc(gT_ready, 1)
                    act.wait_ge(y_sb, s + 1)
                    act.dma_start(slots0_y[ds(s * P, P), :], y_slot).then_inc(y_stored, 16)
                act.wait_ge(y_stored, total * 16 + 16)
                act.sem_inc(all_stored, 1)

        w1_flat = w1_sb[:, :, :, :].rearrange("p q k h -> p (q k h)")
        picked = w1_flat.rearrange("p (i k d) -> p i k d", i=NT, k=2)
        XNT1 = w1_flat[:, 0:NT * D].rearrange("p (i k t) -> p i k t", i=NT, k=DK)
        XA1 = half_flat[:, 2 * NT * T:2 * NT * T + NT * D].rearrange("p (i d) -> p i d", i=NT)
        XB1 = half_flat[:, 2 * NT * T + NT * D:2 * NT * T + 2 * NT * D].rearrange("p (i d) -> p i d", i=NT)
        W12 = wg_sb[:, :, :, :].rearrange("p q k h -> p (q k h)").rearrange("p (e k h) -> p e k h", e=E, k=DK)
        W3 = wv_sb[:, :, :].rearrange("p k h -> p (k h)").rearrange("p (e k d) -> p e k d", e=E, k=HK1)
        wc_sb = region(4096, DK, D)
        wn_sb = region(6144, DK, D)
        bias1_bc = region(8192, D)
        picked_in = [sem(f"picked_in{i}") for i in range(NT)]
        gnn1_in, w12_in, w3_in = (sem(n) for n in "gnn1_in w12_in w3_in".split())
        indeg_ps, ut_ps, ut_sb, out1_ps, out1_done = (
            sem(n) for n in "indeg_ps ut_ps ut_sb out1_ps out1_done".split())
        mid = Norm("mid")
        zeros_ready = sem("zeros_ready")
        cb_ready, cb_ps, parts_ready, ut_part = (sem(n) for n in "cb_ready cb_ps parts_ready ut_part".split())
        parts_f = region(8704, P)
        zeros_f = region(8960, HALF // 2)
        zeros_h = region(8960, HALF, dt=bf16)

        with nc.Block() as block:

            @block.sync
            def _(sp):
                sp.dma_start(wc_sb, wc.rearrange("(k p) d -> p k d", p=P)).then_inc(gnn1_in, 16)
                sp.dma_start(wn_sb, wn.rearrange("(k p) d -> p k d", p=P)).then_inc(gnn1_in, 16)
                sp.dma_start(bias1_bc, row_bc(gnn1_b, D)).then_inc(gnn1_in, 16)

            @block.gpsimd
            def _(pool):
                nc.gpsimd.memset(zeros_f, 0.0).then_inc(zeros_ready, 1)
                for i in range(NT):
                    for k in range(2):
                        nc.gpsimd.indirect_dma_start(picked[:, i, k, :], None, slots0_y,
                                                     bass.IndirectOffsetOnAxis(dest_i[:, k, i:i + 1], 0)
                                                     ).then_inc(picked_in[i], 16)

            @block.vector
            def _(dve):
                def own(ins):
                    after(dve, dve_own, ins)

                dve.wait_ge(counts_in, 16)
                nc.vector.tensor_reduce(sm[:, 0, 0:1], CAB[:, NT:2 * NT, :].rearrange("p t s -> p (t s)"), AX, ALU.max,
                                        apply_absolute_value=True).then_inc(cb_ready, 1)
                dve.wait_ge(cb_ps, 1)
                own(nc.vector.tensor_reduce(parts_f[0:1, 0:1], PS[0:1, 4, 0:P], AX, ALU.max))
                nc.vector.tensor_scalar(parts[0:1, :], parts_f[0:1, 0:1], 0.0, 1.0, ALU.is_gt, ALU.add).then_inc(parts_ready, 1)
                for i in range(NT):
                    dve.wait_ge(picked_in[i], 32)
                    own(nc.vector.scalar_tensor_tensor(X[:, i, :], picked[:, i, 0, :], gate[:, 0, i:i + 1], X[:, i, :],
                                                       ALU.mult, ALU.add))
                    own(nc.vector.scalar_tensor_tensor(X[:, i, :], picked[:, i, 1, :], gate[:, 1, i:i + 1], X[:, i, :],
                                                       ALU.mult, ALU.add))
                norm_tiles(own, mid)
                norm_apply(own, dve, mid)
                for i in range(NT):
                    dve.wait_ge(xa_ready, NT + i + 1)
                    nc.vector.scalar_tensor_tensor(XB1[:, i, :], XN[:, i, :], SPLIT, XA1[:, i, :], ALU.mult,
                                                   ALU.subtract).then_inc(xs_ready, 1)
                dve.wait_ge(indeg_ps, 1)
                own(nc.vector.tensor_reduce(wdeg[:, :], PS[:, 5, 0:2 * NT].rearrange("p (i m) -> p i m", m=2), AX, ALU.add))
                own(nc.vector.reciprocal(wdeg[:, :], wdeg[:, :]))
                dve.wait_ge(gnn1_in, 48)
                for i in range(NT):
                    alpha, gamma = PS[:, 6 + i % 2, :], PS[:, 2 + i % 2, :]
                    own(nc.vector.tensor_tensor(X[:, i, :], X[:, i, :], bias1_bc, ALU.add))
                    dve.wait_ge(out1_ps, i + 1)
                    own(nc.vector.scalar_tensor_tensor(X[:, i, :], gamma, wdeg[:, i:i + 1], X[:, i, :], ALU.mult, ALU.add))
                    nc.vector.tensor_tensor(X[:, i, :], alpha, X[:, i, :], ALU.add).then_inc(out1_done, 1)

            @block.tensor
            def _(pe):
                pe.wait_ge(cb_ready, 1)
                nc.tensor.transpose(PS[0:1, 4, 0:P], sm[:, 0, 0:1], ident[:, :]).then_inc(cb_ps, 1)
                for i in range(NT):
                    for m in range(2):
                        for c in range(NT):
                            last = nc.tensor.matmul(PS[:, 5, 2 * i + m:2 * i + m + 1], CAB[:, m * NT + c, i * P:(i + 1) * P],
                                                    ones_b[:, 0:1], start=(c == 0), stop=(c == NT - 1))
                last.then_inc(indeg_ps, 1)
                transposes_and_logits(pe, mid, XNT1, None)
                pe.wait_ge(zeros_ready, 1)
                pe.wait_ge(parts_ready, 1)
                n_parts = pe.value_load(parts[0:1, 0:1], min_val=1, max_val=2)
                pe.wait_ge(xs_ready, 2 * NT)
                for g in range(2 * DK):
                    dk, rh = g // 2, g % 2
                    if g >= 2:
                        pe.wait_ge(ut_sb, g - 1)
                    nc.tensor.matmul(PS[:, 2 + g % 2, :], zeros_h[:, 0:P], zeros_h[:, :], start=True, stop=False,
                                     skip_group_check=True)
                    with pe.Fori(0, n_parts) as m:
                        for x_part in (XA1, XB1):
                            for c in range(NT):
                                last = nc.tensor.matmul(PS[:, 2 + g % 2, :], x_part[:, c, dk * P:(dk + 1) * P],
                                                        CAB[:, ds(m * NT + c, 1), rh * HALF:(rh + 1) * HALF], start=False,
                                                        stop=True, skip_group_check=True)
                        last.then_inc(ut_part, 1)
                    pe.wait_ge(ut_part, n_parts * (g + 1))
                    pe.sem_inc(ut_ps, 1)
                pe.wait_ge(ut_sb, 2 * DK)
                pe.wait_ge(mid.xnt_sb, NT)
                pe.wait_ge(gnn1_in, 48)
                for i in range(NT):
                    if i >= 2:
                        pe.wait_ge(out1_done, i - 1)
                    for k in range(DK):
                        nc.tensor.matmul(PS[:, 2 + i % 2, :], MT[:, k, i * P:(i + 1) * P], wn_sb[:, k, :],
                                         start=(k == 0), stop=(k == DK - 1))
                    for k in range(DK):
                        last = nc.tensor.matmul(PS[:, 6 + i % 2, :], XNT1[:, i, k, :], wc_sb[:, k, :],
                                                start=(k == 0), stop=(k == DK - 1))
                    last.then_inc(out1_ps, 1)

            @block.scalar
            def _(act):
                norm_std(act, mid)
                for i in range(NT):
                    act.wait_ge(mid.normed, i + 1)
                    nc.scalar.activation(XA1[:, i, :], XN[:, i, :], ACT.Copy, scale=SPLIT).then_inc(xa_ready, 1)
                xnt_copies(act, mid, XNT1)
                for g in range(2 * DK):
                    dk, rh = g // 2, g % 2
                    act.wait_ge(ut_ps, g + 1)
                    nc.scalar.activation(MT[:, dk, rh * HALF:(rh + 1) * HALF], PS[:, 2 + g % 2, :], ACT.Copy,
                                         scale=1.0 / SPLIT).then_inc(ut_sb, 1)
        s_gate = sm[:, 4:6, :]
        kept = sm[:, 2:4, :]
        coef = gate
        with nc.Block() as block:
            r1 = route[1]

            @block.sync
            def _(sp):
                for e in range(E):
                    sp.dma_start(W12[:, e, :, 0:H1], e1_w1[e].rearrange("(k p) h -> p k h", p=P)).then_inc(w12_in, 16)
                    sp.dma_start(W12[:, e, :, H1:2 * H1], e1_w2[e].rearrange("(k p) h -> p k h", p=P)).then_inc(w12_in, 16)
                    sp.dma_start(W3[:, e, :, :], e1_w3[e].rearrange("(k p) d -> p k d", p=P)).then_inc(w3_in, 16)

            @block.vector
            def _(dve):
                def own(ins):
                    after(dve, dve_own, ins)

                norm_tiles(own, r1)
                norm_apply(own, dve, r1)
                dve.wait_ge(r1.logits_ps, 1)
                own(nc.vector.tensor_tensor(rt[:, 0], PS[:, 4, 0:NT * E].rearrange("p (i e) -> p i e", i=NT),
                                            over_tiles(rb1_bc[:, :], P, NT, E), ALU.add))
                top_two(own)
                nc.vector.tensor_tensor(sm[:, 6, :], topv[:, 1, :], topv[:, 0, :], ALU.subtract).then_inc(r1.exp_in, 1)
                nc.vector.tensor_copy(oh_b[:, :, :], rt[:, 1])
                nc.vector.tensor_copy(oh2_b[:, :, :], rt[:, 2]).then_inc(r1.pairs_ready, 1)
                dve.wait_ge(r1.exp_out, 1)
                own(nc.vector.tensor_scalar(sm[:, 0, :], sm[:, 7, :], 1.0, None, ALU.add))
                own(nc.vector.reciprocal(s_gate[:, 0, :], sm[:, 0, :]))
                own(nc.vector.tensor_tensor(s_gate[:, 1, :], sm[:, 7, :], s_gate[:, 0, :], ALU.mult))
                dve.wait_ge(r1.pairs_ps, 1)
                own(nc.vector.tensor_copy(nexp[:, 0:2, :], PS[:, 5, 0:2 * E].rearrange("p (a e) -> p a e", a=2)))
                own(nc.vector.tensor_scalar(nexp[:, 0:2, :], nexp[:, 0:2, :], float(T), None, ALU.is_ge))
                for k in range(2):
                    own(nc.vector.tensor_tensor(rt[:, 4], rt[:, 1 + k], over_tiles(nexp[:, k, :], P, NT, E), ALU.mult))
                    own(nc.vector.tensor_reduce(kept[:, k, :], rt[:, 4], AX, ALU.add))
                    own(nc.vector.tensor_tensor(kept[:, k, :], kept[:, k, :], last_tok[:, :], ALU.mult))
                    own(nc.vector.tensor_scalar(kept[:, k, :], kept[:, k, :], -1.0, 1.0, ALU.mult, ALU.add))
                    own(nc.vector.tensor_tensor(rt[:, 4], rt[:, 1 + k], e_idx[:, :, :], ALU.mult))
                    own(nc.vector.tensor_reduce(dest[:, k, :], rt[:, 4], AX, ALU.add))
                    own(nc.vector.tensor_tensor(dest[:, k, :], dest[:, k, :], kept[:, k, :], ALU.mult))
                own(nc.vector.tensor_tensor(sm[:, 0, :], dest[:, 0, :], dest[:, 1, :], ALU.max))
                own(nc.vector.tensor_tensor(rt[:, 5], e_idx[:, :, :], spread(sm[:, 0, :], P, NT, E), ALU.is_equal))
                nc.vector.tensor_copy(oh_b[:, :, :], rt[:, 5]).then_inc(r1.mask_ready, 1)
                own(nc.vector.tensor_tensor(topv[:, :, :], s_gate, kept, ALU.mult))
                own(nc.vector.tensor_tensor(coef[:, 0, :], topv[:, 0, :], topv[:, 1, :], ALU.add))
                own(nc.vector.tensor_scalar(kept, kept, -1.0, 1.0, ALU.mult, ALU.add))
                own(nc.vector.tensor_tensor(topv[:, :, :], s_gate, kept, ALU.mult))
                own(nc.vector.tensor_tensor(coef[:, 1, :], topv[:, 0, :], topv[:, 1, :], ALU.add))
                slot_tables(own, dve, r1, rtab1, [rt[:, 5]])
                own(nc.vector.tensor_tensor(slot_cmp[:, :, :], over_tiles(nexp[:, 1, :], P, SLOTS1 + 1, E),
                                            slot_idx[:, :, :], ALU.is_le))
                own(nc.vector.tensor_reduce(slot_row[:, :], slot_cmp[:, :, :], AX, ALU.add))
                own(nc.vector.tensor_scalar(expert_of[0:1, :], slot_row[0:1, :], -1.0, None, ALU.add))

            @block.scalar
            def _(act):
                norm_std(act, r1)
                xnt_copies(act, r1, XNT)
                act.wait_ge(r1.exp_in, 1)
                nc.scalar.activation(sm[:, 7, :], sm[:, 6, :], ACT.Exp).then_inc(r1.exp_out, 1)

            @block.tensor
            def _(pe):
                transposes_and_logits(pe, r1, XNT, rw1_sb)
                pe.wait_ge(r1.pairs_ready, 1)
                for i in range(NT):
                    nc.tensor.matmul(PS[:, 5, 0:E], ones_b[:, :], oh_b[:, i, :], start=(i == 0), stop=(i == NT - 1))
                for m, hot in enumerate((oh_b, oh2_b)):
                    for i in range(NT):
                        last = nc.tensor.matmul(PS[:, 5, E:2 * E], ones_b[:, :], hot[:, i, :], start=(m == 0 and i == 0),
                                                stop=(m == 1 and i == NT - 1))
                last.then_inc(r1.pairs_ps, 1)
                positions(pe, r1)

            @block.gpsimd
            def _(pool):
                scatter(pool, r1, slots1_x, 1)

        x1_slot = region(4096, D)
        x1T = region(4608, DK, P)
        y1_slot = region(5120, D)
        left = region(5632, H1)
        act_in = region(5888, H1)
        act_out = region(6144, H1)
        aT = region(6400, HK1, P)
        (ab_ps, x1tr_ps, x1T_ready, left_ready, prod_ready, gelu_done, atr_ps, aT_ready, y1_ps, y1_free, y1_sb,
         y1_stored, x1_in) = (
            sem(n) for n in "ab_ps x1tr_ps x1T_ready left_ready prod_ready gelu_done atr_ps aT_ready y1_ps y1_free y1_sb "
                            "y1_stored x1_in".split())
        with nc.Block() as block:

            @block.sync
            def _(sp):
                total = sp.value_load(rtab1[0:1, 2 * E:2 * E + 1], min_val=E, max_val=SLOTS1 - 1)
                with sp.Fori(0, total) as s:
                    sp.sem_inc(y_filled[1], 16)
                with sp.Fori(total, SLOTS1) as s:
                    sp.dma_start(slots1_y[ds(s * P, P), :], slots1_x[ds(s * P, P), :]).then_inc(y_filled[1], 16)
                sp.wait_ge(y_filled[1], SLOTS1 * 16)

            @block.gpsimd
            def _(pool):
                total = pool.value_load(rtab1[0:1, 2 * E:2 * E + 1], min_val=E, max_val=SLOTS1 - 1)
                pool.dma_start(x1_slot, slots1_x[0:P, :]).then_inc(x1_in, 16)
                with pool.Fori(1, total + 1) as s:
                    pool.wait_ge(x1tr_ps, s)
                    pool.dma_start(x1_slot, slots1_x[ds(s * P, P), :]).then_inc(x1_in, 16)

            @block.tensor
            def _(pe):
                def x_transposes():
                    for k in range(DK):
                        last = nc.tensor.transpose(PS[:, 7, k * P:(k + 1) * P], x1_slot[:, k * P:(k + 1) * P], ident[:, :])
                    last.then_inc(x1tr_ps, 1)

                def up(e, s):
                    for k in range(DK):
                        last = nc.tensor.matmul(PS[:, ds(s % 2 + 4, 1), :], x1T[:, k, :], W12[:, ds(e, 1), k, :],
                                                start=(k == 0), stop=(k == DK - 1))
                    last.then_inc(ab_ps, 1)

                pe.wait_ge(w12_in, 32 * E)
                pe.wait_ge(w3_in, 16 * E)
                pe.wait_ge(x1_in, 16)
                x_transposes()
                pe.wait_ge(x1T_ready, 1)
                up(0, 0)
                total = pe.value_load(rtab1[0:1, 2 * E:2 * E + 1], min_val=E, max_val=SLOTS1 - 1)
                with pe.Fori(0, total) as s:
                    here = pe.value_load(expert_of[0:1, ds(s, 1)], min_val=0, max_val=E - 1)
                    ahead = pe.value_load(expert_of[0:1, ds(s + 1, 1)], min_val=0, max_val=E - 1)
                    pe.wait_ge(x1_in, s * 16 + 32)
                    x_transposes()
                    pe.wait_ge(x1T_ready, s + 2)
                    up(ahead, s + 1)
                    pe.wait_ge(gelu_done, s + 1)
                    for k in range(HK1):
                        last = nc.tensor.transpose(PS[:, 1, k * P:(k + 1) * P], act_out[:, k * P:(k + 1) * P], ident[:, :])
                    last.then_inc(atr_ps, 1)
                    pe.wait_ge(aT_ready, s + 1)
                    pe.wait_ge(y1_free, s + 1)
                    for k in range(HK1):
                        last = nc.tensor.matmul(PS[:, 2, :], aT[:, k, :], W3[:, ds(here, 1), k, :],
                                                start=(k == 0), stop=(k == HK1 - 1))
                    last.then_inc(y1_ps, 1)

            @block.vector
            def _(dve):
                dve.sem_inc(y1_free, 1)
                total = dve.value_load(rtab1[0:1, 2 * E:2 * E + 1], min_val=E, max_val=SLOTS1 - 1)
                def xT_copy():
                    nc.vector.tensor_copy(x1T, PS[:, 7, :].rearrange("p (k t) -> p k t", k=DK)).then_inc(x1T_ready, 1)

                dve.wait_ge(x1tr_ps, 1)
                xT_copy()
                with dve.Fori(0, total) as s:
                    dve.wait_ge(ab_ps, s + 1)
                    nc.vector.tensor_copy(left, PS[:, ds(s % 2 + 4, 1), 0:H1]).then_inc(left_ready, 1)
                    dve.wait_ge(x1tr_ps, s + 2)
                    xT_copy()
                    dve.wait_ge(left_ready, s + 1)
                    nc.vector.tensor_tensor(act_in, PS[:, ds(s % 2 + 4, 1), H1:2 * H1], left, ALU.mult).then_inc(prod_ready, 1)
                    dve.wait_ge(atr_ps, s + 1)
                    nc.vector.tensor_copy(aT, PS[:, 1, 0:H1].rearrange("p (k t) -> p k t", k=HK1)).then_inc(aT_ready, 1)
                    dve.wait_ge(y1_ps, s + 1)
                    dve.wait_ge(y1_stored, s * 16 + 16)
                    nc.vector.tensor_copy(y1_slot, PS[:, 2, :]).then_inc(y1_sb, 1)
                    dve.wait_ge(y1_sb, s + 1)
                    dve.sem_inc(y1_free, 1)

            @block.scalar
            def _(act):
                act.sem_inc(y1_stored, 16)
                total = act.value_load(rtab1[0:1, 2 * E:2 * E + 1], min_val=E, max_val=SLOTS1 - 1)
                with act.Fori(0, total) as s:
                    act.wait_ge(prod_ready, s + 1)
                    nc.scalar.activation(act_out, act_in, ACT.Gelu).then_inc(gelu_done, 1)
                    act.wait_ge(y1_sb, s + 1)
                    act.dma_start(slots1_y[ds(s * P, P), :], y1_slot).then_inc(y1_stored, 16)
                act.wait_ge(y1_stored, total * 16 + 16)
                act.sem_inc(all_stored, 1)

        final_x, stored = sem("final_x"), sem("stored")
        with nc.Block() as block:

            @block.gpsimd
            def _(pool):
                for i in range(NT):
                    nc.gpsimd.indirect_dma_start(picked[:, i, 0, :], None, slots1_y,
                                                 bass.IndirectOffsetOnAxis(dest_i[:, 0, i:i + 1], 0)
                                                 ).then_inc(picked_in[i], 16)

            @block.vector
            def _(dve):
                def own(ins):
                    after(dve, dve_own, ins)

                for i in range(NT):
                    own(nc.vector.scalar_tensor_tensor(X[:, i, :], XN[:, i, :], coef[:, 1, i:i + 1], X[:, i, :],
                                                       ALU.mult, ALU.add))
                    dve.wait_ge(picked_in[i], 32 + 16)
                    nc.vector.scalar_tensor_tensor(X[:, i, :], picked[:, i, 0, :], coef[:, 0, i:i + 1], X[:, i, :],
                                                   ALU.mult, ALU.add).then_inc(final_x, 1)

            @block.sync
            def _(sp):
                for i in range(NT):
                    sp.wait_ge(final_x, i + 1)
                    sp.dma_start(out[i * P:(i + 1) * P, :], X[:, i, :]).then_inc(stored, 16)
                sp.wait_ge(stored, 16 * NT)


_INS = ['x', 'src', 'dst', 'L0_gnn_W', 'L0_gnn_b', 'L0_ffn_router_w', 'L0_ffn_router_b', 'L0_ffn_w1', 'L0_ffn_b1',
        'L0_ffn_wg', 'L0_ffn_bg', 'L0_ffn_wv', 'L0_ffn_bv', 'L0_ffn_w2', 'L0_ffn_b2', 'L1_gnn_wc', 'L1_gnn_wn',
        'L1_gnn_bias', 'L1_ffn_Wr', 'L1_ffn_br', 'L1_ffn_W1', 'L1_ffn_W2', 'L1_ffn_W3']
_OUTS = [((1024, 512), 'float32')]


def kernel(**inputs):
    import numpy as _np
    import concourse.bacc as _bacc
    from concourse import mybir as _mybir
    from concourse.bass_utils import run_bass_kernel_spmd as _run

    nc = _bacc.Bacc("TRN2", target_bir_lowering=False, num_devices=1)
    arrays, args = {}, []
    for name in _INS:
        a = _np.ascontiguousarray(inputs[name])
        arrays[f"in_{name}_dram"] = a
        args.append(nc.dram_tensor(f"in_{name}_dram", a.shape, _mybir.dt.from_np(a.dtype), kind="ExternalInput").ap())
    for i, (shape, dtype) in enumerate(_OUTS):
        dt = _mybir.dt.from_np(_np.dtype(dtype))
        args.append(nc.dram_tensor(f"out_{i}_dram", shape, dt, kind="ExternalOutput").ap())
    gnn_moe_two_layer_kernel(nc, *args)
    r = _run(nc, [arrays], core_ids=[0])
    got = tuple(r.results[0][f"out_{i}_dram"] for i in range(len(_OUTS)))
    return got[0]
```

```python
import concourse.bass as bass
from concourse import mybir
from contextlib import ExitStack


def gnn_moe_two_layer_kernel(
    nc, x, src, dst, gnn0_w, gnn0_b, router0_w, router0_b, w1, b1, wg, bg, wv, bv, w2, b2,
    wc, wn, gnn1_b, router1_w, router1_b, e1_w1, e1_w2, e1_w3, out,
):
    f32, bf16, f16, i32 = mybir.dt.float32, mybir.dt.bfloat16, mybir.dt.float16, mybir.dt.int32
    ALU = mybir.AluOpType
    ACT = mybir.ActivationFunctionType
    AX = mybir.AxisListType.X
    ds = bass.ds

    P = 128
    T, D = x.shape
    NT = T // P
    DK = D // P
    EDGES = src.shape[0]
    CG = 4
    NG = EDGES // (CG * P)
    E, _, H = w1.shape
    HK = H // P
    HALF = 512
    H1 = e1_w1.shape[2]
    HK1 = H1 // P
    SLOTS0 = 2 * T // P + E + 1
    SLOTS1 = T // P + E + 1
    NOH = 2
    EPS = 1e-5
    BIG = 1e30
    SPLIT = 2048.0
    W_UP, H_UP, G_UP = 512.0, 4.0, 1.0 / 16
    M_UP = 0.125
    PIECE = 1024
    W1P, WGP, WVP, W2P = DK * H // PIECE, HK * H // PIECE, HK * H // PIECE, HK * D // PIECE
    UPP, DOWNP = W1P + WGP, WVP + W2P
    EP = UPP + DOWNP
    RING = 6

    ctx = ExitStack()
    with ctx:
        def sb(name, shape, dt=f32):
            return ctx.enter_context(nc.sbuf_tensor(name, shape, dt))

        def sem(name):
            return ctx.enter_context(nc.semaphore(name))

        def dram(name, shape, dt=f32):
            return nc.dram_tensor(name, shape, dt, kind="Internal").ap()

        counts_d = dram("edge_counts", [2, NT, P, T], f16)
        x_saved = dram("x_saved", [T, D])
        slots0_x = dram("slots0_x", [SLOTS0 * P, D])
        slots0_y = dram("slots0_y", [SLOTS0 * P, D])
        slots1_x = dram("slots1_x", [SLOTS1 * P, D])
        slots1_y = dram("slots1_y", [SLOTS1 * P, D])

        X = sb("X", [P, NT, D])
        SPARE = 3 * PIECE // 2
        U = sb("U", [P, (2 * UPP + DOWNP) * PIECE + SPARE])
        R = sb("R", [P, 9216])

        def region(at, *shape, dt=f32):
            n = 1
            for m in shape:
                n *= m
            words = n if dt in (f32, i32) else n // 2
            v = R[:, at:at + words]
            if dt != f32:
                v = v.bitcast(dt)
            if len(shape) == 2:
                v = v.rearrange("p (a b) -> p a b", a=shape[0])
            if len(shape) == 3:
                v = v.rearrange("p (a b c) -> p a b c", a=shape[0], b=shape[1])
            return v

        UH = U[:, :].bitcast(f16)
        UP0, UP1, DOWN = 0, UPP, 2 * UPP

        def place(block):
            return block * PIECE + (SPARE if block >= UP1 else 0)

        def half(block, low, cols):
            second = (1 - low) if UP1 <= block < DOWN else low
            at = 2 * place(block) + second * PIECE
            return UH[:, at + cols.start:at + cols.stop]

        X_flat = X[:, :, :].rearrange("p i d -> p (i d)")
        ring = [X_flat[:, r * PIECE:(r + 1) * PIECE] for r in range(4)] + [region(4096, PIECE), region(4096 + PIECE, PIECE)]
        W1_AT, WG_AT = (UP0, UP1 + WGP), (UP0 + W1P, UP1)

        def up_group(q, g):
            n = UPP // 3
            return (list(range(UP0 + g * n, UP0 + (g + 1) * n)), list(range(UP1 + UPP - 1 - g * n, UP1 + UPP - 1 - (g + 1) * n, -1)))[q]

        def raw_piece(q, block):
            at = place(block) + (1 - 2 * q) * SPARE
            return U[:, at:at + PIECE]

        def load_up(eng, q, g, e):
            blocks = sorted(up_group(q, g))
            w, first = (w1, blocks[0] - W1_AT[q]) if g == 0 else (wg, blocks[0] - WG_AT[q])
            part = w[ds(e, 1), first * P:(first + len(blocks)) * P, :].rearrange("a (k p) c -> p (a k) c", p=P)
            at = place(blocks[0]) + (1 - 2 * q) * SPARE
            to = U[:, at:at + len(blocks) * PIECE].rearrange("p (k c) -> p k c", c=PIECE)
            eng.dma_start(to, part).then_inc(up_in[g], 16)
        half_flat = U[:, 0:UPP * PIECE].bitcast(f16)
        CAB = half_flat[:, 0:2 * NT * T].rearrange("p (m s) -> p m s", s=T)
        wv_flat = U[:, place(DOWN):place(DOWN + WVP)]
        AT = wv_flat[:, 0:NT * T // 2].bitcast(f16).rearrange("p (t s) -> p t s", t=NT)
        split_flat = wv_flat[:, NT * T // 2:NT * T // 2 + NT * D].bitcast(f16)
        XA = split_flat[:, 0:NT * D].rearrange("p (i d) -> p i d", i=NT)
        XB = split_flat[:, NT * D:2 * NT * D].rearrange("p (i d) -> p i d", i=NT)
        w2_flat = U[:, place(DOWN + WVP):place(DOWN + DOWNP)]
        MT = w2_flat.rearrange("p (k t) -> p k t", k=DK)
        MT1 = MT.rearrange("p k t -> p (k t)").bitcast(f16).rearrange("p (k a t) -> p k a t", k=DK, a=2)
        XNT = w2_flat.rearrange("p (i k t) -> p i k t", i=NT, k=DK)
        ct_stage = region(0, 2, T)
        ca_stage = region(2048, 2, T, dt=f16)
        cb_stage = split_flat[:, 0:2 * T].rearrange("p (a s) -> p a s", a=2)
        oh_src = w2_flat[:, 0:NOH * CG * T // 2].bitcast(bf16).rearrange("p (a b n) -> p a b n", a=NOH, b=CG)
        oh_dst = region(3072, NOH, CG, P, dt=bf16)
        edges_T = region(3584, 2, CG, NG)
        b1_rows = region(3840, P)[0:E * HK]
        zero_b = region(3968, HALF, dt=bf16)
        edges_i = region(0, 2, CG * P, dt=i32)[0:NG]
        edges_f = region(1024, 2, CG * P)[0:NG]
        W_raw = region(4352, DK, D)
        WTH = region(6400, DK * 2, D, dt=f16).rearrange("p (k a) d -> p k a d", a=2)
        bias_bc = region(8448, D)
        iota_h = region(6400, T, dt=f16)
        XN = region(0, NT, D)

        ident = sb("ident", [P, P])
        ones_b = sb("ones_b", [P, P], bf16)
        upper_b = sb("upper_b", [P, P], bf16)
        ones_f = sb("ones_f", [P, 1])
        eps_t = sb("eps_t", [P, 1])
        tile_lo = sb("tile_lo", [P, NT])
        chunk_up = sb("chunk_up", [P, 1])
        chunk_down = sb("chunk_down", [P, 1])
        e_key = sb("e_key", [P, NT, E])
        e_idx = sb("e_idx", [P, NT, E])
        k128 = sb("k128", [P, E, 8])
        before = sb("before", [P, E, E])
        last_tok = sb("last_tok", [P, NT])
        b1T = sb("b1T", [P, E * HK])
        etab = sb("etab", [1, 2 * NT], i32)
        parts = sb("parts", [1, 1], i32)
        rtab = sb("rtab", [1, 2 * E + 1], i32)
        plan = sb("plan", [1, E], i32)
        rtab1 = sb("rtab1", [1, 2 * E + 1], i32)
        expert_of = sb("expert_of", [1, SLOTS1 + 1], i32)
        slot_idx = sb("slot_idx", [P, SLOTS1 + 1, E])
        slot_row = sb("slot_row", [P, SLOTS1 + 1])
        slot_cmp = region(8192, SLOTS1 + 1, E)
        sm = sb("sm", [P, 8, NT])
        mv = sb("mv", [P, NT, 2])
        bst = sb("bst", [P, NT, 6])
        rstd = sb("rstd", [P, NT])
        dinv = sb("dinv", [P, NT])
        wdeg = sb("wdeg", [P, NT])
        dinv_ab = sb("dinv_ab", [P, NT, 2], f16)
        rw_sb = sb("rw_sb", [P, DK, E])
        rb_bc = sb("rb_bc", [P, E])
        rw1_sb = sb("rw1_sb", [P, DK, E])
        rb1_bc = sb("rb1_bc", [P, E])
        rt = region(8704, 6 * NT, E).rearrange("p (a i) e -> p a i e", a=6)
        cmp8 = sb("cmp8", [P, E, 8])
        oh_b = sb("oh_b", [P, NT, E], bf16)
        oh2_b = sb("oh2_b", [P, NT, E], bf16)
        topv = sb("topv", [P, 2, NT])
        gate = sb("gate", [P, 2, NT])
        nexp = sb("nexp", [P, 3, E])
        dest = sb("dest", [P, 2, NT])
        dest_i = sb("dest_i", [P, 2, NT], i32)
        PS = ctx.enter_context(nc.psum_tensor("PS", [P, 8, HALF], f32))

        dve_own, act_own, pool_own, pe_own = sem("dve_own"), sem("act_own"), sem("pool_own"), sem("pe_own")
        own_count = {}

        def after(eng, own, ins):
            own_count[id(own)] = own_count.get(id(own), 0) + 1
            ins.then_inc(own, 1)
            eng.wait_ge(own, own_count[id(own)])

        edges_in, x_in, gnn0_in, r_in, zeros_out = (
            sem(n) for n in "edges_in x_in gnn0_in r_in zeros_out".split())
        up_in = [sem(f"up_in{g}") for g in range(3)]
        ring_in = [sem(f"ring_in{i}") for i in range(RING)]
        hi_done, lo_done = sem("hi_done"), sem("lo_done")
        bias_in, b2_in = sem("bias_in"), sem("b2_in")
        x_moved = sem("x_moved")
        consts_ready = sem("consts_ready")
        oh_free = [sem(f"oh_free{t}") for t in range(NT)]
        oh_ready = [sem(f"oh_ready{t}") for t in range(NT)]
        counts_copied, at_ready = sem("counts_copied"), sem("at_ready")
        cb_made = sem("cb_made")
        counts_out = [sem(f"counts_out{i}") for i in range(2)]
        edge_rows, edge_T_ps, span, span_ps, etab_ready = (
            sem(n) for n in "edge_rows edge_T_ps span span_ps etab_ready".split())
        wt_ps, wt_sb = sem("wt_ps"), sem("wt_sb")

        with nc.Block() as block:

            @block.sync
            def _(sp):
                sp.dma_start(edges_i[:, 0, :], src.rearrange("(k e) -> k e", e=CG * P)).then_inc(edges_in, 16)
                sp.dma_start(edges_i[:, 1, :], dst.rearrange("(k e) -> k e", e=CG * P)).then_inc(edges_in, 16)
                sp.dma_start(W_raw, gnn0_w.rearrange("(o p) d -> p o d", p=P)).then_inc(gnn0_in, 16)
                sp.dma_start(b1_rows[:, :], b1.rearrange("e (j p) -> (e j) p", p=P)).then_inc(gnn0_in, 16)
                sp.dma_start(X[:, :, :], x.rearrange("(i p) d -> p i d", p=P)).then_inc(x_in, 16)
                sp.dma_start(bias_bc, gnn0_b.rearrange("(a d) -> a d", a=1).broadcast_to([P, D])).then_inc(gnn0_in, 16)
                for r_sb, rb, r_dram, rb_dram in ((rw_sb, rb_bc, router0_w, router0_b),
                                                  (rw1_sb, rb1_bc, router1_w, router1_b)):
                    sp.dma_start(r_sb[:, :, :], r_dram.rearrange("(k p) e -> p k e", p=P)).then_inc(r_in, 16)
                    sp.dma_start(rb[:, :], rb_dram.rearrange("(a e) -> a e", a=1).broadcast_to([P, E])).then_inc(r_in, 16)
                sp.wait_ge(consts_ready, 1)
                zeros = zero_b.bitcast(f32).rearrange("p (a d) -> p a d", a=1)
                for slots, n in ((slots0_x, SLOTS0), (slots1_x, SLOTS1)):
                    sp.dma_start(slots.rearrange("(p s) d -> p (s d)", p=P).rearrange("p (m c) -> p m c", c=D // 2),
                                 zeros.broadcast_to([P, 2 * n, D // 2])).then_inc(zeros_out, 16)
                for t in range(NT):
                    sp.wait_ge(counts_copied, t + 1)
                    sp.dma_start(counts_d[0, t], ca_stage[:, t % 2, :]).then_inc(counts_out[t % 2], 16)
                    sp.wait_ge(cb_made, t + 1)
                    sp.dma_start(counts_d[1, t], cb_stage[:, t % 2, :]).then_inc(counts_out[t % 2], 16)
                    if t == 0:
                        for e in range(2):
                            for g in range(3 - e):
                                load_up(sp, e, g, e)
                for i in range(2):
                    sp.wait_ge(counts_out[i], 32 * (NT // 2))
                sp.wait_ge(zeros_out, 32)

            @block.gpsimd
            def _(pool):
                def own(ins):
                    after(pool, pool_own, ins)

                own(nc.gpsimd.memset(ident[:, :], 0.0))
                own(nc.gpsimd.affine_select(out=ident[:, :], in_=ident[:, :], compare_op=ALU.not_equal, fill=1.0,
                                            base=0, pattern=[[-1, P]], channel_multiplier=1))
                own(nc.gpsimd.iota(tile_lo[:, :], [[P, NT]], base=0, channel_multiplier=0,
                                   allow_small_or_imprecise_dtypes=True))
                own(nc.gpsimd.iota(chunk_up[:, :], [[0, 1]], base=1, channel_multiplier=1,
                                   allow_small_or_imprecise_dtypes=True))
                own(nc.gpsimd.iota(chunk_down[:, :], [[0, 1]], base=NG, channel_multiplier=-1,
                                   allow_small_or_imprecise_dtypes=True))
                own(nc.gpsimd.memset(zero_b, 0.0))
                nc.gpsimd.iota(iota_h[:, :], [[1, T]], base=0, channel_multiplier=0,
                               allow_small_or_imprecise_dtypes=True).then_inc(consts_ready, 1)
                own(nc.gpsimd.memset(ones_b[:, :], 1.0))
                own(nc.gpsimd.memset(ones_f[:, :], 1.0))
                own(nc.gpsimd.memset(eps_t[:, :], EPS))
                own(nc.gpsimd.affine_select(out=upper_b[:, :], in_=ones_b[:, :], compare_op=ALU.is_gt, fill=0.0,
                                            base=0, pattern=[[1, P]], channel_multiplier=-1))
                own(nc.gpsimd.iota(e_key[:, :, :], [[0, NT], [-1, E]], base=E, channel_multiplier=0,
                                   allow_small_or_imprecise_dtypes=True))
                own(nc.gpsimd.iota(e_idx[:, :, :], [[0, NT], [1, E]], base=0, channel_multiplier=0,
                                   allow_small_or_imprecise_dtypes=True))
                own(nc.gpsimd.iota(k128[:, :, :], [[0, E], [P, 8]], base=P, channel_multiplier=0,
                                   allow_small_or_imprecise_dtypes=True))
                own(nc.gpsimd.memset(before[:, :, :], 1.0))
                own(nc.gpsimd.affine_select(out=before[:, :, :], in_=before[:, :, :], compare_op=ALU.is_gt, fill=0.0,
                                            base=0, pattern=[[1, E], [-1, E]], channel_multiplier=0))
                own(nc.gpsimd.iota(slot_idx[:, :, :], [[1, SLOTS1 + 1], [0, E]], base=0, channel_multiplier=0,
                                   allow_small_or_imprecise_dtypes=True))
                own(nc.gpsimd.memset(last_tok[:, :], 0.0))
                own(nc.gpsimd.affine_select(out=last_tok[:, :], in_=last_tok[:, :], compare_op=ALU.not_equal, fill=1.0,
                                            base=-(T - 1), pattern=[[P, NT]], channel_multiplier=1))
                for t in range(NT):
                    pool.wait_ge(counts_copied, t + 1)
                    if t >= 2:
                        pool.wait_ge(counts_out[t % 2], 32 * (t // 2))
                    nc.gpsimd.tensor_tensor(cb_stage[:, t % 2, :], ct_stage[:, t % 2, :], ca_stage[:, t % 2, :],
                                            ALU.subtract).then_inc(cb_made, 1)
                    own(nc.gpsimd.tensor_scalar(AT[:, t, :], ct_stage[:, t % 2, :], 1.0, None, ALU.min))
                    nc.gpsimd.affine_select(out=AT[:, t, t * P:(t + 1) * P], in_=AT[:, t, t * P:(t + 1) * P],
                                            compare_op=ALU.not_equal, fill=1.0, base=0, pattern=[[-1, P]],
                                            channel_multiplier=1).then_inc(at_ready, 1)

            @block.vector
            def _(dve):
                def own(ins):
                    after(dve, dve_own, ins)

                dve.wait_ge(edges_in, 32)
                nc.vector.tensor_copy(edges_f[:, :, :], edges_i[:, :, :]).then_inc(edge_rows, 1)
                dve.wait_ge(edge_rows, 1)
                dve.wait_ge(consts_ready, 1)
                g = slice(0, NG)
                own(nc.vector.tensor_reduce(sm[g, 0, 0:1], edges_f[:, 1, :], AX, ALU.min))
                own(nc.vector.tensor_reduce(sm[g, 0, 1:2], edges_f[:, 1, :], AX, ALU.max))
                own(nc.vector.tensor_scalar(sm[g, 1, :], tile_lo[g, :], sm[g, 0, 1:2], None, ALU.is_le))
                own(nc.vector.tensor_scalar(sm[g, 2, :], tile_lo[g, :], float(P), sm[g, 0, 0:1], ALU.add, ALU.is_gt))
                own(nc.vector.tensor_tensor(sm[g, 1, :], sm[g, 1, :], sm[g, 2, :], ALU.mult))
                nc.vector.tensor_scalar(sm[g, 3, :], sm[g, 1, :], chunk_down[g, 0:1], None, ALU.mult)
                nc.vector.tensor_scalar(sm[g, 4, :], sm[g, 1, :], chunk_up[g, 0:1], None, ALU.mult).then_inc(span, 1)
                dve.wait_ge(edge_T_ps, 1)
                own(nc.vector.tensor_copy(edges_T[:, :, :, :],
                                          PS[:, 0, 0:2 * CG * NG].rearrange("p (a b k) -> p a b k", a=2, b=CG)))
                dve.wait_ge(span_ps, 1)
                own(nc.vector.tensor_reduce(sm[0:NT, 5, 0:1], PS[0:NT, 1, 0:NG], AX, ALU.max))
                own(nc.vector.tensor_reduce(sm[0:NT, 6, 0:1], PS[0:NT, 1, NG:2 * NG], AX, ALU.max))
                own(nc.vector.tensor_scalar(sm[0:NT, 5, 0:1], sm[0:NT, 5, 0:1], -1.0, float(NG), ALU.mult, ALU.add))
                own(nc.vector.tensor_scalar(sm[0:NT, 5, 0:1], sm[0:NT, 5, 0:1], float(NG - 1), None, ALU.min))
                own(nc.vector.tensor_tensor(sm[0:NT, 6, 0:1], sm[0:NT, 6, 0:1], sm[0:NT, 5, 0:1], ALU.subtract))
                nc.vector.tensor_scalar(sm[0:NT, 6, 0:1], sm[0:NT, 6, 0:1], 1.0, None, ALU.max).then_inc(span, 1)
                dve.wait_ge(span_ps, 2)
                nc.vector.tensor_copy(etab[0:1, :], PS[0:1, 1, 256:256 + 2 * NT]).then_inc(etab_ready, 1)
                dve.wait_ge(etab_ready, 1)
                for t in range(NT):
                    first = dve.value_load(etab[0:1, t:t + 1], min_val=0, max_val=NG - 1)
                    n = dve.value_load(etab[0:1, NT + t:NT + t + 1], min_val=1, max_val=NG)
                    with dve.Fori(0, n) as j:
                        k = nc.s_assert_within(first + j, 0, NG - 1,
                                               skip_runtime_bounds_check_because="a span ends at the last group")
                        dve.wait_ge(oh_free[t], j + 1)
                        buf = dve.snap(j % NOH)
                        for c in range(CG):
                            nc.vector.tensor_scalar(oh_dst[:, ds(buf, 1), c, :],
                                                    iota_h[:, t * P:(t + 1) * P].rearrange("p (a n) -> p a n", a=1),
                                                    edges_T[:, 1, c, ds(k, 1)], None, ALU.is_equal)
                            last = nc.vector.tensor_scalar(oh_src[:, ds(buf, 1), c, :],
                                                           iota_h[:, :].rearrange("p (a n) -> p a n", a=1),
                                                           edges_T[:, 0, c, ds(k, 1)], None, ALU.is_equal)
                        last.then_inc(oh_ready[t], 1)

            @block.tensor
            def _(pe):
                pe.wait_ge(consts_ready, 1)
                pe.wait_ge(edge_rows, 1)
                for m in range(2 * CG):
                    last = nc.tensor.transpose(PS[:, 0, m * NG:(m + 1) * NG], edges_f[:, m // CG, m % CG * P:(m % CG + 1) * P],
                                               ident[0:NG, 0:NG])
                last.then_inc(edge_T_ps, 1)
                pe.wait_ge(span, 1)
                nc.tensor.transpose(PS[0:NT, 1, 0:NG], sm[0:NG, 3, :], ident[0:NG, 0:NG])
                nc.tensor.transpose(PS[0:NT, 1, NG:2 * NG], sm[0:NG, 4, :], ident[0:NG, 0:NG]).then_inc(span_ps, 1)
                pe.wait_ge(span, 2)
                nc.tensor.matmul(PS[0:1, 1, 256:256 + NT], sm[0:NT, 5, 0:1], ident[0:NT, 0:NT], start=True, stop=True)
                nc.tensor.matmul(PS[0:1, 1, 256 + NT:256 + 2 * NT], sm[0:NT, 6, 0:1], ident[0:NT, 0:NT],
                                 start=True, stop=True).then_inc(span_ps, 1)
                pe.wait_ge(etab_ready, 1)
                for t in range(NT):
                    if t >= 2:
                        pe.wait_ge(counts_copied, t - 1)
                    acc = [PS[:, 2 + 2 * (t % 2) + b, :] for b in range(2)]
                    nc.tensor.matmul(acc[0], zero_b[:, 0:P], zero_b[:, :], start=True, stop=False,
                                     skip_group_check=True).then_inc(oh_free[t], NOH)
                    nc.tensor.matmul(acc[1], zero_b[:, 0:P], zero_b[:, :], start=True, stop=False, skip_group_check=True)
                    n = pe.value_load(etab[0:1, NT + t:NT + t + 1], min_val=1, max_val=NG)
                    with pe.Fori(0, n) as j:
                        pe.wait_ge(oh_ready[t], j + 1)
                        buf = pe.snap(j % NOH)
                        for c in range(CG):
                            for b in range(2):
                                last = nc.tensor.matmul(acc[b], oh_dst[:, ds(buf, 1), c, :],
                                                        oh_src[:, ds(buf, 1), c, b * HALF:(b + 1) * HALF], start=False,
                                                        stop=True, skip_group_check=True)
                        last.then_inc(oh_free[t], 1)

            @block.scalar
            def _(act):
                act.wait_ge(etab_ready, 1)
                for t in range(NT):
                    n = act.value_load(etab[0:1, NT + t:NT + t + 1], min_val=1, max_val=NG)
                    act.wait_ge(oh_free[t], n + NOH)
                    if t >= 2:
                        act.wait_ge(counts_out[t % 2], 32 * (t // 2))
                        act.wait_ge(at_ready, t - 1)
                    counts = PS[:, 2 + 2 * (t % 2):4 + 2 * (t % 2), :].rearrange("p a b -> p (a b)")
                    nc.scalar.activation(ct_stage[:, t % 2, :], counts, ACT.Copy)
                    nc.scalar.activation(ca_stage[:, t % 2, :], counts, ACT.Copy).then_inc(counts_copied, 1)

        def norm_stats(own, act_ready, act_done, gathered=False):
            for i in range(0 if gathered else NT):
                nc.vector.bn_stats(bst[:, i, :], X[:, i, :])
            own(nc.vector.tensor_copy(sm[:, 7, 0:1], ones_f[:, :]))
            for i in range(NT):
                last = nc.vector.bn_aggr(mv[:, i, :], bst[:, i, :])
            last.then_inc(act_ready, 1)

        stats0, std0 = sem("stats0"), sem("std0")
        deg_ps, deg_sb, dinv_ready = sem("deg_ps"), sem("deg_sb"), sem("dinv_ready")
        xn_ready, xa_ready = sem("xn_ready"), sem("xa_ready")
        agg_high = sem("agg_high")
        wdeg_ps, xs_ready, mt_ps, mt_sb, out_ps, out_done = (
            sem(n) for n in "wdeg_ps xs_ready mt_ps mt_sb out_ps out_done".split())

        with nc.Block() as block:

            @block.tensor
            def _(pe):
                for i in range(NT):
                    for c in range(NT):
                        last = nc.tensor.matmul(PS[:, 0, i:i + 1], AT[:, c, i * P:(i + 1) * P], ones_b[:, 0:1],
                                                start=(c == 0), stop=(c == NT - 1))
                last.then_inc(deg_ps, 1)
                pe.wait_ge(gnn0_in, 48)
                for dk in range(DK):
                    for o in range(DK):
                        last = nc.tensor.transpose(PS[:, 4 + dk, o * P:(o + 1) * P],
                                                   W_raw[:, o, dk * P:(dk + 1) * P], ident[:, :])
                    last.then_inc(wt_ps, 1)
                pe.wait_ge(gnn0_in, 48)
                nc.tensor.transpose(PS[:, 2, 0:E * HK], b1_rows[:, :], ident[0:E * HK, 0:E * HK]).then_inc(wt_ps, 1)
                pe.wait_ge(dinv_ready, 1)
                for i in range(NT):
                    for c in range(NT):
                        last = nc.tensor.matmul(PS[:, 1, 2 * i:2 * i + 2], AT[:, c, i * P:(i + 1) * P], dinv_ab[:, c, :],
                                                start=(c == 0), stop=(c == NT - 1))
                last.then_inc(wdeg_ps, 1)
                pe.wait_ge(xs_ready, NT)
                for g in range(2 * DK):
                    dk, rh = g // 2, g % 2
                    if g >= 2:
                        pe.wait_ge(mt_sb, DK + g - 1)
                    else:
                        pe.wait_ge(wt_sb, DK + 1)
                    for m, part in enumerate((XA, XB)):
                        for c in range(NT):
                            last = nc.tensor.matmul(PS[:, 2 + g % 2, :], part[:, c, dk * P:(dk + 1) * P],
                                                    AT[:, c, rh * HALF:(rh + 1) * HALF], start=(m == 0 and c == 0),
                                                    stop=(m == 1 and c == NT - 1))
                    last.then_inc(mt_ps, 1)
                pe.wait_ge(mt_sb, 3 * DK)
                for i in range(NT):
                    if i >= 2:
                        pe.wait_ge(out_done, i - 1)
                    for dk in range(DK):
                        for a, b in ((0, 0), (0, 1), (1, 0)):
                            last = nc.tensor.matmul(PS[:, 4 + i % 2, :], MT1[:, dk, a, i * P:(i + 1) * P], WTH[:, dk, b, :],
                                                    start=(dk == 0 and a + b == 0), stop=(dk == DK - 1 and a == 1))
                    last.then_inc(out_ps, 1)

            @block.vector
            def _(dve):
                def own(ins):
                    after(dve, dve_own, ins)

                dve.wait_ge(x_in, 16)
                norm_stats(own, stats0, std0)
                dve.wait_ge(deg_ps, 1)
                nc.vector.tensor_copy(sm[:, 0, :], PS[:, 0, 0:NT]).then_inc(deg_sb, 1)
                dve.wait_ge(std0, 2)
                nc.vector.reciprocal(rstd[:, :], sm[:, 1, :])
                own(nc.vector.reciprocal(dinv[:, :], sm[:, 2, :]))
                own(nc.vector.scalar_tensor_tensor(rstd[:, :], rstd[:, :], SPLIT, dinv[:, :], ALU.mult, ALU.mult))
                own(nc.vector.tensor_scalar(dinv_ab[:, :, 0], dinv[:, :], SPLIT, None, ALU.mult))
                nc.vector.scalar_tensor_tensor(dinv_ab[:, :, 1], dinv[:, :], SPLIT, dinv_ab[:, :, 0], ALU.mult,
                                               ALU.subtract).then_inc(dinv_ready, 1)
                for i in range(NT + 1):
                    if i < NT:
                        nc.vector.tensor_scalar(XN[:, i, :], X[:, i, :], mv[:, i, 0:1], rstd[:, i:i + 1],
                                                ALU.subtract, ALU.mult).then_inc(xn_ready, 1)
                    if i >= 1:
                        dve.wait_ge(xa_ready, i)
                        nc.vector.tensor_tensor(XB[:, i - 1, :], XN[:, i - 1, :], XA[:, i - 1, :],
                                                ALU.subtract).then_inc(xs_ready, 1)
                for dk in range(DK):
                    dve.wait_ge(wt_sb, dk + 1)
                    nc.vector.scalar_tensor_tensor(WTH[:, dk, 1, :], PS[:, 4 + dk, :], W_UP, WTH[:, dk, 0, :], ALU.mult,
                                                   ALU.subtract).then_inc(mt_sb, 1)
                for g in range(2 * DK):
                    dk, rh = g // 2, g % 2
                    cols = slice(rh * HALF, (rh + 1) * HALF)
                    dve.wait_ge(agg_high, g + 1)
                    nc.vector.scalar_tensor_tensor(MT1[:, dk, 1, cols], PS[:, 2 + g % 2, :], 1.0 / SPLIT,
                                                   MT1[:, dk, 0, cols], ALU.mult, ALU.subtract).then_inc(mt_sb, 1)
                own(nc.vector.tensor_scalar(dinv[:, :], dinv[:, :], 1.0 / W_UP, None, ALU.mult))
                dve.wait_ge(wdeg_ps, 1)
                own(nc.vector.tensor_reduce(wdeg[:, :], PS[:, 1, 0:2 * NT].rearrange("p (i a) -> p i a", a=2), AX, ALU.add))
                own(nc.vector.tensor_scalar(wdeg[:, :], wdeg[:, :], W_UP / SPLIT, None, ALU.mult))
                dve.wait_ge(gnn0_in, 48)
                for i in range(NT):
                    dve.wait_ge(out_ps, i + 1)
                    own(nc.vector.scalar_tensor_tensor(PS[:, 4 + i % 2, :], bias_bc, wdeg[:, i:i + 1],
                                                       PS[:, 4 + i % 2, :], ALU.mult, ALU.add))
                    nc.vector.scalar_tensor_tensor(X[:, i, :], PS[:, 4 + i % 2, :], dinv[:, i:i + 1], X[:, i, :],
                                                   ALU.mult, ALU.add).then_inc(out_done, 1)
                    dve.wait_ge(out_done, i + 1)
                    nc.vector.bn_stats(bst[:, i, :], X[:, i, :])

            @block.scalar
            def _(act):
                act.wait_ge(stats0, 1)
                nc.scalar.activation(sm[:, 1, :], mv[:, :, 1], ACT.Sqrt, bias=eps_t[:, 0:1]).then_inc(std0, 1)
                act.wait_ge(deg_sb, 1)
                nc.scalar.activation(sm[:, 2, :], sm[:, 0, :], ACT.Sqrt).then_inc(std0, 1)
                for dk in range(DK):
                    act.wait_ge(wt_ps, dk + 1)
                    nc.scalar.activation(WTH[:, dk, 0, :], PS[:, 4 + dk, :], ACT.Copy, scale=W_UP).then_inc(wt_sb, 1)
                act.wait_ge(wt_ps, DK + 1)
                nc.scalar.activation(b1T[:, :], PS[:, 2, 0:E * HK], ACT.Copy, scale=H_UP).then_inc(wt_sb, 1)
                for i in range(NT):
                    act.wait_ge(xn_ready, i + 1)
                    nc.scalar.activation(XA[:, i, :], XN[:, i, :], ACT.Copy).then_inc(xa_ready, 1)
                for g in range(2 * DK):
                    dk, rh = g // 2, g % 2
                    act.wait_ge(mt_ps, g + 1)
                    nc.scalar.activation(MT1[:, dk, 0, rh * HALF:(rh + 1) * HALF], PS[:, 2 + g % 2, :], ACT.Copy,
                                         scale=1.0 / SPLIT).then_inc(agg_high, 1)
        def spread(ap, *shape):
            return ap.rearrange("p (n a) -> p n a", a=1).broadcast_to(list(shape))

        def over_tiles(ap, *shape):
            return ap.rearrange("p (a m) -> p a m", a=1).broadcast_to(list(shape))

        class Norm:
            def __init__(self, n):
                self.stats, self.std, self.normed = sem(f"stats_{n}"), sem(f"std_{n}"), sem(f"normed_{n}")
                self.xnt_ps, self.xnt_sb = sem(f"xnt_ps_{n}"), sem(f"xnt_sb_{n}")

        class Routing(Norm):
            def __init__(self, n):
                super().__init__(n)
                self.logits_ps, self.exp_in, self.exp_out = sem(f"logits_ps_{n}"), sem(f"exp_in_{n}"), sem(f"exp_out_{n}")
                self.mask_ready, self.pos_ps, self.dest_ready = sem(f"mask_ready_{n}"), sem(f"pos_ps_{n}"), sem(f"dest_ready_{n}")
                self.pairs_ready, self.pairs_ps, self.scattered = sem(f"pairs_ready_{n}"), sem(f"pairs_ps_{n}"), sem(f"scattered_{n}")

        route = [Routing(0), Routing(1)]

        def norm_tiles(dve_own_fn, r):
            norm_stats(dve_own_fn, r.stats, r.std, gathered=True)

        def norm_apply(own, dve, r):
            dve.wait_ge(r.std, 1)
            own(nc.vector.reciprocal(rstd[:, :], sm[:, 1, :]))
            for i in range(NT):
                nc.vector.tensor_scalar(XN[:, i, :], X[:, i, :], mv[:, i, 0:1], rstd[:, i:i + 1],
                                        ALU.subtract, ALU.mult).then_inc(r.normed, 1)

        def norm_std(act, r):
            act.wait_ge(r.stats, 1)
            nc.scalar.activation(sm[:, 1, :], mv[:, :, 1], ACT.Sqrt, bias=eps_t[:, 0:1]).then_inc(r.std, 1)

        def transposes_and_logits(pe, r, xnt, r_sb):
            for i in range(NT + 1):
                if i < NT:
                    pe.wait_ge(r.normed, i + 1)
                    if i >= 2:
                        pe.wait_ge(r.xnt_sb, i - 1)
                    for k in range(DK):
                        last = nc.tensor.transpose(PS[:, i % 2, k * P:(k + 1) * P], XN[:, i, k * P:(k + 1) * P],
                                                   ident[:, :])
                    last.then_inc(r.xnt_ps, 1)
                if i >= 1 and r_sb is not None:
                    pe.wait_ge(r.xnt_sb, i)
                    for k in range(DK):
                        last = nc.tensor.matmul(PS[:, 4, (i - 1) * E:i * E], xnt[:, i - 1, k, :], r_sb[:, k, :],
                                                start=(k == 0), stop=(k == DK - 1))
            if r_sb is not None:
                last.then_inc(r.logits_ps, 1)

        def xnt_copies(act, r, xnt):
            for i in range(NT):
                act.wait_ge(r.xnt_ps, i + 1)
                nc.scalar.activation(xnt[:, i, :, :], PS[:, i % 2, :].rearrange("p (k t) -> p k t", k=DK),
                                     ACT.Copy).then_inc(r.xnt_sb, 1)

        def top_two(own):
            for k in range(2):
                vals = rt[:, 0] if k == 0 else rt[:, 3]
                own(nc.vector.tensor_reduce(topv[:, k, :], vals, AX, ALU.max))
                own(nc.vector.tensor_tensor(rt[:, 4], vals, spread(topv[:, k, :], P, NT, E), ALU.is_equal))
                own(nc.vector.tensor_tensor(rt[:, 4], rt[:, 4], e_key[:, :, :], ALU.mult))
                own(nc.vector.tensor_reduce(sm[:, 0, :], rt[:, 4], AX, ALU.max))
                own(nc.vector.tensor_tensor(rt[:, 1 + k], rt[:, 4], spread(sm[:, 0, :], P, NT, E), ALU.is_equal))
                if k == 0:
                    own(nc.vector.scalar_tensor_tensor(rt[:, 3], rt[:, 1], -BIG, rt[:, 0], ALU.mult, ALU.add))

        def positions(pe, r):
            pe.wait_ge(r.mask_ready, 1)
            pos = PS[:, 0, 0:NT * E].rearrange("p (i e) -> p i e", i=NT)
            nc.tensor.matmul(PS[:, 0, 0:NT * E], upper_b[:, :], oh_b[:, :, :].rearrange("p i e -> p (i e)"),
                             start=True, stop=False)
            for i in range(NT - 1):
                nc.tensor.matmul(pos[:, i + 1:NT, :], ones_b[:, :],
                                 oh_b[:, i:i + 1, :].broadcast_to([P, NT - 1 - i, E]), start=False, stop=(i == NT - 2))
            for i in range(NT):
                last = nc.tensor.matmul(PS[:, 1, 0:E], ones_b[:, :], oh_b[:, i, :], start=(i == 0), stop=(i == NT - 1))
            last.then_inc(r.pos_ps, 1)

        def slot_tables(own, dve, r, tab, hots):
            dve.wait_ge(r.pos_ps, 1)
            own(nc.vector.tensor_tensor(cmp8[:, :, :], spread(PS[:, 1, 0:E], P, E, 8), k128[:, :, :], ALU.is_gt))
            own(nc.vector.tensor_reduce(nexp[:, 0, :], cmp8[:, :, :], AX, ALU.add))
            own(nc.vector.tensor_scalar(nexp[:, 0, :], nexp[:, 0, :], 1.0, None, ALU.add))
            own(nc.vector.tensor_tensor(cmp8[:, :, :], before[:, :, :], over_tiles(nexp[:, 0, :], P, E, E), ALU.mult))
            own(nc.vector.tensor_reduce(nexp[:, 1, :], cmp8[:, :, :], AX, ALU.add))
            own(nc.vector.tensor_scalar(nexp[:, 2, :], nexp[:, 1, :], float(P), None, ALU.mult))
            own(nc.vector.tensor_tensor(rt[:, 4], PS[:, 0, 0:NT * E].rearrange("p (i e) -> p i e", i=NT),
                                        over_tiles(nexp[:, 2, :], P, NT, E), ALU.add))
            for k, hot in enumerate(hots):
                own(nc.vector.tensor_tensor(rt[:, 3], rt[:, 4], hot, ALU.mult))
                own(nc.vector.tensor_reduce(dest[:, k, :], rt[:, 3], AX, ALU.add))
                nc.vector.tensor_copy(dest_i[:, k, :], dest[:, k, :])
            nc.vector.tensor_copy(tab[0:1, 0:2 * E].rearrange("p (a e) -> p a e", a=2), nexp[0:1, 0:2, :])
            nc.vector.tensor_tensor(tab[0:1, 2 * E:2 * E + 1], nexp[0:1, 0, E - 1:E], nexp[0:1, 1, E - 1:E],
                                    ALU.add).then_inc(r.dest_ready, 1)

        def scatter(pool, r, slots, choices):
            pool.wait_ge(r.dest_ready, 1)
            for k in range(choices):
                for i in range(NT):
                    nc.gpsimd.indirect_dma_start(slots, bass.IndirectOffsetOnAxis(dest_i[:, k, i:i + 1], 0),
                                                 XN[:, i, :], None).then_inc(r.scattered, 16)
            pool.wait_ge(r.scattered, 16 * NT * choices)

        hT = region(0, 2, HK, P, dt=f16)
        gated = region(1024, H)
        gT = region(2048, 2, HK, P, dt=f16)
        bg_bc = region(6144, H)
        bv_bc = region(7168, H)
        b2_bc = region(8192, D)
        x_slot = region(3072, D)
        xT = region(3584, 2, DK, P, dt=f16)
        y_slot = region(8704, D)

        def load_down(eng, e, i):
            w, rows, first = (wv, P, i) if i < WVP else (w2, 2 * P, i - WVP)
            part = w[ds(e, 1), first * rows:(first + 1) * rows, :].rearrange("a (k p) c -> p (a k) c", p=P)
            to = ring[i % RING].rearrange("p (k c) -> p k c", k=rows // P)
            eng.dma_start(to, part).then_inc(ring_in[i % RING], 16)

        def split_high(piece, block):
            nc.scalar.activation(half(block, 0, range(PIECE)), piece, ACT.Copy, scale=W_UP).then_inc(hi_done, 1)

        def split_low(piece, block):
            nc.vector.scalar_tensor_tensor(half(block, 1, range(PIECE)), piece, W_UP, half(block, 0, range(PIECE)),
                                           ALU.mult, ALU.subtract).then_inc(lo_done, 1)

        def row_bc(ap, n):
            return ap.rearrange("(a d) -> a d", a=1).broadcast_to([P, n])

        def high_of_down(act, e, pieces):
            for i in pieces:
                act.wait_ge(ring_in[i % RING], e * (DOWNP // RING * 16) + 16 * (i // RING + 1))
                split_high(ring[i % RING], DOWN + i)

        def low_of_down(dve, e, pieces):
            for i in pieces:
                dve.wait_ge(hi_done, e * EP + (UPP + i + 1))
                split_low(ring[i % RING], DOWN + i)

        def high_of_up(act, e, q, g):
            act.wait_ge(up_in[g], e * 16 + 32)
            for n, block in enumerate(up_group(1 - q, g)):
                act.wait_ge(lo_done, e * EP + (UPP + DOWNP + g * (UPP // 3) + n - 1))
                split_high(raw_piece(1 - q, block), block)

        def low_of_up(dve, e, q, g):
            for n, block in enumerate(up_group(1 - q, g)):
                dve.wait_ge(hi_done, e * EP + (UPP + DOWNP + g * (UPP // 3) + n + 1))
                dve.wait_ge(lo_done, e * EP + (UPP + DOWNP + g * (UPP // 3) + n))
                split_low(raw_piece(1 - q, block), block)

        with nc.Block() as block:
            r0 = route[0]

            @block.sync
            def _(sp):
                sp.dma_start(x_saved.rearrange("(i p) d -> p i d", p=P), X[:, :, :]).then_inc(x_moved, 16)
                sp.dma_start(bg_bc, row_bc(bg[0], H)).then_inc(bias_in, 16)
                sp.dma_start(bv_bc, row_bc(bv[0], H)).then_inc(bias_in, 16)
                sp.dma_start(b2_bc, row_bc(b2[0], D)).then_inc(b2_in, 16)
                sp.wait_ge(x_moved, 16)
                sp.wait_ge(r0.normed, NT)
                for i in range(RING):
                    load_down(sp, 0, i)

            @block.vector
            def _(dve):
                def own(ins):
                    after(dve, dve_own, ins)

                norm_tiles(own, r0)
                norm_apply(own, dve, r0)
                dve.wait_ge(r_in, 64)
                dve.wait_ge(r0.logits_ps, 1)
                own(nc.vector.tensor_tensor(rt[:, 0], PS[:, 4, 0:NT * E].rearrange("p (i e) -> p i e", i=NT),
                                            over_tiles(rb_bc[:, :], P, NT, E), ALU.add))
                own(nc.vector.tensor_reduce(sm[:, 0, :], rt[:, 0], AX, ALU.max))
                nc.vector.tensor_tensor(rt[:, 1], rt[:, 0], spread(sm[:, 0, :], P, NT, E), ALU.subtract).then_inc(r0.exp_in, 1)
                dve.wait_ge(r0.exp_out, 1)
                own(nc.vector.tensor_reduce(sm[:, 2, :], rt[:, 2], AX, ALU.add))
                own(nc.vector.reciprocal(sm[:, 3, :], sm[:, 2, :]))
                own(nc.vector.tensor_tensor(rt[:, 0], rt[:, 2], spread(sm[:, 3, :], P, NT, E), ALU.mult))
                top_two(own)
                nc.vector.tensor_copy(gate[:, :, :], topv[:, :, :])
                nc.vector.tensor_tensor(oh_b[:, :, :], rt[:, 1], rt[:, 2], ALU.add).then_inc(r0.mask_ready, 1)
                slot_tables(own, dve, r0, rtab, [rt[:, 1], rt[:, 2]])
                packed, field = sm[0:1, 0, 0:E], sm[0:1, 2, 0:E]
                own(nc.vector.scalar_tensor_tensor(packed, nexp[0:1, 1, :], 16.0, nexp[0:1, 0, :], ALU.mult, ALU.add))
                for latest in (1, 2, NT):
                    own(nc.vector.tensor_scalar(field, nexp[0:1, 0, :], -1.0, float(latest), ALU.add, ALU.min))
                    own(nc.vector.tensor_scalar(field[:, E - 1:E], nexp[0:1, 0, E - 1:E], 0.0, 15.0, ALU.mult, ALU.add))
                    own(nc.vector.scalar_tensor_tensor(packed, packed, 16.0, field, ALU.mult, ALU.add))
                own(nc.vector.tensor_copy(plan[0:1, :], packed))
                for i in range(UPP):
                    dve.wait_ge(hi_done, i + 1)
                    if i > 0:
                        dve.wait_ge(lo_done, i)
                    split_low(raw_piece(0, UP0 + i), UP0 + i)

            @block.scalar
            def _(act):
                norm_std(act, r0)
                xnt_copies(act, r0, XNT)
                act.wait_ge(r0.exp_in, 1)
                nc.scalar.activation(rt[:, 2], rt[:, 1], ACT.Exp).then_inc(r0.exp_out, 1)
                for g in range(3):
                    act.wait_ge(up_in[g], 32 if g < 2 else 16)
                    for i in up_group(0, g):
                        if i >= UP0 + 2:
                            act.wait_ge(lo_done, i - UP0 - 1)
                        split_high(raw_piece(0, i), i)

            @block.tensor
            def _(pe):
                pe.wait_ge(r_in, 64)
                transposes_and_logits(pe, r0, XNT, rw_sb)
                positions(pe, r0)

            @block.gpsimd
            def _(pool):
                scatter(pool, r0, slots0_x, 2)

        (h_ps, xtr_ps, xT_high, xT_ready, h_biased, hT_high, hT_ready, g_ps, v_ps, g_biased, silu_done, v_ready,
         gated_ready, gtr_ps, gT_high, gT_ready, y_ps, y_free, y_sb, y_stored, xg_in) = (
            sem(n) for n in "h_ps xtr_ps xT_high xT_ready h_biased hT_high hT_ready g_ps v_ps g_biased silu_done "
                            "v_ready gated_ready gtr_ps gT_high gT_ready y_ps y_free y_sb y_stored xg_in".split())

        all_stored, counts_in = sem("all_stored"), sem("counts_in")
        y_filled = sem("y_filled")

        def plan_of(eng, e):
            word = eng.value_load(plan[0:1, ds(e, 1)], min_val=0, max_val=SLOTS0 << 16)

            def field(shift, low, high):
                return nc.s_assert_within(eng.snap((word >> shift) & 15) if shift < 16 else eng.snap(word >> shift), low, high,
                                          skip_runtime_bounds_check_because="the first router packs it so")

            n, base, last = field(12, 1, NT), field(16, 0, SLOTS0 - 3), field(0, 0, 15)
            return n, base, (eng.snap(last & 8), field(8, 0, 15), field(4, 0, 15), last)

        def bank_blocks(bank):
            return PS[:, bank, :].rearrange("p (k t) -> p k t", k=HALF // P)

        with nc.Block() as block:

            @block.sync
            def _(sp):
                def down_pieces(e, pieces):
                    for i in pieces:
                        before_it = i - RING + 1 if i >= RING else i - RING + 1 + DOWNP - EP
                        sp.wait_ge(lo_done, e * EP + (UPP + before_it))
                        load_down(sp, e, i)

                sp.wait_ge(xg_in, 16)
                down_pieces(0, range(RING, DOWNP))
                load_up(sp, 1, 2, 1)
                total = sp.value_load(rtab[0:1, 2 * E:2 * E + 1], min_val=E, max_val=SLOTS0 - 2)
                with sp.Fori(0, total) as s:
                    sp.sem_inc(y_filled, 16)
                with sp.Fori(total, SLOTS0) as s:
                    sp.dma_start(slots0_y[ds(s * P, P), :], slots0_x[ds(s * P, P), :]).then_inc(y_filled, 16)
                sp.wait_ge(y_filled, SLOTS0 * 16)

                def load_expert(e, q, done):
                    down_pieces(e, range(RING))
                    sp.wait_ge(g_biased, done * 2)
                    sp.dma_start(bg_bc, bg[ds(e, 1), :].broadcast_to([P, H])).then_inc(bias_in, 16)
                    sp.wait_ge(v_ready, done * 2)
                    sp.dma_start(bv_bc, bv[ds(e, 1), :].broadcast_to([P, H])).then_inc(bias_in, 16)
                    down_pieces(e, range(RING, DOWNP))
                    if q is not None:
                        load_up(sp, 1 - q, 0, e + 1)
                    sp.wait_ge(y_sb, done)
                    sp.dma_start(b2_bc, b2[ds(e, 1), :].broadcast_to([P, D])).then_inc(b2_in, 16)
                    if q is not None:
                        for g in (1, 2):
                            load_up(sp, 1 - q, g, e + 1)

                with sp.Fori(0, (E - 2) // 2) as pair:
                    for q in (1, 0):
                        e = pair * 2 + (2 - q)
                        done = sp.value_load(rtab[0:1, ds(E + e, 1)], min_val=1, max_val=SLOTS0 - 2)
                        load_expert(e, q, done)
                done = sp.value_load(rtab[0:1, 2 * E - 1:2 * E], min_val=1, max_val=SLOTS0 - 2)
                load_expert(E - 1, None, done)
                sp.wait_ge(v_ps, done * 2)
                sp.dma_start(CAB, counts_d.rearrange("m t p s -> p (m t) s")).then_inc(counts_in, 16)
                sp.wait_ge(lo_done, UPP + EP * (E - 1) + DOWNP)
                sp.dma_start(X[:, :, :], x_saved.rearrange("(i p) d -> p i d", p=P)).then_inc(x_moved, 16)

            @block.gpsimd
            def _(pool):
                total = pool.value_load(rtab[0:1, 2 * E:2 * E + 1], min_val=E, max_val=SLOTS0 - 2)
                pool.dma_start(x_slot, slots0_x[0:P, :]).then_inc(xg_in, 16)
                with pool.Fori(1, total + 2) as s:
                    pool.wait_ge(xtr_ps, s)
                    pool.dma_start(x_slot, slots0_x[ds(s * P, P), :]).then_inc(xg_in, 16)

            @block.tensor
            def _(pe):
                def x_transposes():
                    for k in range(DK):
                        last = nc.tensor.transpose(PS[:, 7, k * P:(k + 1) * P], x_slot[:, k * P:(k + 1) * P], ident[:, :])
                    last.then_inc(xtr_ps, 1)

                def product(out, pairs, start, stop):
                    for n, (left, right) in enumerate(pairs):
                        for a, b in ((0, 0), (0, 1), (1, 0)):
                            last = nc.tensor.matmul(out, left(a), right(b), start=(start and n == 0 and a + b == 0),
                                                    stop=(stop and n == len(pairs) - 1 and a == 1))
                    return last

                def gate_or_value(first, n, bank, done, halfway=None):
                    pairs = [(lambda a, k=k: hT[:, a, k, :],
                              lambda b, k=k: half(first + k, b, range(n * HALF, (n + 1) * HALF))) for k in range(HK)]
                    product(PS[:, bank, :], pairs[:HK // 2], True, False)
                    if halfway is not None:
                        halfway()
                    product(PS[:, bank, :], pairs[HK // 2:], False, True).then_inc(done, 1)

                def gated_transposes(n):
                    for k in range(4):
                        at = n * HALF + k * P
                        last = nc.tensor.transpose(PS[:, 2 * n, k * P:(k + 1) * P], gated[:, at:at + P], ident[:, :])
                    last.then_inc(gtr_ps, 1)

                def hidden(q, s):
                    pe.wait_ge(xT_ready, s + 1)
                    for m in range(HK):
                        last = product(PS[:, m // 4, (m % 4) * P:(m % 4 + 1) * P], [
                            (lambda a, k=k: half(W1_AT[q] + k, a, range(m * P, (m + 1) * P)),
                             lambda b, k=k: xT[:, b, k, :]) for k in range(DK)], True, True)
                        if m % 4 == 3:
                            last.then_inc(h_ps, 1)

                pe.wait_ge(xg_in, 16)
                x_transposes()
                pe.wait_ge(lo_done, W1P)
                hidden(0, 0)
                pe.wait_ge(xg_in, 32)
                x_transposes()
                with pe.Fori(0, E // 2) as pair:
                    for q in range(2):
                        e = pair * 2 + q
                        n, base, (_, _, _, last_slot) = plan_of(pe, e)
                        with pe.Fori(0, n) as j:
                            s = base + j
                            pe.wait_ge(hT_ready, s * 2 + 2)
                            pe.wait_ge(lo_done, e * EP + UPP)
                            gate_or_value(WG_AT[q], 0, 2, g_ps)
                            gate_or_value(WG_AT[q], 1, 3, g_ps)
                            pe.wait_ge(lo_done, e * EP + UPP + WVP)
                            gate_or_value(DOWN, 0, 4, v_ps)

                            def first_transposes():
                                pe.wait_ge(gated_ready, s * 2 + 1)
                                gated_transposes(0)

                            gate_or_value(DOWN, 1, 5, v_ps, first_transposes)
                            pe.wait_ge(gT_ready, s * 2 + 1)
                            with pe.If(j < last_slot):
                                hidden(q, s + 1)
                            with pe.If(j == last_slot):
                                pe.wait_ge(lo_done, e * EP + EP + W1P)
                                hidden(1 - q, s + 1)
                            pe.wait_ge(xg_in, s * 16 + 48)
                            x_transposes()
                            pe.wait_ge(gated_ready, s * 2 + 2)
                            gated_transposes(1)
                            pe.wait_ge(lo_done, e * EP + EP)
                            pe.wait_ge(y_free, s + 1)
                            for h in range(2):
                                if h == 1:
                                    pe.wait_ge(gT_ready, s * 2 + 2)
                                last = product(PS[:, 6, :], [
                                    (lambda a, k=k: gT[:, a, k, :],
                                     lambda b, k=k: half(DOWN + WVP + k // 2, b, range(k % 2 * D, (k % 2 + 1) * D)))
                                    for k in range(4 * h, 4 * h + 4)], h == 0, h == 1)
                            last.then_inc(y_ps, 1)

            @block.vector
            def _(dve):
                def low_of_x(s):
                    dve.wait_ge(xT_high, s + 1)
                    nc.vector.scalar_tensor_tensor(xT[:, 1, :, :], PS[:, 7, :].rearrange("p (k t) -> p k t", k=DK), SPLIT,
                                                   xT[:, 0, :, :], ALU.mult, ALU.subtract).then_inc(xT_ready, 1)

                def hidden_whole(e, s):
                    for h in range(2):
                        dve.wait_ge(h_ps, s * 2 + 1 + h)
                        bias = b1T[:, ds(e * HK + h * 4, 4)].rearrange("p (k a) -> p k a", a=1)
                        nc.vector.scalar_tensor_tensor(bank_blocks(h), bank_blocks(h),
                                                       H_UP / (W_UP * SPLIT), bias.broadcast_to([P, 4, P]),
                                                       ALU.mult, ALU.add).then_inc(h_biased, 1)

                def low_of_hidden(s):
                    for h in range(2):
                        k = slice(4 * h, 4 * h + 4)
                        dve.wait_ge(hT_high, s * 2 + 1 + h)
                        nc.vector.tensor_tensor(hT[:, 1, k, :], bank_blocks(h), hT[:, 0, k, :],
                                                ALU.subtract).then_inc(hT_ready, 1)

                def low_of_gated(s, h):
                    dve.wait_ge(gT_high, s * 2 + 1 + h)
                    k = slice(4 * h, 4 * h + 4)
                    nc.vector.scalar_tensor_tensor(gT[:, 1, k, :], PS[:, 2 * h, :].rearrange("p (k t) -> p k t", k=4),
                                                   G_UP, gT[:, 0, k, :], ALU.mult, ALU.subtract).then_inc(gT_ready, 1)

                dve.sem_inc(y_free, 1)
                low_of_x(0)
                hidden_whole(0, 0)
                low_of_hidden(0)
                low_of_x(1)
                low_of_down(dve, 0, range(WVP))
                with dve.Fori(0, E // 2) as pair:
                    for q in range(2):
                        e = pair * 2 + q
                        n, base, times = plan_of(dve, e)

                        def split_ahead(g):
                            with dve.If(j == times[g]):
                                low_of_up(dve, e, q, g)

                        def gated_half(s, h):
                            cols = slice(h * HALF, (h + 1) * HALF)
                            dve.wait_ge(v_ps, s * 2 + 1 + h)
                            nc.vector.scalar_tensor_tensor(PS[:, 4 + h, :], PS[:, 4 + h, :], 1.0 / (W_UP * H_UP),
                                                           bv_bc[:, cols], ALU.mult, ALU.add).then_inc(v_ready, 1)
                            dve.wait_ge(v_ready, s * 2 + 1 + h)
                            dve.wait_ge(silu_done, s * 2 + 1 + h)
                            nc.vector.tensor_tensor(gated[:, cols], gated[:, cols], PS[:, 4 + h, :],
                                                    ALU.mult).then_inc(gated_ready, 1)

                        with dve.Fori(0, n) as j:
                            s = base + j
                            with dve.If(j < 1):
                                low_of_down(dve, e, range(WVP, DOWNP))
                            dve.wait_ge(bias_in, e * 32 + 32)
                            for h in range(2):
                                cols = slice(h * HALF, (h + 1) * HALF)
                                dve.wait_ge(g_ps, s * 2 + 1 + h)
                                nc.vector.scalar_tensor_tensor(gated[:, cols], PS[:, 2 + h, :], 1.0 / (W_UP * H_UP),
                                                               bg_bc[:, cols], ALU.mult, ALU.add).then_inc(g_biased, 1)
                            split_ahead(0)
                            gated_half(s, 0)
                            low_of_gated(s, 0)
                            split_ahead(1)
                            gated_half(s, 1)
                            split_ahead(2)
                            with dve.If(j == times[3]):
                                hidden_whole(nc.s_assert_within(
                                    e + 1, 1, E - 1, skip_runtime_bounds_check_because="not for the last expert"), s + 1)
                            with dve.If(j < times[3]):
                                hidden_whole(e, s + 1)
                            low_of_hidden(s + 1)
                            low_of_gated(s, 1)
                            low_of_x(s + 2)
                            with dve.If(j == times[3]):
                                low_of_down(dve, e + 1, range(WVP))
                            dve.wait_ge(y_ps, s + 1)
                            dve.wait_ge(y_stored, s * 16 + 16)
                            dve.wait_ge(b2_in, e * 16 + 16)
                            nc.vector.scalar_tensor_tensor(y_slot, PS[:, 6, :], 1.0 / (W_UP * G_UP), b2_bc, ALU.mult,
                                                           ALU.add).then_inc(y_sb, 1)
                            dve.wait_ge(y_sb, s + 1)
                            dve.sem_inc(y_free, 1)

            @block.scalar
            def _(act):
                def high_of_x():
                    nc.scalar.activation(xT[:, 0, :, :], PS[:, 7, :].rearrange("p (k t) -> p k t", k=DK),
                                         ACT.Copy, scale=SPLIT).then_inc(xT_high, 1)

                nc.scalar.activation(sm[:, 7, 0:1], eps_t[:, 0:1], ACT.Silu)
                act.sem_inc(y_stored, 16)
                act.wait_ge(xtr_ps, 1)
                high_of_x()

                def high_of_hidden(s):
                    for h in range(2):
                        act.wait_ge(h_biased, s * 2 + 1 + h)
                        k = slice(4 * h, 4 * h + 4)
                        nc.scalar.activation(hT[:, 0, k, :], bank_blocks(h), ACT.Copy).then_inc(hT_high, 1)

                def high_of_gated(s, h):
                    act.wait_ge(gtr_ps, s * 2 + 1 + h)
                    k = slice(4 * h, 4 * h + 4)
                    nc.scalar.activation(gT[:, 0, k, :], PS[:, 2 * h, :].rearrange("p (k t) -> p k t", k=4),
                                         ACT.Copy, scale=G_UP).then_inc(gT_high, 1)

                high_of_hidden(0)
                act.wait_ge(xtr_ps, 2)
                high_of_x()
                high_of_down(act, 0, range(WVP))
                with act.Fori(0, E // 2) as pair:
                    for q in range(2):
                        e = pair * 2 + q
                        n, base, times = plan_of(act, e)

                        def split_ahead(g):
                            with act.If(j == times[g]):
                                high_of_up(act, e, q, g)

                        with act.Fori(0, n) as j:
                            s = nc.s_assert_within(base + j, 0, SLOTS0 - 3,
                                                   skip_runtime_bounds_check_because="the slots in use are fewer")
                            with act.If(j < 1):
                                high_of_down(act, e, range(WVP, DOWNP))
                            split_ahead(0)
                            for h in range(2):
                                cols = slice(h * HALF, (h + 1) * HALF)
                                act.wait_ge(g_biased, s * 2 + 1 + h)
                                nc.scalar.activation(gated[:, cols], gated[:, cols], ACT.Silu).then_inc(silu_done, 1)
                            high_of_gated(s, 0)
                            split_ahead(1)
                            split_ahead(2)
                            high_of_hidden(s + 1)
                            high_of_gated(s, 1)
                            act.wait_ge(xtr_ps, s + 3)
                            high_of_x()
                            with act.If(j == times[3]):
                                high_of_down(act, e + 1, range(WVP))
                            act.wait_ge(y_sb, s + 1)
                            act.dma_start(slots0_y[ds(s * P, P), :], y_slot).then_inc(y_stored, 16)
                total = act.value_load(rtab[0:1, 2 * E:2 * E + 1], min_val=E, max_val=SLOTS0 - 2)
                act.wait_ge(y_stored, total * 16 + 16)
                act.sem_inc(all_stored, 1)

        w1_flat = U[:, place(DOWN):place(DOWN) + 2 * NT * D]
        picked = w1_flat.rearrange("p (i k d) -> p i k d", i=NT, k=2)
        XNT1 = w1_flat[:, 0:NT * D].rearrange("p (i k t) -> p i k t", i=NT, k=DK)
        XNT2 = U[:, place(DOWN) + 2 * NT * D:place(DOWN) + 3 * NT * D].rearrange("p (i k t) -> p i k t", i=NT, k=DK)
        XA1 = half_flat[:, 2 * NT * T:2 * NT * T + NT * D].rearrange("p (i d) -> p i d", i=NT)
        XB1 = half_flat[:, 2 * NT * T + NT * D:2 * NT * T + 2 * NT * D].rearrange("p (i d) -> p i d", i=NT)
        W12 = U[:, 0:E * DK * 2 * H1].rearrange("p (e k h) -> p e k h", e=E, k=DK)
        W3 = U[:, E * DK * 2 * H1:E * (DK * 2 * H1 + HK1 * D)].rearrange("p (e k d) -> p e k d", e=E, k=HK1)
        XT1 = XNT1.rearrange("p i k t -> p (i k t)").bitcast(f16).rearrange("p (i a k t) -> p i a k t", i=NT, a=2, k=DK)
        gnn1_halves = U[:, place(DOWN) + NT * D:place(DOWN) + 2 * NT * D].bitcast(f16).rearrange(
            "p (w a k d) -> p w a k d", w=2, a=2, k=DK)
        wc_sb = region(4096, DK, D)
        wn_sb = region(6144, DK, D)
        bias1_bc = region(8192, D)
        picked_in = [sem(f"picked_in{i}") for i in range(NT)]
        gnn1_in, mix1_in = (sem(n) for n in "gnn1_in mix1_in".split())
        indeg_ps, ut_ps, ut_sb, out1_ps, out1_done = (
            sem(n) for n in "indeg_ps ut_ps ut_sb out1_ps out1_done".split())
        mid = Norm("mid")
        xt1_high = sem("xt1_high")
        cb_ready, cb_ps, parts_ready, ut_part = (sem(n) for n in "cb_ready cb_ps parts_ready ut_part".split())
        parts_f = rt[:, 0, 0, :]
        any_left = rt[:, 1, 0, 0:1]
        abs_out = half_flat[:, 2 * NT * T:3 * NT * T]
        zeros_f = region(8960, HALF // 2)
        zeros_h = region(8960, HALF, dt=bf16)

        with nc.Block() as block:

            @block.sync
            def _(sp):
                sp.wait_ge(picked_in[NT - 1], 32)
                sp.dma_start(wc_sb, wc.rearrange("(k p) d -> p k d", p=P)).then_inc(gnn1_in, 16)
                sp.dma_start(wn_sb, wn.rearrange("(k p) d -> p k d", p=P)).then_inc(gnn1_in, 16)
                sp.dma_start(bias1_bc, row_bc(gnn1_b, D)).then_inc(gnn1_in, 16)

            @block.gpsimd
            def _(pool):
                nc.gpsimd.memset(zeros_f, 0.0).then_inc(consts_ready, 1)
                for i in range(NT):
                    for k in range(2):
                        nc.gpsimd.indirect_dma_start(picked[:, i, k, :], None, slots0_y,
                                                     bass.IndirectOffsetOnAxis(dest_i[:, k, i:i + 1], 0)
                                                     ).then_inc(picked_in[i], 16)

            @block.vector
            def _(dve):
                def own(ins):
                    after(dve, dve_own, ins)

                dve.wait_ge(x_moved, 32)
                for i in range(NT):
                    dve.wait_ge(picked_in[i], 32)
                    own(nc.vector.scalar_tensor_tensor(X[:, i, :], picked[:, i, 0, :], gate[:, 0, i:i + 1], X[:, i, :],
                                                       ALU.mult, ALU.add))
                    own(nc.vector.scalar_tensor_tensor(X[:, i, :], picked[:, i, 1, :], gate[:, 1, i:i + 1], X[:, i, :],
                                                       ALU.mult, ALU.add))
                    nc.vector.bn_stats(bst[:, i, :], X[:, i, :])
                norm_stats(own, mid.stats, mid.std, gathered=True)
                dve.wait_ge(cb_ps, 1)
                own(nc.vector.tensor_reduce(parts_f[0:1, 0:1], PS[0:1, 4, 0:P], AX, ALU.max))
                nc.vector.tensor_scalar(parts[0:1, :], parts_f[0:1, 0:1], 0.0, 1.0, ALU.is_gt, ALU.add).then_inc(parts_ready, 1)
                norm_apply(own, dve, mid)
                for i in range(NT):
                    dve.wait_ge(xt1_high, i + 1)
                    nc.vector.scalar_tensor_tensor(XT1[:, i, 1, :, :], PS[:, i % 2, :].rearrange("p (k t) -> p k t", k=DK),
                                                   SPLIT, XT1[:, i, 0, :, :], ALU.mult, ALU.subtract).then_inc(mid.xnt_sb, 1)
                    dve.wait_ge(xa_ready, NT + i + 1)
                    nc.vector.scalar_tensor_tensor(XB1[:, i, :], XN[:, i, :], SPLIT, XA1[:, i, :], ALU.mult,
                                                   ALU.subtract).then_inc(xs_ready, 1)
                split_before = UPP + EP * (E - 1) + DOWNP
                for k in range(2 * DK):
                    dve.wait_ge(hi_done, split_before + k + 1)
                    nc.vector.scalar_tensor_tensor(gnn1_halves[:, k // DK, 1, k % DK, :], (wc_sb, wn_sb)[k // DK][:, k % DK, :],
                                                   W_UP, gnn1_halves[:, k // DK, 0, k % DK, :], ALU.mult,
                                                   ALU.subtract).then_inc(lo_done, 1)
                for g in range(2 * DK):
                    dk, rh = g // 2, g % 2
                    dve.wait_ge(agg_high, 2 * DK + g + 1)
                    cols = slice(rh * HALF, (rh + 1) * HALF)
                    nc.vector.scalar_tensor_tensor(MT1[:, dk, 1, cols], PS[:, 2 + g % 2, :], M_UP / SPLIT,
                                                   MT1[:, dk, 0, cols], ALU.mult, ALU.subtract).then_inc(ut_sb, 1)
                dve.wait_ge(indeg_ps, 1)
                own(nc.vector.tensor_reduce(wdeg[:, :], PS[:, 5, 0:2 * NT].rearrange("p (i m) -> p i m", m=2), AX, ALU.add))
                own(nc.vector.reciprocal(wdeg[:, :], wdeg[:, :]))
                own(nc.vector.tensor_scalar(wdeg[:, :], wdeg[:, :], 1.0 / (M_UP * W_UP), None, ALU.mult))
                dve.wait_ge(gnn1_in, 48)
                for i in range(NT):
                    alpha, gamma = PS[:, 6 + i % 2, :], PS[:, 2 + i % 2, :]
                    own(nc.vector.tensor_tensor(X[:, i, :], X[:, i, :], bias1_bc, ALU.add))
                    dve.wait_ge(out1_ps, i + 1)
                    own(nc.vector.scalar_tensor_tensor(X[:, i, :], gamma, wdeg[:, i:i + 1], X[:, i, :], ALU.mult, ALU.add))
                    nc.vector.scalar_tensor_tensor(X[:, i, :], alpha, 1.0 / (SPLIT * W_UP), X[:, i, :], ALU.mult,
                                                   ALU.add).then_inc(out1_done, 1)
                    dve.wait_ge(out1_done, i + 1)
                    nc.vector.bn_stats(bst[:, i, :], X[:, i, :])

            @block.tensor
            def _(pe):
                pe.wait_ge(cb_ready, 1)
                nc.tensor.transpose(PS[0:1, 4, 0:P], any_left[:, 0:1], ident[:, :]).then_inc(cb_ps, 1)
                for i in range(NT):
                    for m in range(2):
                        for c in range(NT):
                            last = nc.tensor.matmul(PS[:, 5, 2 * i + m:2 * i + m + 1], CAB[:, m * NT + c, i * P:(i + 1) * P],
                                                    ones_b[:, 0:1], start=(c == 0), stop=(c == NT - 1))
                last.then_inc(indeg_ps, 1)
                transposes_and_logits(pe, mid, None, None)
                pe.wait_ge(consts_ready, 2)
                pe.wait_ge(parts_ready, 1)
                n_parts = pe.value_load(parts[0:1, 0:1], min_val=1, max_val=2)
                pe.wait_ge(xs_ready, 2 * NT)
                for g in range(2 * DK):
                    dk, rh = g // 2, g % 2
                    if g >= 2:
                        pe.wait_ge(ut_sb, g - 1)
                    nc.tensor.matmul(PS[:, 2 + g % 2, :], zeros_h[:, 0:P], zeros_h[:, :], start=True, stop=False,
                                     skip_group_check=True)
                    with pe.Fori(0, n_parts) as m:
                        for x_part in (XA1, XB1):
                            for c in range(NT):
                                last = nc.tensor.matmul(PS[:, 2 + g % 2, :], x_part[:, c, dk * P:(dk + 1) * P],
                                                        CAB[:, ds(m * NT + c, 1), rh * HALF:(rh + 1) * HALF], start=False,
                                                        stop=True, skip_group_check=True)
                        last.then_inc(ut_part, 1)
                    pe.wait_ge(ut_part, n_parts * (g + 1))
                    pe.sem_inc(ut_ps, 1)
                pe.wait_ge(ut_sb, 2 * DK)
                pe.wait_ge(mid.xnt_sb, NT)
                pe.wait_ge(lo_done, UPP + EP * (E - 1) + DOWNP + 2 * DK)
                for i in range(NT):
                    if i >= 2:
                        pe.wait_ge(out1_done, i - 1)
                    for bank, left_of, w in ((2 + i % 2, lambda a, k: MT1[:, k, a, i * P:(i + 1) * P], 1),
                                             (6 + i % 2, lambda a, k: XT1[:, i, a, k, :], 0)):
                        for k in range(DK):
                            for a, b in ((0, 0), (0, 1), (1, 0)):
                                last = nc.tensor.matmul(PS[:, bank, :], left_of(a, k), gnn1_halves[:, w, b, k, :],
                                                        start=(k == 0 and a + b == 0), stop=(k == DK - 1 and a == 1))
                    last.then_inc(out1_ps, 1)

            @block.scalar
            def _(act):
                act.wait_ge(counts_in, 16)
                nc.scalar.activation(abs_out, CAB[:, NT:2 * NT, :].rearrange("p t s -> p (t s)"), ACT.Abs,
                                     accum_out=any_left[:, 0:1]).then_inc(cb_ready, 1)
                norm_std(act, mid)
                for i in range(NT):
                    act.wait_ge(mid.normed, i + 1)
                    nc.scalar.activation(XA1[:, i, :], XN[:, i, :], ACT.Copy, scale=SPLIT).then_inc(xa_ready, 1)
                    act.wait_ge(mid.xnt_ps, i + 1)
                    nc.scalar.activation(XT1[:, i, 0, :, :], PS[:, i % 2, :].rearrange("p (k t) -> p k t", k=DK),
                                         ACT.Copy, scale=SPLIT).then_inc(xt1_high, 1)
                act.wait_ge(gnn1_in, 48)
                for w, raw in enumerate((wc_sb, wn_sb)):
                    for k in range(DK):
                        nc.scalar.activation(gnn1_halves[:, w, 0, k, :], raw[:, k, :], ACT.Copy, scale=W_UP).then_inc(hi_done, 1)
                for g in range(2 * DK):
                    dk, rh = g // 2, g % 2
                    act.wait_ge(ut_ps, g + 1)
                    nc.scalar.activation(MT1[:, dk, 0, rh * HALF:(rh + 1) * HALF], PS[:, 2 + g % 2, :], ACT.Copy,
                                         scale=M_UP / SPLIT).then_inc(agg_high, 1)
        s_gate = sm[:, 4:6, :]
        kept = sm[:, 2:4, :]
        coef = gate
        with nc.Block() as block:
            r1 = route[1]

            @block.sync
            def _(sp):
                for e in range(E):
                    sp.dma_start(W12[:, e, :, 0:H1], e1_w1[e].rearrange("(k p) h -> p k h", p=P)).then_inc(mix1_in, 16)
                    sp.dma_start(W12[:, e, :, H1:2 * H1], e1_w2[e].rearrange("(k p) h -> p k h", p=P)).then_inc(mix1_in, 16)
                    sp.dma_start(W3[:, e, :, :], e1_w3[e].rearrange("(k p) d -> p k d", p=P)).then_inc(mix1_in, 16)

            @block.vector
            def _(dve):
                def own(ins):
                    after(dve, dve_own, ins)

                norm_tiles(own, r1)
                norm_apply(own, dve, r1)
                dve.wait_ge(r1.logits_ps, 1)
                own(nc.vector.tensor_tensor(rt[:, 0], PS[:, 4, 0:NT * E].rearrange("p (i e) -> p i e", i=NT),
                                            over_tiles(rb1_bc[:, :], P, NT, E), ALU.add))
                top_two(own)
                nc.vector.tensor_tensor(sm[:, 6, :], topv[:, 1, :], topv[:, 0, :], ALU.subtract).then_inc(r1.exp_in, 1)
                nc.vector.tensor_copy(oh_b[:, :, :], rt[:, 1])
                nc.vector.tensor_copy(oh2_b[:, :, :], rt[:, 2]).then_inc(r1.pairs_ready, 1)
                dve.wait_ge(r1.exp_out, 1)
                own(nc.vector.tensor_scalar(sm[:, 0, :], sm[:, 7, :], 1.0, None, ALU.add))
                own(nc.vector.reciprocal(s_gate[:, 0, :], sm[:, 0, :]))
                own(nc.vector.tensor_tensor(s_gate[:, 1, :], sm[:, 7, :], s_gate[:, 0, :], ALU.mult))
                dve.wait_ge(r1.pairs_ps, 1)
                own(nc.vector.tensor_copy(nexp[:, 0:2, :], PS[:, 5, 0:2 * E].rearrange("p (a e) -> p a e", a=2)))
                own(nc.vector.tensor_scalar(nexp[:, 0:2, :], nexp[:, 0:2, :], float(T), None, ALU.is_ge))
                for k in range(2):
                    own(nc.vector.tensor_tensor(rt[:, 4], rt[:, 1 + k], over_tiles(nexp[:, k, :], P, NT, E), ALU.mult))
                    own(nc.vector.tensor_reduce(kept[:, k, :], rt[:, 4], AX, ALU.add))
                    own(nc.vector.tensor_tensor(kept[:, k, :], kept[:, k, :], last_tok[:, :], ALU.mult))
                    own(nc.vector.tensor_scalar(kept[:, k, :], kept[:, k, :], -1.0, 1.0, ALU.mult, ALU.add))
                    own(nc.vector.tensor_tensor(rt[:, 4], rt[:, 1 + k], e_idx[:, :, :], ALU.mult))
                    own(nc.vector.tensor_reduce(dest[:, k, :], rt[:, 4], AX, ALU.add))
                    own(nc.vector.tensor_tensor(dest[:, k, :], dest[:, k, :], kept[:, k, :], ALU.mult))
                own(nc.vector.tensor_tensor(sm[:, 0, :], dest[:, 0, :], dest[:, 1, :], ALU.max))
                own(nc.vector.tensor_tensor(rt[:, 5], e_idx[:, :, :], spread(sm[:, 0, :], P, NT, E), ALU.is_equal))
                nc.vector.tensor_copy(oh_b[:, :, :], rt[:, 5]).then_inc(r1.mask_ready, 1)
                own(nc.vector.tensor_tensor(topv[:, :, :], s_gate, kept, ALU.mult))
                own(nc.vector.tensor_tensor(coef[:, 0, :], topv[:, 0, :], topv[:, 1, :], ALU.add))
                own(nc.vector.tensor_scalar(kept, kept, -1.0, 1.0, ALU.mult, ALU.add))
                own(nc.vector.tensor_tensor(topv[:, :, :], s_gate, kept, ALU.mult))
                own(nc.vector.tensor_tensor(coef[:, 1, :], topv[:, 0, :], topv[:, 1, :], ALU.add))
                slot_tables(own, dve, r1, rtab1, [rt[:, 5]])
                own(nc.vector.tensor_tensor(slot_cmp[:, :, :], over_tiles(nexp[:, 1, :], P, SLOTS1 + 1, E),
                                            slot_idx[:, :, :], ALU.is_le))
                own(nc.vector.tensor_reduce(slot_row[:, :], slot_cmp[:, :, :], AX, ALU.add))
                own(nc.vector.tensor_scalar(expert_of[0:1, :], slot_row[0:1, :], -1.0, None, ALU.add))

            @block.scalar
            def _(act):
                norm_std(act, r1)
                xnt_copies(act, r1, XNT2)
                act.wait_ge(r1.exp_in, 1)
                nc.scalar.activation(sm[:, 7, :], sm[:, 6, :], ACT.Exp).then_inc(r1.exp_out, 1)

            @block.tensor
            def _(pe):
                transposes_and_logits(pe, r1, XNT2, rw1_sb)
                pe.wait_ge(r1.pairs_ready, 1)
                for i in range(NT):
                    nc.tensor.matmul(PS[:, 5, 0:E], ones_b[:, :], oh_b[:, i, :], start=(i == 0), stop=(i == NT - 1))
                for m, hot in enumerate((oh_b, oh2_b)):
                    for i in range(NT):
                        last = nc.tensor.matmul(PS[:, 5, E:2 * E], ones_b[:, :], hot[:, i, :], start=(m == 0 and i == 0),
                                                stop=(m == 1 and i == NT - 1))
                last.then_inc(r1.pairs_ps, 1)
                positions(pe, r1)

            @block.gpsimd
            def _(pool):
                scatter(pool, r1, slots1_x, 1)

        x1_slot = region(4096, D)
        x1T = region(4608, DK, P)
        y1_slot = region(5120, D)
        left = region(5632, H1)
        act_in = region(5888, H1)
        act_out = region(6144, H1)
        aT = region(6400, HK1, P)
        (ab_ps, x1tr_ps, x1T_ready, left_ready, prod_ready, gelu_done, atr_ps, aT_ready, y1_ps, y1_sb,
         y1_stored, x1_in) = (
            sem(n) for n in "ab_ps x1tr_ps x1T_ready left_ready prod_ready gelu_done atr_ps aT_ready y1_ps y1_sb "
                            "y1_stored x1_in".split())
        with nc.Block() as block:

            @block.sync
            def _(sp):
                total = sp.value_load(rtab1[0:1, 2 * E:2 * E + 1], min_val=E, max_val=SLOTS1 - 2)
                sp.sem_inc(y1_stored, 16)
                with sp.Fori(0, total) as s:
                    sp.wait_ge(y1_sb, s + 2)
                    sp.dma_start(slots1_y[ds(s * P, P), :], y1_slot).then_inc(y1_stored, 16)
                    sp.sem_inc(y_filled, 16)
                with sp.Fori(total, SLOTS1) as s:
                    sp.dma_start(slots1_y[ds(s * P, P), :], slots1_x[ds(s * P, P), :]).then_inc(y_filled, 16)
                sp.wait_ge(y_filled, (SLOTS0 + SLOTS1) * 16)
                sp.wait_ge(y1_stored, total * 16 + 16)
                sp.sem_inc(all_stored, 1)

            @block.gpsimd
            def _(pool):
                total = pool.value_load(rtab1[0:1, 2 * E:2 * E + 1], min_val=E, max_val=SLOTS1 - 2)
                pool.dma_start(x1_slot, slots1_x[0:P, :]).then_inc(x1_in, 16)
                with pool.Fori(1, total + 2) as s:
                    pool.wait_ge(x1tr_ps, s)
                    pool.dma_start(x1_slot, slots1_x[ds(s * P, P), :]).then_inc(x1_in, 16)

            @block.tensor
            def _(pe):
                def x_transposes():
                    for k in range(DK):
                        last = nc.tensor.transpose(PS[:, 7, k * P:(k + 1) * P], x1_slot[:, k * P:(k + 1) * P], ident[:, :])
                    last.then_inc(x1tr_ps, 1)

                def up(e, s):
                    for k in range(DK):
                        last = nc.tensor.matmul(PS[:, ds(s % 2 + 4, 1), :], x1T[:, k, :], W12[:, ds(e, 1), k, :],
                                                start=(k == 0), stop=(k == DK - 1))
                    last.then_inc(ab_ps, 1)

                pe.wait_ge(mix1_in, 48 * E)
                pe.wait_ge(x1_in, 16)
                x_transposes()
                pe.wait_ge(x1T_ready, 1)
                up(0, 0)
                pe.wait_ge(x1_in, 32)
                x_transposes()
                total = pe.value_load(rtab1[0:1, 2 * E:2 * E + 1], min_val=E, max_val=SLOTS1 - 2)
                with pe.Fori(0, total) as s:
                    here = pe.value_load(expert_of[0:1, ds(s, 1)], min_val=0, max_val=E - 1)
                    ahead = pe.value_load(expert_of[0:1, ds(s + 1, 1)], min_val=0, max_val=E - 1)
                    pe.wait_ge(gelu_done, s + 1)
                    for k in range(HK1):
                        last = nc.tensor.transpose(PS[:, 1, k * P:(k + 1) * P], act_out[:, k * P:(k + 1) * P], ident[:, :])
                    last.then_inc(atr_ps, 1)
                    pe.wait_ge(x1T_ready, s + 2)
                    up(ahead, s + 1)
                    pe.wait_ge(x1_in, s * 16 + 48)
                    x_transposes()
                    pe.wait_ge(aT_ready, s + 1)
                    pe.wait_ge(y1_sb, s + 1)
                    for k in range(HK1):
                        last = nc.tensor.matmul(PS[:, 2, :], aT[:, k, :], W3[:, ds(here, 1), k, :],
                                                start=(k == 0), stop=(k == HK1 - 1))
                    last.then_inc(y1_ps, 1)

            @block.vector
            def _(dve):
                def xT_copy():
                    nc.vector.tensor_copy(x1T, PS[:, 7, :].rearrange("p (k t) -> p k t", k=DK)).then_inc(x1T_ready, 1)

                def product(s):
                    bank = ds(s % 2 + 4, 1)
                    nc.vector.tensor_copy(left, PS[:, bank, 0:H1]).then_inc(left_ready, 1)
                    dve.wait_ge(left_ready, s + 1)
                    nc.vector.tensor_tensor(act_in, PS[:, bank, H1:2 * H1], left, ALU.mult).then_inc(prod_ready, 1)

                dve.wait_ge(x1tr_ps, 1)
                xT_copy()
                dve.wait_ge(ab_ps, 1)
                product(0)
                dve.wait_ge(x1tr_ps, 2)
                xT_copy()
                total = dve.value_load(rtab1[0:1, 2 * E:2 * E + 1], min_val=E, max_val=SLOTS1 - 2)
                with dve.Fori(0, total) as s:
                    dve.wait_ge(atr_ps, s + 1)
                    nc.vector.tensor_copy(aT, PS[:, 1, 0:H1].rearrange("p (k t) -> p k t", k=HK1)).then_inc(aT_ready, 1)
                    dve.wait_ge(ab_ps, s + 2)
                    product(s + 1)
                    dve.wait_ge(x1tr_ps, s + 3)
                    xT_copy()

            @block.scalar
            def _(act):
                nc.scalar.activation(sm[:, 7, 0:1], eps_t[:, 0:1], ACT.Gelu)
                act.sem_inc(y1_sb, 1)
                total = act.value_load(rtab1[0:1, 2 * E:2 * E + 1], min_val=E, max_val=SLOTS1 - 2)
                act.wait_ge(prod_ready, 1)
                nc.scalar.activation(act_out, act_in, ACT.Gelu).then_inc(gelu_done, 1)
                with act.Fori(0, total) as s:
                    act.wait_ge(atr_ps, s + 1)
                    act.wait_ge(prod_ready, s + 2)
                    nc.scalar.activation(act_out, act_in, ACT.Gelu).then_inc(gelu_done, 1)
                    act.wait_ge(y1_ps, s + 1)
                    act.wait_ge(y1_stored, s * 16 + 16)
                    nc.scalar.activation(y1_slot, PS[:, 2, :], ACT.Copy).then_inc(y1_sb, 1)

        final_x, stored = sem("final_x"), sem("stored")
        with nc.Block() as block:

            @block.gpsimd
            def _(pool):
                for i in range(NT):
                    nc.gpsimd.indirect_dma_start(picked[:, i, 0, :], None, slots1_y,
                                                 bass.IndirectOffsetOnAxis(dest_i[:, 0, i:i + 1], 0)
                                                 ).then_inc(picked_in[i], 16)

            @block.vector
            def _(dve):
                def own(ins):
                    after(dve, dve_own, ins)

                for i in range(NT):
                    own(nc.vector.scalar_tensor_tensor(X[:, i, :], XN[:, i, :], coef[:, 1, i:i + 1], X[:, i, :],
                                                       ALU.mult, ALU.add))
                    dve.wait_ge(picked_in[i], 32 + 16)
                    nc.vector.scalar_tensor_tensor(X[:, i, :], picked[:, i, 0, :], coef[:, 0, i:i + 1], X[:, i, :],
                                                   ALU.mult, ALU.add).then_inc(final_x, 1)

            @block.sync
            def _(sp):
                for i in range(NT):
                    sp.wait_ge(final_x, i + 1)
                    sp.dma_start(out[i * P:(i + 1) * P, :], X[:, i, :]).then_inc(stored, 16)
                sp.wait_ge(stored, 16 * NT)


_INS = ['x', 'src', 'dst', 'L0_gnn_W', 'L0_gnn_b', 'L0_ffn_router_w', 'L0_ffn_router_b', 'L0_ffn_w1', 'L0_ffn_b1',
        'L0_ffn_wg', 'L0_ffn_bg', 'L0_ffn_wv', 'L0_ffn_bv', 'L0_ffn_w2', 'L0_ffn_b2', 'L1_gnn_wc', 'L1_gnn_wn',
        'L1_gnn_bias', 'L1_ffn_Wr', 'L1_ffn_br', 'L1_ffn_W1', 'L1_ffn_W2', 'L1_ffn_W3']
_OUTS = [((1024, 512), 'float32')]


def kernel(**inputs):
    import numpy as _np
    import concourse.bacc as _bacc
    from concourse import mybir as _mybir
    from concourse.bass_utils import run_bass_kernel_spmd as _run

    nc = _bacc.Bacc("TRN2", target_bir_lowering=False, num_devices=1)
    arrays, args = {}, []
    for name in _INS:
        a = _np.ascontiguousarray(inputs[name])
        arrays[f"in_{name}_dram"] = a
        args.append(nc.dram_tensor(f"in_{name}_dram", a.shape, _mybir.dt.from_np(a.dtype), kind="ExternalInput").ap())
    for i, (shape, dtype) in enumerate(_OUTS):
        dt = _mybir.dt.from_np(_np.dtype(dtype))
        args.append(nc.dram_tensor(f"out_{i}_dram", shape, dt, kind="ExternalOutput").ap())
    gnn_moe_two_layer_kernel(nc, *args)
    r = _run(nc, [arrays], core_ids=[0])
    got = tuple(r.results[0][f"out_{i}_dram"] for i in range(len(_OUTS)))
    return got[0]
```
